# Optimizing a Trainium2 kernel written in Bass

```python
import numpy as np
import jax
import jax.numpy as jnp

def _softmax(x, axis=-1):
    return jax.nn.softmax(x, axis=axis)

def _gelu(x):
    return jax.nn.gelu(x, approximate=True)

def _silu(x):
    return jax.nn.silu(x)

def _sigmoid(x):
    return jax.nn.sigmoid(x)

def _layernorm(x, axis=-1, eps=1e-05):
    m = jnp.mean(x, axis=axis, keepdims=True)
    v = jnp.var(x, axis=axis, keepdims=True)
    return (x - m) / jnp.sqrt(v + eps)

def _scatter_add(tgt, idx, src, axis=0):
    return tgt.at[idx].add(src)

def _segment_sum(src, seg, n):
    return jax.ops.segment_sum(src, seg, n)
kernel_name = 'mk_sandwich_d1_jaxref_r8_26f988'

def setup_inputs(seed: int=0):
    np.random.seed(seed)
    _w = jnp.asarray

    def _L0_attn_setup():
        import jax, jax.numpy as jnp
        import numpy as np
        from math import sqrt
        E = 128
        H = 16
        HS = E // H
        EPS = 1e-08

        def _layer_norm(x, gamma, beta):
            mean = jnp.mean(x, axis=-1, keepdims=True)
            std = jnp.sqrt(jnp.mean((x - mean) ** 2, axis=-1, keepdims=True))
            return gamma * ((x - mean) / (std + EPS)) + beta
        key = jax.random.key(seed)
        ks = jax.random.split(key, 8)
        B, S = (2, 256)
        scale = 1.0 / sqrt(E)
        return {'x': jax.random.normal(ks[0], (B, S, E), dtype=jnp.float32), 'Wq': jax.random.normal(ks[1], (E, E), dtype=jnp.float32) * scale, 'bq': jnp.zeros((E,), dtype=jnp.float32), 'Wk': jax.random.normal(ks[2], (E, E), dtype=jnp.float32) * scale, 'bk': jnp.zeros((E,), dtype=jnp.float32), 'Wv': jax.random.normal(ks[3], (E, E), dtype=jnp.float32) * scale, 'bv': jnp.zeros((E,), dtype=jnp.float32), 'Wo': jax.random.normal(ks[4], (E, E), dtype=jnp.float32) * scale, 'bo': jnp.zeros((E,), dtype=jnp.float32), 'gamma': jnp.ones((E,), dtype=jnp.float32), 'beta': jnp.zeros((E,), dtype=jnp.float32)}
    _L0_attn_in = _L0_attn_setup()

    def _L0_ffn_setup():
        import jax, jax.numpy as jnp
        import numpy as np
        D, H, E, K = (128, 512, 8, 2)
        B, T = (2, 256)

        def _layernorm(x, g, b, eps=1e-05):
            mu = jnp.mean(x, axis=-1, keepdims=True)
            var = jnp.mean(jnp.square(x - mu), axis=-1, keepdims=True)
            return (x - mu) * jax.lax.rsqrt(var + eps) * g + b

        def _expert(x, g, b, W1, b1, W2, b2, Wo, bo):
            x = _layernorm(x, g, b)
            x1 = x @ W1 + b1
            x2 = jnp.clip(x @ W2 + b2, -20.0, 20.0)
            hidden = jnp.clip(x1 * (x2 * jax.nn.sigmoid(x2)), -10000.0, 10000.0)
            return jnp.clip(hidden @ Wo + bo, -10000.0, 10000.0)
        key = jax.random.key(seed)
        ks = jax.random.split(key, 6)
        s = 0.02
        return {'x': jax.random.normal(ks[0], (B, T, D), jnp.float32), 'ln_g': jnp.ones((D,), jnp.float32), 'ln_b': jnp.zeros((D,), jnp.float32), 'router_w': jax.random.normal(ks[1], (D, E), jnp.float32) * s, 'eg': jnp.ones((E, D), jnp.float32), 'eb': jnp.zeros((E, D), jnp.float32), 'W1': jax.random.normal(ks[2], (E, D, H), jnp.float32) * s, 'b1': jnp.zeros((E, H), jnp.float32), 'W2': jax.random.normal(ks[3], (E, D, H), jnp.float32) * s, 'b2': jnp.zeros((E, H), jnp.float32), 'Wo': jax.random.normal(ks[4], (E, H, D), jnp.float32) * s, 'bo': jnp.zeros((E, D), jnp.float32)}
    _L0_ffn_in = _L0_ffn_setup()
    _d = {'L0_attn_x': _L0_attn_in['x'], 'L0_attn_Wq': _L0_attn_in['Wq'], 'L0_attn_bq': _L0_attn_in['bq'], 'L0_attn_Wk': _L0_attn_in['Wk'], 'L0_attn_bk': _L0_attn_in['bk'], 'L0_attn_Wv': _L0_attn_in['Wv'], 'L0_attn_bv': _L0_attn_in['bv'], 'L0_attn_Wo': _L0_attn_in['Wo'], 'L0_attn_bo': _L0_attn_in['bo'], 'L0_attn_gamma': _L0_attn_in['gamma'], 'L0_attn_beta': _L0_attn_in['beta'], 'L0_ffn_ln_g': _L0_ffn_in['ln_g'], 'L0_ffn_ln_b': _L0_ffn_in['ln_b'], 'L0_ffn_router_w': _L0_ffn_in['router_w'], 'L0_ffn_eg': _L0_ffn_in['eg'], 'L0_ffn_eb': _L0_ffn_in['eb'], 'L0_ffn_W1': _L0_ffn_in['W1'], 'L0_ffn_b1': _L0_ffn_in['b1'], 'L0_ffn_W2': _L0_ffn_in['W2'], 'L0_ffn_b2': _L0_ffn_in['b2'], 'L0_ffn_Wo': _L0_ffn_in['Wo'], 'L0_ffn_bo': _L0_ffn_in['bo']}
    _x0 = _d['L0_attn_x']
    _d['L0_attn_x'] = jax.random.normal(jax.random.fold_in(jax.random.key(seed), 1), (16, 256, 128), dtype=_x0.dtype)
    del _x0
    return _d

def reference(L0_attn_x, L0_attn_Wq, L0_attn_bq, L0_attn_Wk, L0_attn_bk, L0_attn_Wv, L0_attn_bv, L0_attn_Wo, L0_attn_bo, L0_attn_gamma, L0_attn_beta, L0_ffn_ln_g, L0_ffn_ln_b, L0_ffn_router_w, L0_ffn_eg, L0_ffn_eb, L0_ffn_W1, L0_ffn_b1, L0_ffn_W2, L0_ffn_b2, L0_ffn_Wo, L0_ffn_bo):

    def _L0_attn_ref(x, Wq, bq, Wk, bk, Wv, bv, Wo, bo, gamma, beta):
        import jax, jax.numpy as jnp
        import numpy as np
        from math import sqrt
        E = 128
        H = 16
        HS = E // H
        EPS = 1e-08

        def _layer_norm(x, gamma, beta):
            mean = jnp.mean(x, axis=-1, keepdims=True)
            std = jnp.sqrt(jnp.mean((x - mean) ** 2, axis=-1, keepdims=True))
            return gamma * ((x - mean) / (std + EPS)) + beta
        B, S, _ = x.shape
        q = (x @ Wq + bq).reshape(B, H, S, HS)
        k = (x @ Wk + bk).reshape(B, H, S, HS)
        v = (x @ Wv + bv).reshape(B, H, S, HS)
        scores = jnp.einsum('bhqd,bhkd->bhqk', q, k) / sqrt(HS)
        attn = jax.nn.softmax(scores, axis=-1)
        out = jnp.einsum('bhqk,bhkd->bhqd', attn, v).reshape(B, S, E)
        out = out @ Wo + bo
        return _layer_norm(x + out, gamma, beta)

    def _L0_ffn_ref(x, ln_g, ln_b, router_w, eg, eb, W1, b1, W2, b2, Wo, bo):
        import jax, jax.numpy as jnp
        import numpy as np
        D, H, E, K = (128, 512, 8, 2)
        B, T = (2, 256)

        def _layernorm(x, g, b, eps=1e-05):
            mu = jnp.mean(x, axis=-1, keepdims=True)
            var = jnp.mean(jnp.square(x - mu), axis=-1, keepdims=True)
            return (x - mu) * jax.lax.rsqrt(var + eps) * g + b

        def _expert(x, g, b, W1, b1, W2, b2, Wo, bo):
            x = _layernorm(x, g, b)
            x1 = x @ W1 + b1
            x2 = jnp.clip(x @ W2 + b2, -20.0, 20.0)
            hidden = jnp.clip(x1 * (x2 * jax.nn.sigmoid(x2)), -10000.0, 10000.0)
            return jnp.clip(hidden @ Wo + bo, -10000.0, 10000.0)
        Bb, Tt, Dd = x.shape
        xf = _layernorm(x.reshape(-1, Dd), ln_g, ln_b)
        N = xf.shape[0]
        logits = xf @ router_w
        scores, idx = jax.lax.top_k(logits, K)
        gate = jax.nn.softmax(scores, axis=-1)
        gates_e = jnp.zeros((N, E), xf.dtype).at[jnp.arange(N)[:, None], idx].add(gate)

        def body(acc, p):
            gcol, g, b, w1, bb1, w2, bb2, wo, bbo = p
            return (acc + gcol[:, None] * _expert(xf, g, b, w1, bb1, w2, bb2, wo, bbo), None)
        out, _ = jax.lax.scan(body, jnp.zeros_like(xf), (gates_e.T, eg, eb, W1, b1, W2, b2, Wo, bo))
        return out.reshape(Bb, Tt, Dd)
    x = L0_attn_x
    x = x + _layernorm(_L0_attn_ref(_layernorm(x, axis=-1), L0_attn_Wq, L0_attn_bq, L0_attn_Wk, L0_attn_bk, L0_attn_Wv, L0_attn_bv, L0_attn_Wo, L0_attn_bo, L0_attn_gamma, L0_attn_beta), axis=-1)
    x = x + _layernorm(_L0_ffn_ref(_layernorm(x, axis=-1), L0_ffn_ln_g, L0_ffn_ln_b, L0_ffn_router_w, L0_ffn_eg, L0_ffn_eb, L0_ffn_W1, L0_ffn_b1, L0_ffn_W2, L0_ffn_b2, L0_ffn_Wo, L0_ffn_bo), axis=-1)
    return x

_drawn_inputs = setup_inputs


def setup_inputs(seed=0):
    import zlib

    import numpy as np

    out = dict(_drawn_inputs(seed))
    spreads = {'L0_attn_bq': (0.0, 0.1),
     'L0_attn_bk': (0.0, 0.1),
     'L0_attn_bv': (0.0, 0.1),
     'L0_attn_bo': (0.0, 0.1),
     'L0_attn_gamma': (1.0, 0.2),
     'L0_attn_beta': (0.0, 0.1),
     'L0_ffn_ln_g': (1.0, 0.2),
     'L0_ffn_ln_b': (0.0, 0.1),
     'L0_ffn_eg': (1.0, 0.6),
     'L0_ffn_eb': (0.0, 0.8),
     'L0_ffn_b1': (0.0, 0.295),
     'L0_ffn_b2': (0.0, 0.291),
     'L0_ffn_bo': (0.0, 0.1)}
    factors = {}
    for name, (base, spread) in spreads.items():
        noise = np.random.default_rng([zlib.crc32(name.encode()), seed]).standard_normal(out[name].shape)
        drawn = base * np.exp(spread * noise) if base else spread * noise
        out[name] = jnp.asarray(drawn.astype(out[name].dtype))
    for name, factor in factors.items():
        out[name] = (out[name] * factor).astype(out[name].dtype)
    return out
```

```python
from contextlib import ExitStack

import concourse.bass as bass
from concourse import mybir

F32 = mybir.dt.float32
F32R = mybir.dt.float32r
I32 = mybir.dt.int32
U32 = mybir.dt.uint32
ALU = mybir.AluOpType
ACT = mybir.ActivationFunctionType
AX = mybir.AxisListType

P = 128
BATCH, SEQ, D = 16, 256, 128
TOK = BATCH * SEQ
TILES = TOK // P
HEADS, HD = 16, 8
COLS = D // HD
RPH = SEQ // HEADS
SCALE = HD ** -0.5

STEP = 512
STEPS = TOK // STEP
TPS = STEP // P
UNITS = TOK // P
RING = 4
GROUPS = 2 * UNITS
ROUND = 2 * RING
PARTS = 4 * HD
ZERO_TO = 96
LAG_T, LAG_PV, LAG_OUT = 4, 5, 6
MAX_ROWS = 2


def attention(nc, io, keep):
    x_all, u_all, ident, numden = keep.x_all, keep.u_all, keep.ident, keep.numden
    with ExitStack() as ctx:
        def sb(name, shape, dt=F32):
            return ctx.enter_context(nc.sbuf_tensor(name, shape, dt))

        def ps(name, shape):
            return ctx.enter_context(nc.psum_tensor(name, shape, F32))

        def sem(name):
            return ctx.enter_context(nc.semaphore(name))

        def dram(name, shape, dt=F32):
            return nc.dram_tensor(name, shape, dt).ap()

        q_parts = dram("q_parts", [P, 4, TOK])
        k_parts = dram("k_parts", [P, 4, TOK])
        v_rows = dram("v_rows", [P, 4, TOK // 4])

        w_qkv = sb("w_qkv", [P, 3, D])
        b_qkv = sb("b_qkv", [P, 3])
        bo_all = sb("bo_all", [P, D])
        bn = sb("bn", [P, TILES, 6])
        mean = sb("mean", [P, TILES])
        var = sb("var", [P, TILES])
        rstd = sb("rstd", [P, TILES])
        tmp = sb("tmp", [P, 4, TILES])
        minus_half = sb("minus_half", [P, TILES])
        u_step = [sb(f"u_step{i}", [P, TPS, D]) for i in range(2)]
        ut = [sb(f"ut{i}", [P, STEP]) for i in range(2)]
        parts_out = [[sb(f"parts_out{i}{k}", [P, 2, STEP], F32R) for k in range(2)] for i in range(2)]
        v_out = [sb(f"v_out{i}", [P, STEP]) for i in range(2)]

        qt = [sb(f"qt{r}", [P, SEQ, 8], F32R) for r in range(RING)]
        kt = [sb(f"kt{r}", [P, SEQ, 8], F32R) for r in range(RING)]
        vs = [sb(f"vs{r}", [P, SEQ, 2]) for r in range(RING)]
        vt = [sb(f"vt{r}", [P, 2, 4, 32]) for r in range(2)]
        mx = [sb(f"mx{r}", [P, 2, 8]) for r in range(2)]
        mhl = [sb(f"mhl{r}", [P, MAX_ROWS, 2, 8], F32R) for r in range(2)]
        pt = [sb(f"pt{r}", [P, 4 * SEQ]) for r in range(4)]
        os_ = [sb(f"os{r}", [P, COLS, 64]) for r in range(2)]

        s_ps = [ps(f"s_ps{i}", [P, 512]) for i in range(2)]
        st_ps = [ps(f"st_ps{i}", [P, 2, 512]) for i in range(2)]
        pv_ps = ps("pv_ps", [P, 512])
        m_ps = ps("m_ps", [P, 512])
        ut_ps = s_ps
        qkv_ps = [st_ps[0][:, 0, :], st_ps[0][:, 1, :], st_ps[1][:, 0, :]]

        consts_in = sem("consts_in")
        x_in = [sem(f"x_in{i}") for i in range(2)]
        ident_ready = sem("ident_ready")
        half_ready = sem("half_ready")
        stats_ready = sem("stats_ready")
        chain = sem("chain")
        var_ready = sem("var_ready")
        rstd_ready = sem("rstd_ready")
        norm_ready = sem("norm_ready")
        ubo_ready = sem("ubo_ready")
        tp_ready = sem("tp_ready")
        ut_ready = sem("ut_ready")
        qkv_ready = sem("qkv_ready")
        hi_ready = sem("hi_ready")
        lo_ready = sem("lo_ready")
        v_ready = sem("v_ready")
        stored = [sem(f"stored{i}") for i in range(2)]
        q_cleared = sem("q_cleared")
        k_cleared = sem("k_cleared")
        v_cleared = sem("v_cleared")
        unit_in = [sem(f"unit_in{r}") for r in range(RING)]
        s_ready = sem("s_ready")
        max_ready = sem("max_ready")
        mh_ready = sem("mh_ready")
        ml_ready = sem("ml_ready")
        m_in = [sem(f"m_in{r}") for r in range(4)]
        st_ready = sem("st_ready")
        exp_ready = sem("exp_ready")
        vt_ready = sem("vt_ready")
        vp_ready = sem("vp_ready")
        pv_ready = sem("pv_ready")
        os_ready = sem("os_ready")
        numden_out = [sem(f"numden_out{i}") for i in range(2)]

        block = ctx.enter_context(nc.Block())

        def steps(eng, body):
            with eng.Fori(0, STEPS // 2) as it:
                for p in range(2):
                    body(it * 2 + p, p)

        def groups(eng, body, lag, peeled=1):
            for G in range(peeled * ROUND):
                body(G // ROUND, G % ROUND)
            with eng.Fori(peeled, GROUPS // ROUND) as it:
                for g in range(ROUND):
                    body(it, g)
            for G in range(GROUPS, GROUPS + lag):
                body(G // ROUND, G % ROUND)

        def present(G, lag, total=GROUPS):
            return not isinstance(G, int) or 0 <= G - lag < total

        def unit_of(R, g, lag):
            return R * RING + (g - lag) // 2

        def pair_of(R, g, lag):
            return R * (RING // 2) + (g - lag) // 4

        def m_in_count(R, g, lag):
            return R * (32 * RING // 2) + 32 * ((g - lag) // 4 + 1)

        def s_at_least(s, n):
            return not isinstance(s, int) or s >= n

        def stores_before(s, p):
            return (s - p) * 40

        @block.sync
        def _(sp):
            for n, name in enumerate(("Wq", "Wk", "Wv")):
                sp.dma_start(w_qkv[:, n, :], io[name]).then_inc(consts_in, 16)
            for n, name in enumerate(("bq", "bk", "bv")):
                sp.dma_start(b_qkv[:, n:n + 1], io[name].rearrange("(p o) -> p o", o=1)).then_inc(consts_in, 16)
            sp.dma_start(bo_all[:, :], io["bo"].rearrange("(o d) -> o d", o=1).broadcast_to([P, D])).then_inc(consts_in, 16)
            xt = io["x"].rearrange("b (t p) d -> p (b t) d", p=P)
            for i in range(2):
                half = slice(i * TILES // 2, (i + 1) * TILES // 2)
                sp.dma_start(x_all[:, half, :], xt[:, half, :]).then_inc(x_in[i], 16)

            def store(s, p):
                at = bass.ds(s * STEP, STEP)
                for k, parts in enumerate((q_parts, k_parts)):
                    sp.wait_ge(lo_ready, 2 * s + k + 1)
                    src = parts_out[p][k][:, :, :].bitcast(F32)
                    sp.dma_start(parts[:, 0:2, at], src).then_inc(stored[p], 16)
                    sp.dma_start(parts[:, 2:4, at], src[:, ::-1, :] if k else src).then_inc(stored[p], 16)
                sp.wait_ge(v_ready, 4 * s + 4)
                sp.dma_start(v_rows[:, :, bass.ds(s * (STEP // 4), STEP // 4)],
                             v_out[p][:, :].rearrange("p (j t) -> p j t", j=4)).then_inc(stored[p], 16)

            steps(sp, store)

            for p in range(2):
                sp.wait_ge(stored[p], 16 * 5 * STEPS // 2)
            sp.wait_ge(q_cleared, RING)
            sp.wait_ge(k_cleared, 2 * RING)

            def load(U, r, reuse):
                if reuse:
                    sp.wait_ge(st_ready, 4 * U - 4 * RING + 4)
                    sp.wait_ge(q_cleared, RING)
                    sp.wait_ge(vt_ready, 2 * U - 2 * RING + 2)
                at = bass.ds(U * P, P)
                for dst, src in ((qt[r], q_parts), (kt[r], k_parts)):
                    sp.dma_start(dst[0:PARTS, :, :].bitcast(F32).rearrange("d (c r) h -> d c (r h)", c=COLS),
                                 src[:, :, bass.ds(U * P, P)].rearrange("(c d) a t -> (d a) c t", d=HD)).then_inc(unit_in[r], 16)
                sp.dma_start(vs[r][0:PARTS, :, :].rearrange("d (c r) i -> d c (r i)", c=COLS),
                             v_rows[:, :, bass.ds(U * 32, 32)].rearrange("(c d) j t -> (d j) c t", d=HD)).then_inc(unit_in[r], 16)

            def numden_store(K, p):
                sp.wait_ge(os_ready, 4 * K + 4)
                for j in range(4):
                    dst = numden[:, :, bass.ds(K * 2 * P + 64 * j, 64)].rearrange("c d t -> d c t")
                    sp.dma_start(dst, os_[p][32 * j:32 * j + 2 * HD, :, :]).then_inc(numden_out[p], 16)

            def group(R, g):
                G = R * ROUND + g
                if g % 4 == 0 and present(G, 12):
                    numden_store(pair_of(R, g, 12), (g - 12) // 4 % 2)
                if g % 2 == 0 and present(G, 0):
                    load(unit_of(R, g, 0), g // 2, not isinstance(G, int) or G >= ROUND)
                if g % 2 == 0 and present(G, 4):
                    sp.wait_ge(ml_ready, unit_of(R, g, 4) + 1)
                    r = (g - 4) % ROUND // 2
                    for o in range(MAX_ROWS):
                        dst = qt[r][ZERO_TO + o:ZERO_TO + o + 1, :, :].bitcast(F32)
                        sp.dma_start(dst.rearrange("o (p a) h -> o p (a h)", a=2),
                                     mhl[r % 2][:, o].bitcast(F32).rearrange("p a h -> p (a h)")).then_inc(m_in[r % 2], 16)

            groups(sp, group, 9, 2)
            for p in range(2):
                sp.wait_ge(numden_out[p], 16 * 4 * UNITS // 4)

        @block.gpsimd
        def _(pool):
            pool.memset(ident[:, :], 0.0).then_inc(ident_ready, 1)
            pool.wait_ge(ident_ready, 1)
            pool.affine_select(out=ident[:, :], in_=ident[:, :], compare_op=ALU.not_equal, fill=1.0, base=0,
                               pattern=[[-1, P]], channel_multiplier=1).then_inc(ident_ready, 1)
            pool.memset(minus_half[:, :], -0.5).then_inc(half_ready, 1)
            for r in range(RING):
                pool.memset(qt[r][:, :, :].bitcast(F32), 0.0).then_inc(q_cleared, 1)
            pool.wait_ge(half_ready, 1)
            pool.wait_ge(var_ready, 1)
            pool.tensor_tensor(rstd[:, :], var[:, :], minus_half[:, :], ALU.pow).then_inc(rstd_ready, 1)
            pool.wait_ge(consts_in, 7 * 16)

            def residual(s, p):
                for t in range(TPS):
                    pool.wait_ge(norm_ready, TPS * s + t + 1)
                    pool.tensor_tensor(u_all[:, bass.ds(TPS * s + t, 1), :].rearrange("p o d -> p (o d)"),
                                       u_step[p][:, t, :], bo_all[:, :], ALU.add).then_inc(ubo_ready, 1)

            steps(pool, residual)

        def numden_before(R, g):
            return R * 64 + 64 * ((g - LAG_OUT) // 8)

        @block.scalar
        def _(act):
            act.wait_ge(consts_in, 7 * 16)

            def evacuate(s, p):
                act.wait_ge(tp_ready, s + 1)
                if s_at_least(s, 2):
                    act.wait_ge(qkv_ready, 3 * s - 3)
                act.activation(ut[p][:, :].rearrange("p (t r h) -> p t h r", t=TPS, h=8),
                               ut_ps[p][:, :].rearrange("p (t h r) -> p t h r", t=TPS, h=8), ACT.Copy).then_inc(ut_ready, 1)
                if s_at_least(s, 2):
                    act.wait_ge(stored[p], stores_before(s, p))
                for k in range(2):
                    act.wait_ge(qkv_ready, 3 * s + k + 1)
                    act.activation(parts_out[p][k][:, 0, :], qkv_ps[k], ACT.Identity, bias=b_qkv[:, k:k + 1])\
                        .then_inc(hi_ready, 1)
                act.wait_ge(qkv_ready, 3 * s + 3)
                for j in range(4):
                    act.activation(v_out[p][:, :].rearrange("p (j t r i) -> p j t r i", t=TPS, j=4, i=2)[:, j],
                                   qkv_ps[2].rearrange("p (t r i j) -> p j t r i", t=TPS, j=4, i=2)[:, j],
                                   ACT.Identity, bias=b_qkv[:, 2:3]).then_inc(v_ready, 1)

            for s in range(2):
                evacuate(s, s)
            with act.Fori(1, STEPS // 2) as it:
                for p in range(2):
                    evacuate(it * 2 + p, p)

            def group(R, g):
                G = R * ROUND + g
                if present(G, LAG_OUT):
                    f = (g - LAG_OUT) % ROUND
                    act.wait_ge(pv_ready, G - LAG_OUT + 1)
                    if f % 4 == 0 and (not isinstance(G, int) or G - LAG_OUT >= 8):
                        act.wait_ge(numden_out[f // 4], numden_before(R, g))
                    at = (f % 4) * RPH
                    act.activation(os_[f // 4][:, :, at:at + RPH],
                                   pv_ps[:, 0:SEQ].rearrange("p (c r) -> p c r", r=RPH), ACT.Copy).then_inc(os_ready, 1)
                if present(G, LAG_T):
                    f = (g - LAG_T) % ROUND
                    for pair in range(2):
                        act.wait_ge(st_ready, 2 * (G - LAG_T) + pair + 1)
                        if not isinstance(G, int) or G - LAG_T >= 2:
                            act.wait_ge(pv_ready, G - LAG_T - 1)
                        if pair == 1:
                            act.wait_ge(vt_ready, G - LAG_T + 1)
                            act.activation(vt[f % 2][:, :, :, 0:HD], m_ps[:, 0:64].rearrange("p (a d j) -> p a j d", a=2, j=4),
                                           ACT.Copy).then_inc(vp_ready, 1)
                        act.activation(pt[(2 * f + pair) % 4][:, :], st_ps[pair][:, :, :].rearrange("p a b -> p (a b)"),
                                       ACT.Exp, scale=SCALE).then_inc(exp_ready, 1)

            act.wait_ge(v_cleared, 2)
            groups(act, group, LAG_OUT)

        @block.vector
        def _(dve):
            for r in range(RING):
                dve.memset(kt[r][0:ZERO_TO, :, :].bitcast(F32), 0.0).then_inc(k_cleared, 1)
                dve.memset(kt[r][ZERO_TO:P, :, :].bitcast(F32), 1.0).then_inc(k_cleared, 1)
                
            for r in range(2):
                dve.memset(vt[r][:, :, :, :], 1.0).then_inc(v_cleared, 1)
            for i in range(2):
                dve.wait_ge(x_in[i], 16)
                with dve.Fori(i * TILES // 8, (i + 1) * TILES // 8) as it:
                    for t in range(4):
                        dve.bn_stats(bn[:, bass.ds(it * 4 + t, 1), :].rearrange("p o s -> p (o s)"),
                                     x_all[:, bass.ds(it * 4 + t, 1), :].rearrange("p o d -> p (o d)")).then_inc(stats_ready, 1)
            dve.wait_ge(stats_ready, TILES)
            dve.tensor_tensor(tmp[:, 0, :], bn[:, :, 1], bn[:, :, 4], ALU.add).then_inc(chain, 1)
            dve.tensor_tensor(tmp[:, 1, :], bn[:, :, 1], bn[:, :, 4], ALU.subtract).then_inc(chain, 1)
            dve.tensor_tensor(tmp[:, 2, :], bn[:, :, 2], bn[:, :, 5], ALU.add).then_inc(chain, 1)
            dve.wait_ge(chain, 3)
            dve.tensor_scalar(mean[:, :], tmp[:, 0, :], 0.5, None, ALU.mult).then_inc(chain, 1)
            dve.scalar_tensor_tensor(var[:, :], tmp[:, 1, :], 0.25, tmp[:, 1, :], ALU.mult, ALU.mult).then_inc(chain, 1)
            dve.tensor_scalar(tmp[:, 3, :], tmp[:, 2, :], 1.0 / D, 1e-5, ALU.mult, ALU.add).then_inc(chain, 1)
            dve.wait_ge(chain, 6)
            dve.tensor_tensor(var[:, :], var[:, :], tmp[:, 3, :], ALU.add).then_inc(var_ready, 1)
            dve.wait_ge(rstd_ready, 1)

            def normalise(s, p):
                if s_at_least(s, 2):
                    dve.wait_ge(tp_ready, s - 1)
                    dve.wait_ge(ubo_ready, TPS * s - TPS)
                for t in range(TPS):
                    at = bass.ds(TPS * s + t, 1)
                    dve.tensor_scalar(u_step[p][:, t, :], x_all[:, at, :].rearrange("p o d -> p (o d)"), mean[:, at], rstd[:, at],
                                      ALU.subtract, ALU.mult).then_inc(norm_ready, 1)

            def low_parts(s, p):
                if s_at_least(s, 2):
                    dve.wait_ge(stored[p], stores_before(s, p))
                for k in range(2):
                    dve.wait_ge(hi_ready, 2 * s + k + 1)
                    dve.scalar_tensor_tensor(parts_out[p][k][:, 1, :], qkv_ps[k], b_qkv[:, k:k + 1],
                                             parts_out[p][k][:, 0, :].bitcast(F32), ALU.add, ALU.subtract).then_inc(lo_ready, 1)

            dve.wait_ge(consts_in, 7 * 16)
            normalise(0, 0)
            normalise(1, 1)
            low_parts(0, 0)
            with dve.Fori(1, STEPS // 2) as it:
                normalise(it * 2, 0)
                low_parts(it * 2 - 1, 1)
                normalise(it * 2 + 1, 1)
                low_parts(it * 2, 0)
            low_parts(STEPS - 1, 1)

            def group(R, g):
                G = R * ROUND + g
                m = g // 2 % 2
                if g % 2 == 0 and (not isinstance(G, int) or G >= 4):
                    dve.wait_ge(ml_ready, unit_of(R, g, 2))
                for j in range(4):
                    dve.wait_ge(s_ready, 4 * G + j + 1)
                    dve.tensor_reduce(mx[m][:, :, 4 * (g % 2) + j], s_ps[j % 2][:, :].rearrange("p (a k) -> p a k", a=2),
                                      AX.X, ALU.max).then_inc(max_ready, 1)
                if g % 2 == 1:
                    dve.wait_ge(max_ready, 4 * G + 4)
                    if not isinstance(G, int) or G >= 4:
                        dve.wait_ge(m_in[m], m_in_count(R, g, 4))
                    high, low = mhl[m][:, 0], mhl[m][:, 1]
                    dve.tensor_scalar(high, mx[m][:, :, :], -1.0, None, ALU.mult).then_inc(mh_ready, 1)
                    dve.wait_ge(mh_ready, unit_of(R, g, 0) + 1)
                    dve.scalar_tensor_tensor(low, mx[m][:, :, :], -1.0, high.bitcast(F32),
                                             ALU.mult, ALU.subtract).then_inc(ml_ready, 1)

            groups(dve, group, 0)

        @block.tensor
        def _(pe):
            pe.wait_ge(ident_ready, 2)
            pe.wait_ge(consts_in, 7 * 16)

            def transposes(s, p):
                if s_at_least(s, 2):
                    pe.wait_ge(ut_ready, s - 1)
                for t in range(TPS):
                    pe.wait_ge(norm_ready, TPS * s + t + 1)
                    mm = pe.transpose(ut_ps[p][:, t * P:(t + 1) * P], u_step[p][:, t, :], ident[:, :])
                mm.then_inc(tp_ready, 1)

            def project(s, p):
                pe.wait_ge(ut_ready, s + 1)
                for k in range(3):
                    if s_at_least(s, 1):
                        if k < 2:
                            pe.wait_ge(lo_ready, 2 * s + k - 1)
                        else:
                            pe.wait_ge(v_ready, 4 * s)
                    pe.matmul(qkv_ps[k], w_qkv[:, k, :], ut[p][:, :], start=True, stop=True).then_inc(qkv_ready, 1)

            transposes(0, 0)
            transposes(1, 1)
            project(0, 0)
            with pe.Fori(1, STEPS // 2) as it:
                transposes(it * 2, 0)
                project(it * 2 - 1, 1)
                transposes(it * 2 + 1, 1)
                project(it * 2, 0)
            project(STEPS - 1, 1)

            pe.wait_ge(lo_ready, 2 * STEPS)
            pe.wait_ge(v_ready, 4 * STEPS)

            def scores(R, G, g, j):
                r = g // 2 % RING
                if j == 0 and g % 2 == 0:
                    pe.wait_ge(unit_in[r], unit_count(R, g))
                if not isinstance(G, int) or 4 * G + j >= 2:
                    pe.wait_ge(max_ready, 4 * G + j - 1)
                for a in range(2):
                    mm = pe.matmul(s_ps[j % 2][:, a * SEQ:(a + 1) * SEQ],
                                   qt[r][0:ZERO_TO, a::2, 4 * (g % 2) + j],
                                   kt[r][0:ZERO_TO, :, 4 * (g % 2) + j], start=True, stop=True)
                mm.then_inc(s_ready, 1)

            def scores_t(R, G, g, j):
                f = (g - LAG_T) % ROUND
                r = f // 2
                if j == 0 and f % 2 == 0:
                    pe.wait_ge(m_in[r % 2], m_in_count(R, g, LAG_T))
                n = 2 * (G - LAG_T) + j // 2
                if j % 2 == 0 and (not isinstance(G, int) or n >= 2):
                    pe.wait_ge(exp_ready, n - 1)
                for a in range(2):
                    mm = pe.matmul(st_ps[j // 2][:, j % 2, a * SEQ:(a + 1) * SEQ],
                                   kt[r][0:ZERO_TO + MAX_ROWS, a::2, 4 * (f % 2) + j],
                                   qt[r][0:ZERO_TO + MAX_ROWS, :, 4 * (f % 2) + j], start=True, stop=True)
                if j % 2 == 1:
                    mm.then_inc(st_ready, 1)

            def values(g):
                f = (g - LAG_T) % ROUND
                for a in range(2):
                    mm = pe.transpose(m_ps[:, a * 32:(a + 1) * 32], vs[f // 2][0:PARTS, a::2, f % 2], ident[0:PARTS, 0:PARTS])
                mm.then_inc(vt_ready, 1)

            def weigh(G, g):
                f = (g - LAG_PV) % ROUND
                pe.wait_ge(exp_ready, 2 * (G - LAG_PV) + 2)
                pe.wait_ge(vp_ready, G - LAG_PV + 1)
                if not isinstance(G, int) or G - LAG_PV >= 1:
                    pe.wait_ge(os_ready, G - LAG_PV)
                for a in range(2):
                    for j in range(4):
                        mm = pe.matmul(pv_ps[32 * j:32 * j + 32, 0:SEQ], vt[f % 2][:, a, j, :],
                                       pt[(2 * f + j // 2) % 4][:, (2 * (j % 2) + a) * SEQ:(2 * (j % 2) + a + 1) * SEQ],
                                       start=(a == 0), stop=(a == 1))
                mm.then_inc(pv_ready, 1)

            def group(R, g):
                G = R * ROUND + g
                for j in range(4):
                    if j == 3 and present(G, LAG_T + 1):
                        pe.wait_ge(vp_ready, G - LAG_T)
                    if present(G, 0):
                        scores(R, G, g, j)
                    if j == 3 and present(G, LAG_T):
                        values(g)
                    if present(G, LAG_T):
                        scores_t(R, G, g, j)
                if present(G, LAG_PV):
                    weigh(G, g)

            def unit_count(R, g):
                return R * 48 + 48

            groups(pe, group, LAG_PV)



EXPERTS, HID = 8, 512
CHUNKS = HID // P
SLOTS = 2 * TOK // P + EXPERTS
BLOCKS = EXPERTS * TOK // P + SLOTS - 2 * TOK // P
DUMP = 2 * TOK
FROUND = 8


def routing(nc, io, keep):
    K = keep
    with ExitStack() as ctx:
        def sb(name, shape, dt=F32):
            return ctx.enter_context(nc.sbuf_tensor(name, shape, dt))

        def ps(name, shape):
            return ctx.enter_context(nc.psum_tensor(name, shape, F32))

        def sem(name):
            return ctx.enter_context(nc.semaphore(name))

        wo = sb("wo", [P, D])
        vecs = sb("vecs", [P, 4, D])
        router = sb("router", [P, EXPERTS])
        nt = [sb(f"nt{p}", [P, 2 * P]) for p in range(2)]
        dt_ = [sb(f"dt{p}", [P, 2 * P]) for p in range(2)]
        rt = [sb(f"rt{p}", [P, 2 * P]) for p in range(2)]
        ot = [sb(f"ot{p}", [P, 2 * P]) for p in range(2)]
        y = sb("y", [P, TILES, D])
        z = sb("z", [P, TILES, D])
        nobody = sb("nobody", [P, BLOCKS, 2], U32)
        zero = sb("zero", [1, D])
        stage = [sb(f"stage{p}", [P, D]) for p in range(2)]
        xft = [sb(f"xft{p}", [P, D]) for p in range(2)]
        bn = sb("bn2", [P, TILES, 6])
        sm = sb("sm", [P, 12, TILES])
        consts = sb("consts", [P, 2, TILES])
        logits = sb("logits", [P, TILES, EXPERTS])
        big = sb("big", [P, 2, TILES * EXPERTS * EXPERTS])
        before = sb("before", [P, EXPERTS, EXPERTS])
        tri = sb("tri", [P, P])
        ones = sb("ones", [P, P])
        region = sb("region", [P, EXPERTS])
        keep_on = sb("keep_on", [P, EXPERTS, TILES])
        sel = sb("sel", [P, 3, TILES, EXPERTS])
        work = sb("work", [P, 8, TILES, EXPERTS])
        slot_f = sb("slot_f", [P, 2, TILES])
        slot = sb("slot", [P, 2, TILES], U32)
        slot_i = sb("slot_i", [P, 2, TILES], I32)
        lane_i = sb("lane_i", [P, 2, TILES], I32)
        block_f = sb("block_f", [P, 2, TILES])
        slot_c = [sb(f"slot_c{p}", [P, 2], U32) for p in range(2)]
        ids = sb("ids", [P, TILES, 2, 2], U32)
        ids_c = [sb(f"ids_c{p}", [P, 4], U32) for p in range(2)]
        tiles_i = sb("tiles_i", [P, SLOTS])
        chunk = sb("chunk", [P, TILES])
        ex = sb("ex", [P, 8, EXPERTS])
        tl = sb("tl", [P, 6, SLOTS])
        tex = sb("tex", [P, 3, SLOTS, EXPERTS])

        yp = [ps(f"yp{p}", [P, 2, D]) for p in range(2)]
        tp = [ps(f"tp{p}", [P, P]) for p in range(2)]
        lp = ps("lp", [P, TILES, EXPERTS])
        cp = ps("cp", [P, 2, TILES * EXPERTS])

        params_in = sem("params_in")
        nd_in = [sem(f"nd_in{p}") for p in range(2)]
        ot_ready = sem("ot_ready")
        rt_ready = sem("rt_ready")
        yp_ready = sem("yp_ready")
        y_ready = sem("y_ready")
        dchain = sem("dchain")
        v_to_pow = sem("v_to_pow")
        pow_done = sem("pow_done")
        gconst = sem("gconst")
        stage_ready = sem("stage_ready")
        tp_done = sem("tp_done")
        xft_ready = sem("xft_ready")
        lp_ready = sem("lp_ready")
        sel_ready = sem("sel_ready")
        cp_ready = sem("cp_ready")
        slot_ready = sem("slot_ready")
        rows_ready = sem("rows_ready")
        rows_out = sem("rows_out")
        filled_out = sem("filled_out")
        row_copied = sem("row_copied")
        sent = [sem(f"sent{p}") for p in range(2)]
        score_ready = sem("score_ready")
        exp_done = sem("exp_done")

        block = ctx.enter_context(nc.Block())

        def pairs(eng, body, n=UNITS // 2):
            for k in range(2):
                body(k, k)
            with eng.Fori(1, n // 2) as it:
                for p in range(2):
                    body(it * 2 + p, p)

        def late(k, n):
            return not isinstance(k, int) or k >= n

        @block.sync
        def _(sp):
            sp.dma_start(wo[:, :], io["Wo"]).then_inc(params_in, 16)
            for n, name in enumerate(("gamma", "beta", "ln_g", "ln_b")):
                sp.dma_start(vecs[:, n, :], io[name].rearrange("(o d) -> o d", o=1).broadcast_to([P, D])).then_inc(params_in, 16)
            sp.dma_start(router[:, :], io["router_w"]).then_inc(params_in, 16)

            def load(k, p):
                if late(k, 2):
                    sp.wait_ge(ot_ready, 4 * k - 4)
                at = bass.ds(k * 2 * P, 2 * P)
                sp.dma_start(nt[p][:, :], K.numden[:, 0:HD, at].rearrange("c d t -> c d t")).then_inc(nd_in[p], 16)
                sp.dma_start(dt_[p][:, :], K.numden[:, HD:2 * HD, at]).then_inc(nd_in[p], 16)

            pairs(sp, load)
            sp.wait_ge(gconst, 19)
            sp.dma_start(K.dispatch.rearrange("(p b) k -> p (b k)", p=P), nobody[:, :, :].rearrange("p b k -> p (b k)")).then_inc(filled_out, 16)
            sp.dma_start(K.z_rows[TOK:TOK + 1, :], zero[:, :]).then_inc(rows_out, 16)
            sp.wait_ge(rows_ready, 1)
            sp.dma_start(K.z_rows[0:TOK, :].rearrange("(t p) d -> p t d", p=P), z[:, :, :]).then_inc(rows_out, 16)
            sp.wait_ge(rows_out, 32)

        @block.gpsimd
        def _(pool):
            pool.memset(consts[:, 0, :], -0.5).then_inc(gconst, 1)
            pool.memset(consts[:, 1, :], 0.5).then_inc(gconst, 1)
            pool.memset(tri[:, :], 1.0).then_inc(gconst, 1)
            pool.memset(ones[:, :], 1.0).then_inc(gconst, 1)
            pool.memset(before[:, :, :], 1.0).then_inc(gconst, 1)
            pool.memset(keep_on[:, :, :], 1.0).then_inc(gconst, 1)
            pool.wait_ge(gconst, 6)
            pool.affine_select(out=tri[:, :], in_=tri[:, :], compare_op=ALU.is_gt, fill=0.0, base=0,
                               pattern=[[1, P]], channel_multiplier=-1).then_inc(gconst, 1)
            pool.affine_select(out=before[:, :, :], in_=before[:, :, :], compare_op=ALU.is_gt, fill=0.0, base=0,
                               pattern=[[1, EXPERTS], [-1, EXPERTS]], channel_multiplier=0).then_inc(gconst, 1)
            pool.affine_select(out=keep_on[:, :, :], in_=keep_on[:, :, :], compare_op=ALU.is_gt, fill=0.0, base=0,
                               pattern=[[0, EXPERTS], [1, TILES]], channel_multiplier=0).then_inc(gconst, 1)
            pool.memset(zero[:, :], 0.0).then_inc(gconst, 1)
            pool.iota(region[:, :], [[TOK // P, EXPERTS]], base=0, channel_multiplier=0,
                      allow_small_or_imprecise_dtypes=True).then_inc(gconst, 1)
            for k in range(2):
                pool.iota(ids[:, :, k, 0], [[P, TILES]], base=0, channel_multiplier=1).then_inc(gconst, 1)
                pool.iota(ids[:, :, k, 1], [[2 * P, TILES]], base=k, channel_multiplier=2).then_inc(gconst, 1)
            pool.iota(tiles_i[:, :], [[1, SLOTS]], base=0, channel_multiplier=0,
                      allow_small_or_imprecise_dtypes=True).then_inc(gconst, 1)
            pool.iota(chunk[:, :], [[P, TILES]], base=0, channel_multiplier=0,
                      allow_small_or_imprecise_dtypes=True).then_inc(gconst, 1)
            pool.iota(nobody[:, :, 0], [[0, BLOCKS]], base=TOK, channel_multiplier=0).then_inc(gconst, 1)
            pool.iota(nobody[:, :, 1], [[P, BLOCKS]], base=DUMP, channel_multiplier=1).then_inc(gconst, 1)
            for n, exponent in enumerate((1, 0, 0, 0, 0)):
                pool.wait_ge(v_to_pow, n + 1)
                pool.tensor_tensor(sm[:, 11, :], sm[:, 10, :], consts[:, exponent, :], ALU.pow).then_inc(pow_done, 1)
            pool.wait_ge(slot_ready, 1)
            pool.wait_ge(filled_out, 16)
            pool.wait_ge(gconst, 19)

            def send(t, p):
                if late(t, 2):
                    pool.wait_ge(sent[p], (t - p) * 16)
                at = bass.ds(t, 1)
                pool.tensor_copy(slot_c[p][:, :], slot[:, :, at].rearrange("p k o -> p (k o)")).then_inc(row_copied, 1)
                pool.tensor_copy(ids_c[p][:, :], ids[:, at, :, :].rearrange("p o k a -> p (o k a)")).then_inc(row_copied, 1)
                pool.wait_ge(row_copied, 2 * t + 2)
                pool.nop(nofuse=True)
                for k in range(2):
                    pool.indirect_dma_start(K.dispatch[:, :], bass.IndirectOffsetOnAxis(slot_c[p][:, k:k + 1], 0),
                                            ids_c[p][:, 2 * k:2 * k + 2], None).then_inc(sent[p], 16)

            for t in range(2):
                send(t, t)
            with pool.Fori(1, TILES // 2) as it:
                for p in range(2):
                    send(it * 2 + p, p)
            for p in range(2):
                pool.wait_ge(sent[p], 16 * TILES)

        @block.scalar
        def _(act):
            def turned(t, p):
                act.wait_ge(tp_done, t + 1)
                if late(t, 2):
                    act.wait_ge(lp_ready, t - 1)
                act.activation(xft[p][:, :], tp[p][:, :], ACT.Copy).then_inc(xft_ready, 1)

            pairs(act, turned, TILES)
            act.wait_ge(score_ready, 1)
            act.activation(work[:, 1, :, :], work[:, 0, :, :], ACT.Exp).then_inc(exp_done, 1)

        @block.tensor
        def _(pe):
            pe.wait_ge(params_in, 6 * 16)

            def project(k, p):
                pe.wait_ge(ot_ready, 4 * k + 4)
                if late(k, 2):
                    pe.wait_ge(y_ready, k - 1)
                for u in range(2):
                    mm = pe.matmul(yp[p][:, u, :], ot[p][:, u * P:(u + 1) * P], wo[:, :], start=True, stop=True)
                mm.then_inc(yp_ready, 1)

            pairs(pe, project)

            def score(t, p):
                pe.wait_ge(stage_ready, t + 1)
                if late(t, 2):
                    pe.wait_ge(xft_ready, t - 1)
                pe.transpose(tp[p][:, :], stage[p][:, :], K.ident[:, :]).then_inc(tp_done, 1)
                pe.wait_ge(xft_ready, t + 1)
                pe.matmul(lp[:, bass.ds(t, 1), :].rearrange("p o e -> p (o e)"), xft[p][:, :], router[:, :],
                          start=True, stop=True).then_inc(lp_ready, 1)

            pairs(pe, score, TILES)
            pe.wait_ge(sel_ready, 1)
            pe.wait_ge(gconst, 7)
            chosen = sel[:, 2, :, :].rearrange("p t e -> p (t e)")
            pe.matmul(cp[:, 0, :], tri[:, :], chosen, start=True, stop=True)
            pe.matmul(cp[:, 1, :], ones[:, :], chosen, start=True, stop=True, skip_group_check=True).then_inc(cp_ready, 1)

        @block.vector
        def _(dve):
            count = [0]

            def settled(*made):
                for ins in made:
                    ins.then_inc(dchain, 1)
                    count[0] += 1
                dve.wait_ge(dchain, count[0])

            dve.wait_ge(params_in, 6 * 16)
            dve.wait_ge(gconst, 19)

            def attend(k, p):
                dve.wait_ge(nd_in[p], (k - p) * 16 + 32)
                if late(k, 2):
                    dve.wait_ge(yp_ready, k - 1)
                dve.reciprocal(rt[p][:, :], dt_[p][:, :]).then_inc(rt_ready, 1)
                dve.wait_ge(rt_ready, k + 1)
                for u in range(2):
                    for i in range(2):
                        a, b = (x[p][:, :].rearrange("p (j u i r) -> p u i j r", j=4, u=2, i=2)[:, u, i] for x in (nt, rt))
                        dve.tensor_tensor(ot[p][:, :].rearrange("p (u i j r) -> p u i j r", u=2, i=2, j=4)[:, u, i], a, b,
                                          ALU.mult).then_inc(ot_ready, 1)
                dve.wait_ge(yp_ready, k + 1)
                at = bass.ds(2 * k, 2)
                dve.tensor_tensor(y[:, at, :], yp[p][:, :, :], K.u_all[:, at, :], ALU.add).then_inc(y_ready, 1)

            pairs(dve, attend)
            dve.wait_ge(y_ready, UNITS // 2)

            passes = [0]

            def moments(src, mean, var):
                with dve.Fori(0, TILES // 4) as it:
                    for t in range(4):
                        at = bass.ds(it * 4 + t, 1)
                        dve.bn_stats(bn[:, at, :].rearrange("p o s -> p (o s)"),
                                     src[:, at, :].rearrange("p o d -> p (o d)")).then_inc(dchain, 1)
                count[0] += TILES
                dve.wait_ge(dchain, count[0])
                settled(dve.tensor_tensor(sm[:, 0, :], bn[:, :, 1], bn[:, :, 4], ALU.add),
                        dve.tensor_tensor(sm[:, 1, :], bn[:, :, 1], bn[:, :, 4], ALU.subtract),
                        dve.tensor_tensor(sm[:, 2, :], bn[:, :, 2], bn[:, :, 5], ALU.add))
                settled(dve.tensor_scalar(mean, sm[:, 0, :], 0.5, None, ALU.mult),
                        dve.scalar_tensor_tensor(sm[:, 3, :], sm[:, 1, :], 0.25, sm[:, 1, :], ALU.mult, ALU.mult))
                settled(dve.scalar_tensor_tensor(var, sm[:, 2, :], 1.0 / D, sm[:, 3, :], ALU.mult, ALU.add))

            def power(src, eps):
                passes[0] += 1
                dve.tensor_scalar(sm[:, 10, :], src, eps, None, ALU.add).then_inc(v_to_pow, 1)
                dve.wait_ge(pow_done, passes[0])

            def by_row(v):
                return v.rearrange("p (t o) -> p t o", o=1).broadcast_to([P, TILES, D])

            def by_column(n):
                return vecs[:, n:n + 1, :].broadcast_to([P, TILES, D])

            def normalise(dst, src, mean, scale):
                settled(dve.tensor_tensor(dst, src, by_row(mean), ALU.subtract))
                settled(dve.tensor_tensor(dst, dst, by_row(scale), ALU.mult))

            Y, Z, X = y[:, :, :], z[:, :, :], K.x_all[:, :, :]
            mean, var, r1, r2 = (sm[:, n, :] for n in (4, 5, 6, 7))
            moments(y, mean, var)
            power(var, 0.0)
            settled(dve.tensor_scalar(r2, sm[:, 11, :], 1e-8, None, ALU.add))
            settled(dve.reciprocal(r1, r2))
            normalise(Y, Y, mean, r1)
            settled(dve.tensor_tensor(Y, Y, by_column(0), ALU.mult))
            settled(dve.tensor_tensor(Y, Y, by_column(1), ALU.add))
            moments(y, mean, var)
            power(var, 1e-5)
            normalise(Y, Y, mean, sm[:, 11, :])
            settled(dve.tensor_tensor(X, X, Y, ALU.add))
            moments(K.x_all, mean, var)
            power(var, 1e-5)
            normalise(Y, X, mean, sm[:, 11, :])
            moments(y, mean, var)
            power(var, 1e-5)
            normalise(Y, Y, mean, sm[:, 11, :])
            settled(dve.tensor_tensor(Y, Y, by_column(2), ALU.mult))
            settled(dve.tensor_tensor(Y, Y, by_column(3), ALU.add))

            def show(t, p):
                if late(t, 2):
                    dve.wait_ge(tp_done, t - 1)
                dve.tensor_copy(stage[p][:, :], y[:, bass.ds(t, 1), :].rearrange("p o d -> p (o d)")).then_inc(stage_ready, 1)

            pairs(dve, show, TILES)
            moments(y, mean, var)
            power(var, 1e-5)
            settled(dve.tensor_tensor(Z, Y, by_row(mean), ALU.subtract))
            dve.tensor_tensor(Z, Z, by_row(sm[:, 11, :]), ALU.mult).then_inc(rows_ready, 1)

            dve.wait_ge(lp_ready, TILES)
            settled(dve.tensor_copy(logits[:, :, :], lp[:, :, :]))
            full = [P, TILES, EXPERTS, EXPERTS]
            own = logits[:, :, :].rearrange("p t (i o) -> p t i o", o=1).broadcast_to(full)
            other = logits[:, :, :].rearrange("p t (o j) -> p t o j", o=1).broadcast_to(full)
            more, same = (big[:, n, :].rearrange("p (t i j) -> p t i j", t=TILES, i=EXPERTS) for n in range(2))
            settled(dve.tensor_tensor(more, other, own, ALU.is_gt), dve.tensor_tensor(same, other, own, ALU.is_equal))
            settled(dve.tensor_tensor(same, same, before[:, :, :].rearrange("p (o i) j -> p o i j", o=1).broadcast_to(full), ALU.mult))
            settled(dve.tensor_tensor(more, more, same, ALU.add))
            rank = work[:, 7, :, :]
            settled(dve.tensor_reduce(rank, more, AX.X, ALU.add))
            settled(dve.tensor_scalar(sel[:, 0, :, :], rank, 0.0, None, ALU.is_equal),
                    dve.tensor_scalar(sel[:, 1, :, :], rank, 1.0, None, ALU.is_equal))
            dve.tensor_tensor(sel[:, 2, :, :], sel[:, 0, :, :], sel[:, 1, :, :], ALU.add).then_inc(sel_ready, 1)
            top = sm[:, 8, :]
            settled(dve.tensor_reduce(top, logits[:, :, :], AX.X, ALU.max))
            settled(dve.tensor_tensor(work[:, 0, :, :], logits[:, :, :],
                                      top.rearrange("p (t o) -> p t o", o=1).broadcast_to([P, TILES, EXPERTS]), ALU.subtract))
            settled(dve.tensor_scalar(work[:, 0, :, :], work[:, 0, :, :], 1.0, None, ALU.mult))
            dve.tensor_copy(sm[:, 9, :], top).then_inc(score_ready, 1)
            dve.wait_ge(exp_done, 1)
            for k in range(2):
                settled(dve.tensor_tensor(work[:, 2 + k, :, :], work[:, 1, :, :], sel[:, k, :, :], ALU.mult))
                settled(dve.tensor_reduce(K.gates[:, k, :], work[:, 2 + k, :, :], AX.X, ALU.add))
            settled(dve.tensor_tensor(sm[:, 6, :], K.gates[:, 0, :], K.gates[:, 1, :], ALU.add))
            settled(dve.reciprocal(sm[:, 7, :], sm[:, 6, :]))
            for k in range(2):
                settled(dve.tensor_tensor(K.gates[:, k, :], K.gates[:, k, :], sm[:, 7, :], ALU.mult))
            dve.wait_ge(cp_ready, 1)
            total = work[:, 4, :, :].rearrange("p a b -> p (a b)").rearrange("p (e t) -> p e t", e=EXPERTS)
            upto = work[:, 5, :, :].rearrange("p a b -> p (a b)").rearrange("p (e t) -> p e t", e=EXPERTS)
            settled(dve.tensor_copy(total, cp[:, 1, :].rearrange("p (t e) -> p e t", t=TILES)))
            settled(dve.tensor_tensor_scan(upto.rearrange("p e t -> p (e t)"), keep_on[:, :, :].rearrange("p e t -> p (e t)"),
                                           total.rearrange("p e t -> p (e t)"), 0.0, ALU.mult, ALU.add))
            count_e = ex[:, 0, :]
            settled(dve.tensor_copy(count_e, upto[:, :, TILES - 1]))
            settled(dve.tensor_tensor(upto, upto, total, ALU.subtract))
            place = work[:, 6, :, :]
            settled(dve.tensor_tensor(place, cp[:, 0, :].rearrange("p (t e) -> p t e", t=TILES),
                                      upto.rearrange("p e t -> p t e"), ALU.add))
            for k in range(2):
                settled(dve.tensor_tensor(work[:, 2 + k, :, :], place, sel[:, k, :, :], ALU.mult))
                settled(dve.tensor_reduce(slot_f[:, k, :], work[:, 2 + k, :, :], AX.X, ALU.add))
                settled(dve.tensor_tensor(work[:, 2 + k, :, :], sel[:, k, :, :],
                                          region[:, :].rearrange("p (o e) -> p o e", o=1).broadcast_to([P, TILES, EXPERTS]), ALU.mult))
                settled(dve.tensor_reduce(block_f[:, k, :], work[:, 2 + k, :, :], AX.X, ALU.add))
            settled(dve.tensor_copy(slot_i[:, :, :], slot_f[:, :, :]))
            settled(dve.tensor_scalar(lane_i[:, :, :], slot_i[:, :, :], P - 1, None, ALU.bitwise_and))
            settled(dve.tensor_copy(slot_f[:, :, :], lane_i[:, :, :]))
            settled(dve.tensor_scalar(lane_i[:, :, :], slot_i[:, :, :], 7, None, ALU.arith_shift_right))
            settled(dve.scalar_tensor_tensor(slot_f[:, :, :], slot_f[:, :, :], float(BLOCKS), block_f[:, :, :], ALU.mult, ALU.add))
            settled(dve.tensor_copy(block_f[:, :, :], lane_i[:, :, :]))
            dve.tensor_tensor(slot[:, :, :], slot_f[:, :, :], block_f[:, :, :], ALU.add).then_inc(slot_ready, 1)

            filled = work[:, 2, :, :].rearrange("p a b -> p (a b)").rearrange("p (e t) -> p e t", e=EXPERTS)
            settled(dve.tensor_tensor(filled, count_e.rearrange("p (e o) -> p e o", o=1).broadcast_to([P, EXPERTS, TILES]),
                                      chunk[:, :].rearrange("p (o t) -> p o t", o=1).broadcast_to([P, EXPERTS, TILES]), ALU.is_gt))
            tiles_e, ends_e = ex[:, 1, :], ex[:, 2, :]
            settled(dve.tensor_reduce(tiles_e, filled, AX.X, ALU.add))
            settled(dve.tensor_tensor_scan(ends_e, ones[:, 0:EXPERTS], tiles_e, 0.0, ALU.mult, ALU.add))
            shape = [P, SLOTS, EXPERTS]

            def per_expert(v):
                return v.rearrange("p (o e) -> p o e", o=1).broadcast_to(shape)

            i_of = tiles_i[:, :].rearrange("p (i o) -> p i o", o=1).broadcast_to(shape)
            over, term = tex[:, 0], tex[:, 1]
            settled(dve.tensor_tensor(over, i_of, per_expert(ends_e), ALU.is_ge))
            settled(dve.tensor_tensor(term, over, per_expert(tiles_e), ALU.mult))
            e_of, first = tl[:, 0, :], tl[:, 1, :]
            settled(dve.tensor_reduce(e_of, over, AX.X, ALU.add), dve.tensor_reduce(first, term, AX.X, ALU.add))
            settled(dve.tensor_tensor(tl[:, 3, :], tiles_i[:, :], first, ALU.subtract))
            settled(dve.scalar_tensor_tensor(tl[:, 4, :], e_of, float(TOK // P), tl[:, 3, :], ALU.mult, ALU.add))
            settled(dve.tensor_scalar(K.block[:, :], tl[:, 4, :], float(BLOCKS - 1), None, ALU.min),
                    dve.tensor_scalar(K.expert[:, :], e_of, float(EXPERTS - 1), None, ALU.min))


X_LAG, H_LAG, O_LAG = 1, 3, 4
AHEAD = 2


def experts(nc, io, keep):
    K = keep
    with ExitStack() as ctx:
        def sb(name, shape, dt=F32):
            return ctx.enter_context(nc.sbuf_tensor(name, shape, dt))

        def ps(name, shape):
            return ctx.enter_context(nc.psum_tensor(name, shape, F32))

        def sem(name):
            return ctx.enter_context(nc.semaphore(name))

        w1 = sb("w1", [P, EXPERTS, HID])
        w2 = sb("w2", [P, EXPERTS, HID])
        wo = sb("wo_e", [P, EXPERTS, CHUNKS, D])
        b1 = sb("b1", [P, EXPERTS, HID])
        b2 = sb("b2", [P, EXPERTS, HID])
        bo = sb("bo_e", [P, EXPERTS, D])
        egb = sb("egb", [P, 2, EXPERTS])
        ones = sb("ones_e", [P, P])
        shift = sb("shift", [P, P])
        ids = [sb(f"ids{r}", [P, 2], U32) for r in range(FROUND)]
        rows = [sb(f"rows{r}", [P, D]) for r in range(4)]
        zt = [sb(f"zt{r}", [P, P]) for r in range(2)]
        gate_in = [sb(f"gate_in{r}", [P, HID]) for r in range(2)]
        silu = [sb(f"silu{r}", [P, HID]) for r in range(2)]
        up = [sb(f"up{r}", [P, HID]) for r in range(2)]
        hid = [sb(f"hid{r}", [P, HID]) for r in range(2)]
        ht = [sb(f"ht{r}", [P, HID]) for r in range(2)]
        o_f = [sb(f"o_f{r}", [P, D]) for r in range(2)]
        o = [sb(f"o{r}", [P, D]) for r in range(4)]

        x1_ps = [ps(f"x1_ps{r}", [P, HID]) for r in range(2)]
        x2_ps = [ps(f"x2_ps{r}", [P, HID]) for r in range(2)]
        ht_ps = ps("ht_ps", [P, HID])
        zt_ps = ps("zt_ps", [P, P])
        o_ps = [ps(f"o_ps{r}", [P, D]) for r in range(2)]

        weights_in = sem("weights_in")
        constants = sem("constants")
        shift_ready = sem("shift_ready")
        bias_ready = sem("bias_ready")
        folded = sem("folded")
        rows_in = [sem(f"rows_in{r}") for r in range(4)]
        ids_in = [sem(f"ids_in{r}") for r in range(FROUND)]
        zt_done = sem("zt_done")
        zt_ready = sem("zt_ready")
        x2_ready = sem("x2_ready")
        x1_ready = sem("x1_ready")
        gate_sum = sem("gate_sum")
        gate_ready = sem("gate_ready")
        silu_ready = sem("silu_ready")
        up_ready = sem("up_ready")
        mul_ready = sem("mul_ready")
        hid_ready = sem("hid_ready")
        ht_done = sem("ht_done")
        ht_ready = sem("ht_ready")
        o_done = sem("o_done")
        o_sum = sem("o_sum")
        o_ready = sem("o_ready")
        sent = [sem(f"o_sent{r}") for r in range(4)]

        block = ctx.enter_context(nc.Block())

        def tiles(eng, body, lag):
            for J in range(FROUND):
                body(J, J)
            with eng.Fori(1, SLOTS // FROUND) as it:
                for q in range(FROUND):
                    body(it * FROUND + q, q)
            for q in range(lag):
                body(SLOTS + q, q)

        def present(J, lag):
            return not isinstance(J, int) or 0 <= J - lag < SLOTS

        def late(J, n):
            return not isinstance(J, int) or J >= n

        def filled(J, q, lag, ring, by=16):
            if isinstance(J, int):
                return by * ((J - lag) // ring + 1)
            return (J - q) * (by // ring) + by * ((q - lag) // ring + 1)

        def expert_of(eng, J, lag):
            at = bass.ds(J - lag, 1) if not isinstance(J, int) else slice(J - lag, J - lag + 1)
            return eng.value_load(K.expert[0:1, at], min_val=0, max_val=EXPERTS - 1)

        @block.sync
        def _(sp):
            sp.dma_start(egb[:, 0, :], io["eg"].rearrange("e d -> d e"), allow_slow_non_contiguous=True).then_inc(weights_in, 16)
            sp.dma_start(egb[:, 1, :], io["eb"].rearrange("e d -> d e"), allow_slow_non_contiguous=True).then_inc(weights_in, 16)
            sp.dma_start(w1[:, :, :], io["W1"].rearrange("e d h -> d e h")).then_inc(weights_in, 16)
            sp.dma_start(w2[:, :, :], io["W2"].rearrange("e d h -> d e h")).then_inc(weights_in, 16)
            for dst, name in ((b1, "b1"), (b2, "b2"), (bo, "ebo")):
                sp.dma_start(dst[:, :, :], io[name].rearrange("(o e) h -> o e h", o=1).broadcast_to(dst.shape)).then_inc(weights_in, 16)
            sp.dma_start(wo[:, :, :, :], io["eWo"].rearrange("e (c p) d -> p e c d", p=P)).then_inc(weights_in, 16)

            def lookup(J, q):
                at = bass.ds(J, 1) if not isinstance(J, int) else slice(J, J + 1)
                b = sp.value_load(K.block[0:1, at], min_val=0, max_val=BLOCKS - 1)
                if late(J, FROUND):
                    sp.wait_ge(sent[q % 4], filled(J, q, FROUND, 4))
                src = K.dispatch.rearrange("(p b) k -> p b k", p=P)[:, bass.ds(b, 1), :]
                sp.dma_start(ids[q][:, :], src.rearrange("p o k -> p (o k)")).then_inc(ids_in[q], 16)

            tiles(sp, lookup, 0)

        @block.gpsimd
        def _(pool):
            pool.memset(ones[:, :], 1.0).then_inc(constants, 1)

            def step(J, q):
                if present(J, 0):
                    r = q % 4
                    pool.wait_ge(ids_in[q], filled(J, q, 0, FROUND))
                    if late(J, 4):
                        pool.wait_ge(zt_done, J - 3)
                    pool.nop(nofuse=True)
                    pool.indirect_dma_start(rows[r][:, :], None, K.z_rows[:, :],
                                            bass.IndirectOffsetOnAxis(ids[q][:, 0:1], 0)).then_inc(rows_in[r], 16)
                lag = AHEAD + O_LAG
                if present(J, lag):
                    f = (q - lag) % FROUND
                    pool.wait_ge(o_ready, J - lag + 1)
                    pool.nop(nofuse=True)
                    pool.indirect_dma_start(K.results[:, :], bass.IndirectOffsetOnAxis(ids[f][:, 1:2], 0),
                                            o[f % 4][:, :], None).then_inc(sent[f % 4], 16)

            tiles(pool, step, AHEAD + O_LAG)
            for r in range(4):
                pool.wait_ge(sent[r], 16 * SLOTS // 4)

        @block.scalar
        def _(act):
            def step(J, q):
                if present(J, H_LAG):
                    f = (q - H_LAG) % FROUND
                    act.wait_ge(ht_done, J - H_LAG + 1)
                    if late(J, H_LAG + 2):
                        act.wait_ge(o_done, J - H_LAG - 1)
                    act.activation(ht[f % 2][:, :], ht_ps[:, :], ACT.Copy).then_inc(ht_ready, 1)
                if present(J, 0):
                    act.wait_ge(zt_done, J + 1)
                    if late(J, 2):
                        act.wait_ge(x1_ready, J - 1)
                    act.activation(zt[q % 2][:, :], zt_ps[:, :], ACT.Copy).then_inc(zt_ready, 1)
                if present(J, X_LAG):
                    f = (q - X_LAG) % FROUND
                    act.wait_ge(gate_ready, J - X_LAG + 1)
                    if late(J, X_LAG + 2):
                        act.wait_ge(mul_ready, J - X_LAG - 1)
                    act.activation(silu[f % 2][:, :], gate_in[f % 2][:, :], ACT.Silu).then_inc(silu_ready, 1)

            tiles(act, step, H_LAG)

        @block.vector
        def _(dve):
            dve.wait_ge(weights_in, 8 * 16)
            dve.wait_ge(constants, 1)

            def fold(e):
                at = bass.ds(e, 1)
                if late(e, 1):
                    dve.wait_ge(bias_ready, 2 * e)
                dve.tensor_scalar(shift[:, :], ones[:, :], egb[:, 1, at], None, ALU.mult).then_inc(shift_ready, 1)
                for n, (w, b, acc) in enumerate(((w1, b1, x1_ps[0]), (w2, b2, x2_ps[0]))):
                    dve.wait_ge(bias_ready, 2 * e + n + 1)
                    be, we = (v[:, at, :].rearrange("p o h -> p (o h)") for v in (b, w))
                    dve.tensor_tensor(be, be, acc[:, :], ALU.add).then_inc(folded, 1)
                    dve.tensor_scalar(we, we, egb[:, 0, at], None, ALU.mult).then_inc(folded, 1)

            fold(0)
            with dve.Fori(1, EXPERTS) as e:
                fold(e)
            dve.wait_ge(folded, 4 * EXPERTS)

            def step(J, q):
                if present(J, X_LAG):
                    f = (q - X_LAG) % FROUND
                    n = J - X_LAG
                    e = expert_of(dve, J, X_LAG)
                    bias = [v[:, bass.ds(e, 1), :].rearrange("p o h -> p (o h)") for v in (b1, b2)]
                    dve.wait_ge(x2_ready, n + 1)
                    if late(J, X_LAG + 2):
                        dve.wait_ge(silu_ready, n - 1)
                    dve.tensor_tensor(gate_in[f % 2][:, :], x2_ps[f % 2][:, :], bias[1], ALU.add).then_inc(gate_sum, 1)
                    dve.wait_ge(gate_sum, n + 1)
                    dve.tensor_scalar(gate_in[f % 2][:, :], gate_in[f % 2][:, :], -20.0, 20.0, ALU.max, ALU.min).then_inc(gate_ready, 1)
                if present(J, O_LAG):
                    f = (q - O_LAG) % FROUND
                    n = J - O_LAG
                    e = expert_of(dve, J, O_LAG)
                    dve.wait_ge(o_done, n + 1)
                    if late(J, O_LAG + 2):
                        dve.wait_ge(o_ready, n - 1)
                    dve.tensor_tensor(o_f[f % 2][:, :], o_ps[f % 2][:, :], bo[:, bass.ds(e, 1), :].rearrange("p o d -> p (o d)"),
                                      ALU.add).then_inc(o_sum, 1)
                    dve.wait_ge(o_sum, n + 1)
                    if late(J, O_LAG + 4):
                        dve.wait_ge(sent[f % 4], filled(J, q, O_LAG + 4, 4))
                    dve.tensor_scalar(o[f % 4][:, :], o_f[f % 2][:, :], -1e4, 1e4, ALU.max, ALU.min).then_inc(o_ready, 1)
                if present(J, X_LAG):
                    f = (q - X_LAG) % FROUND
                    n = J - X_LAG
                    dve.wait_ge(x1_ready, n + 1)
                    if late(J, X_LAG + 2):
                        dve.wait_ge(mul_ready, n - 1)
                    dve.tensor_tensor(up[f % 2][:, :], x1_ps[f % 2][:, :], bias[0], ALU.add).then_inc(up_ready, 1)
                    dve.wait_ge(up_ready, n + 1)
                    dve.wait_ge(silu_ready, n + 1)
                    if late(J, X_LAG + 2):
                        dve.wait_ge(ht_done, n - 1)
                    dve.tensor_tensor(hid[f % 2][:, :], up[f % 2][:, :], silu[f % 2][:, :], ALU.mult).then_inc(mul_ready, 1)
                    dve.wait_ge(mul_ready, n + 1)
                    dve.tensor_scalar(hid[f % 2][:, :], hid[f % 2][:, :], -1e4, 1e4, ALU.max, ALU.min).then_inc(hid_ready, 1)

            tiles(dve, step, O_LAG)

        @block.tensor
        def _(pe):
            pe.wait_ge(weights_in, 8 * 16)

            def fold(e):
                pe.wait_ge(shift_ready, e + 1)
                for n, (w, acc) in enumerate(((w1, x1_ps[0]), (w2, x2_ps[0]))):
                    if late(e, 1):
                        pe.wait_ge(folded, 4 * e + 2 * n - 3)
                    pe.matmul(acc[:, :], shift[:, :], w[:, bass.ds(e, 1), :].rearrange("p o h -> p (o h)"),
                              start=True, stop=True).then_inc(bias_ready, 1)

            fold(0)
            with pe.Fori(1, EXPERTS) as e:
                fold(e)
            pe.wait_ge(folded, 4 * EXPERTS)

            def step(J, q):
                if present(J, H_LAG):
                    f = (q - H_LAG) % FROUND
                    n = J - H_LAG
                    pe.wait_ge(hid_ready, n + 1)
                    if late(J, H_LAG + 1):
                        pe.wait_ge(ht_ready, n)
                    for c in range(CHUNKS):
                        mm = pe.transpose(ht_ps[:, c * P:(c + 1) * P], hid[f % 2][:, c * P:(c + 1) * P], K.ident[:, :])
                    mm.then_inc(ht_done, 1)
                if present(J, X_LAG):
                    f = (q - X_LAG) % FROUND
                    n = J - X_LAG
                    e = expert_of(pe, J, X_LAG)
                    pe.wait_ge(zt_ready, n + 1)
                    if late(J, X_LAG + 2):
                        pe.wait_ge(gate_sum, n - 1)
                        pe.wait_ge(up_ready, n - 1)
                    pe.matmul(x2_ps[f % 2][:, :], zt[f % 2][:, :], w2[:, bass.ds(e, 1), :].rearrange("p o h -> p (o h)"),
                              start=True, stop=True).then_inc(x2_ready, 1)
                    pe.matmul(x1_ps[f % 2][:, :], zt[f % 2][:, :], w1[:, bass.ds(e, 1), :].rearrange("p o h -> p (o h)"),
                              start=True, stop=True).then_inc(x1_ready, 1)
                if present(J, 0):
                    pe.wait_ge(rows_in[q % 4], filled(J, q, 0, 4))
                    if late(J, 1):
                        pe.wait_ge(zt_ready, J)
                    pe.transpose(zt_ps[:, :], rows[q % 4][:, :], K.ident[:, :]).then_inc(zt_done, 1)
                if present(J, H_LAG):
                    f = (q - H_LAG) % FROUND
                    n = J - H_LAG
                    e = expert_of(pe, J, H_LAG)
                    pe.wait_ge(ht_ready, n + 1)
                    if late(J, H_LAG + 2):
                        pe.wait_ge(o_sum, n - 1)
                    for c in range(CHUNKS):
                        mm = pe.matmul(o_ps[f % 2][:, :], ht[f % 2][:, c * P:(c + 1) * P],
                                       wo[:, bass.ds(e, 1), c, :].rearrange("p o d -> p (o d)"),
                                       start=(c == 0), stop=(c == CHUNKS - 1))
                    mm.then_inc(o_done, 1)

            tiles(pe, step, H_LAG)


def combine(nc, io, keep, out):
    K = keep
    PART = 4
    N = TILES // PART
    with ExitStack() as ctx:
        def sb(name, shape, dt=F32):
            return ctx.enter_context(nc.sbuf_tensor(name, shape, dt))

        def sem(name):
            return ctx.enter_context(nc.semaphore(name))

        f = [sb(f"f{n}", [P, N, 2, D]) for n in range(PART)]
        bn = sb("bn3", [P, TILES, 6])
        sm = sb("sm3", [P, 5, TILES])
        mv = sb("mv3", [P, 2, TILES])
        r = sb("r3", [P, TILES])
        half = sb("half3", [P, TILES])
        f_in = [sem(f"f_in{n}") for n in range(PART)]
        chain = sem("chain3")
        half_made = sem("half_made")
        var_made = sem("var_made")
        r_made = sem("r_made")
        out_made = sem("out_made")
        out_sent = sem("out_sent")
        block = ctx.enter_context(nc.Block())

        @block.sync
        def _(sp):
            src = K.results[0:DUMP, :].rearrange("(t p k) d -> p t (k d)", p=P, k=2)
            for n in range(PART):
                sp.dma_start(f[n][:, :, :, :].rearrange("p t k d -> p t (k d)"), src[:, n * N:(n + 1) * N, :]).then_inc(f_in[n], 16)
            dst = out.rearrange("b (t p) d -> p (b t) d", p=P)
            for n in range(PART):
                sp.wait_ge(out_made, n + 1)
                sp.dma_start(dst[:, n * N:(n + 1) * N, :], K.x_all[:, n * N:(n + 1) * N, :]).then_inc(out_sent, 16)
            sp.wait_ge(out_sent, 16 * PART)

        @block.gpsimd
        def _(pool):
            pool.memset(half[:, :], -0.5).then_inc(half_made, 1)
            pool.wait_ge(half_made, 1)
            for n in range(PART):
                at = slice(n * N, (n + 1) * N)
                pool.wait_ge(var_made, n + 1)
                pool.tensor_tensor(r[:, at], mv[:, 1, at], half[:, at], ALU.pow).then_inc(r_made, 1)

        @block.vector
        def _(dve):
            count = [0]

            def settled(*made):
                for ins in made:
                    ins.then_inc(chain, 1)
                    count[0] += 1
                dve.wait_ge(chain, count[0])

            def by_row(v):
                return v.rearrange("p (t o) -> p t o", o=1).broadcast_to([P, N, D])

            def add_up(n):
                at = slice(n * N, (n + 1) * N)
                dve.wait_ge(f_in[n], 16)
                a, b = f[n][:, :, 0, :], f[n][:, :, 1, :]
                settled(dve.tensor_tensor(a, a, by_row(K.gates[:, 0, at]), ALU.mult),
                        dve.tensor_tensor(b, b, by_row(K.gates[:, 1, at]), ALU.mult))
                settled(dve.tensor_tensor(a, a, b, ALU.add))
                settled(*[dve.bn_stats(bn[:, n * N + t, :], f[n][:, t, 0, :]) for t in range(N)])
                settled(dve.tensor_tensor(sm[:, 0, at], bn[:, at, 1], bn[:, at, 4], ALU.add),
                        dve.tensor_tensor(sm[:, 1, at], bn[:, at, 1], bn[:, at, 4], ALU.subtract),
                        dve.tensor_tensor(sm[:, 2, at], bn[:, at, 2], bn[:, at, 5], ALU.add))
                settled(dve.tensor_scalar(mv[:, 0, at], sm[:, 0, at], 0.5, None, ALU.mult),
                        dve.scalar_tensor_tensor(sm[:, 3, at], sm[:, 1, at], 0.25, sm[:, 1, at], ALU.mult, ALU.mult),
                        dve.tensor_scalar(sm[:, 4, at], sm[:, 2, at], 1.0 / D, 1e-5, ALU.mult, ALU.add))
                dve.tensor_tensor(mv[:, 1, at], sm[:, 3, at], sm[:, 4, at], ALU.add).then_inc(var_made, 1)

            def finish(n):
                at = slice(n * N, (n + 1) * N)
                a = f[n][:, :, 0, :]
                settled(dve.tensor_tensor(a, a, by_row(mv[:, 0, at]), ALU.subtract))
                dve.wait_ge(r_made, n + 1)
                settled(dve.tensor_tensor(a, a, by_row(r[:, at]), ALU.mult))
                dve.tensor_tensor(K.x_all[:, at, :], K.x_all[:, at, :], a, ALU.add).then_inc(out_made, 1)

            for n in range(PART):
                add_up(n)
                if n:
                    finish(n - 1)
            finish(PART - 1)


def program(nc, io, out):
    with ExitStack() as ctx:
        class keep:
            x_all = ctx.enter_context(nc.sbuf_tensor("x_all", [P, TILES, D], F32))
            ident = ctx.enter_context(nc.sbuf_tensor("ident", [P, P], F32))
            gates = ctx.enter_context(nc.sbuf_tensor("gates", [P, 2, TILES], F32))
            block = ctx.enter_context(nc.sbuf_tensor("block", [P, SLOTS], I32))
            expert = ctx.enter_context(nc.sbuf_tensor("expert", [P, SLOTS], I32))
            numden = nc.dram_tensor("numden", [COLS, 2 * HD, TOK], F32).ap()
            z_rows = nc.dram_tensor("z_rows", [TOK + 1, D], F32).ap()
            dispatch = nc.dram_tensor("dispatch", [P * BLOCKS, 2], U32).ap()
            results = nc.dram_tensor("results", [DUMP + P * BLOCKS, D], F32).ap()

        with nc.sbuf_tensor("u_all", [P, TILES, D], F32) as keep.u_all:
            attention(nc, io, keep)
            routing(nc, io, keep)
        experts(nc, io, keep)
        combine(nc, io, keep, out)


_INS = {"x": "L0_attn_x", "Wq": "L0_attn_Wq", "bq": "L0_attn_bq", "Wk": "L0_attn_Wk", "bk": "L0_attn_bk",
        "Wv": "L0_attn_Wv", "bv": "L0_attn_bv", "Wo": "L0_attn_Wo", "bo": "L0_attn_bo", "gamma": "L0_attn_gamma",
        "beta": "L0_attn_beta", "ln_g": "L0_ffn_ln_g", "ln_b": "L0_ffn_ln_b", "router_w": "L0_ffn_router_w",
        "eg": "L0_ffn_eg", "eb": "L0_ffn_eb", "W1": "L0_ffn_W1", "b1": "L0_ffn_b1", "W2": "L0_ffn_W2",
        "b2": "L0_ffn_b2", "eWo": "L0_ffn_Wo", "ebo": "L0_ffn_bo"}


def kernel(**inputs):
    import numpy as np
    import concourse.bacc as bacc
    from concourse.bass_utils import run_bass_kernel_spmd

    nc = bacc.Bacc("TRN2", target_bir_lowering=False, num_devices=1)
    arrays, io = {}, {}
    for short, name in _INS.items():
        arrays[name] = np.ascontiguousarray(inputs[name])
        io[short] = nc.dram_tensor(name, arrays[name].shape, F32, kind="ExternalInput").ap()
    out = nc.dram_tensor("out", [BATCH, SEQ, D], F32, kind="ExternalOutput").ap()
    program(nc, io, out)
    result = run_bass_kernel_spmd(nc, [arrays], core_ids=[0])
    return result.results[0]["out"]
```

```python
from contextlib import ExitStack

import concourse.bass as bass
from concourse import mybir

F32 = mybir.dt.float32
F32R = mybir.dt.float32r
I32 = mybir.dt.int32
U32 = mybir.dt.uint32
ALU = mybir.AluOpType
ACT = mybir.ActivationFunctionType
AX = mybir.AxisListType

P = 128
BATCH, SEQ, D = 16, 256, 128
TOK = BATCH * SEQ
TILES = TOK // P
HEADS, HD = 16, 8
COLS = D // HD
RPH = SEQ // HEADS
SCALE = HD ** -0.5

STEP = 512
STEPS = TOK // STEP
TPS = STEP // P
UNITS = TOK // P
RING = 4
GROUPS = 2 * UNITS
ROUND = 2 * RING
PARTS = 4 * HD
ZERO_TO = 96
LAG_T, LAG_PV, LAG_OUT = 4, 5, 6
MAX_ROWS = 2


def attention(nc, io, keep):
    x_all, u_all, ident, numden = keep.x_all, keep.u_all, keep.ident, keep.numden
    with ExitStack() as ctx:
        def sb(name, shape, dt=F32):
            return ctx.enter_context(nc.sbuf_tensor(name, shape, dt))

        def ps(name, shape):
            return ctx.enter_context(nc.psum_tensor(name, shape, F32))

        def sem(name):
            return ctx.enter_context(nc.semaphore(name))

        def dram(name, shape, dt=F32):
            return nc.dram_tensor(name, shape, dt).ap()

        q_parts = dram("q_parts", [P, 4, TOK])
        k_parts = dram("k_parts", [P, 4, TOK])
        v_rows = dram("v_rows", [P, 4, TOK // 4])

        w_qkv = sb("w_qkv", [P, 3, D])
        b_qkv = sb("b_qkv", [P, 3])
        bo_all = sb("bo_all", [P, D])
        bn = sb("bn", [P, TILES, 6])
        mean = sb("mean", [P, TILES])
        var = sb("var", [P, TILES])
        rstd = sb("rstd", [P, TILES])
        tmp = sb("tmp", [P, 4, TILES])
        dev = sb("dev", [P, TILES])
        u_step = [sb(f"u_step{i}", [P, TPS, D]) for i in range(2)]
        ut = [sb(f"ut{i}", [P, STEP]) for i in range(2)]
        parts_out = [[sb(f"parts_out{i}{k}", [P, 2, STEP], F32R) for k in range(2)] for i in range(2)]
        v_out = [sb(f"v_out{i}", [P, STEP]) for i in range(2)]

        qt = [sb(f"qt{r}", [P, SEQ, 8], F32R) for r in range(RING)]
        kt = [sb(f"kt{r}", [P, SEQ, 8], F32R) for r in range(RING)]
        vs = [sb(f"vs{r}", [P, SEQ, 2]) for r in range(RING)]
        vt = [sb(f"vt{r}", [P, 2, 4, 32]) for r in range(2)]
        mx = [sb(f"mx{r}", [P, 2, 8]) for r in range(2)]
        mhl = [sb(f"mhl{r}", [P, MAX_ROWS, 2, 8], F32R) for r in range(2)]
        pt = [sb(f"pt{r}", [P, 4 * SEQ]) for r in range(4)]
        os_ = [sb(f"os{r}", [P, COLS, 64]) for r in range(2)]

        s_ps = [ps(f"s_ps{i}", [P, 512]) for i in range(2)]
        st_ps = [ps(f"st_ps{i}", [P, 2, 512]) for i in range(2)]
        pv_ps = ps("pv_ps", [P, 512])
        m_ps = ps("m_ps", [P, 512])
        ut_ps = s_ps
        qkv_ps = [[st_ps[0][:, 0, :], st_ps[0][:, 1, :], st_ps[1][:, 0, :]], [st_ps[1][:, 1, :], pv_ps[:, :], m_ps[:, :]]]

        consts_in = sem("consts_in")
        x_in = [sem(f"x_in{i}") for i in range(2)]
        ident_ready = sem("ident_ready")
        dev_ready = sem("x_dev_ready")
        stats_ready = sem("stats_ready")
        chain = sem("chain")
        var_ready = sem("var_ready")
        rstd_ready = sem("rstd_ready")
        norm_ready = sem("norm_ready")
        ubo_ready = sem("ubo_ready")
        tp_ready = sem("tp_ready")
        ut_ready = sem("ut_ready")
        qkv_ready = sem("qkv_ready")
        hi_ready = sem("hi_ready")
        lo_ready = sem("lo_ready")
        v_ready = sem("v_ready")
        stored = [sem(f"stored{i}") for i in range(2)]
        q_cleared = sem("q_cleared")
        k_cleared = sem("k_cleared")
        v_cleared = sem("v_cleared")
        unit_in = [sem(f"unit_in{r}") for r in range(RING)]
        s_ready = sem("s_ready")
        max_ready = sem("max_ready")
        mh_ready = sem("mh_ready")
        ml_ready = sem("ml_ready")
        m_in = [sem(f"m_in{r}") for r in range(4)]
        st_ready = sem("st_ready")
        exp_ready = sem("exp_ready")
        vt_ready = sem("vt_ready")
        vp_ready = sem("vp_ready")
        pv_ready = sem("pv_ready")
        os_ready = sem("os_ready")
        numden_out = [sem(f"numden_out{i}") for i in range(2)]

        block = ctx.enter_context(nc.Block())

        def steps(eng, body):
            with eng.Fori(0, STEPS // 2) as it:
                for p in range(2):
                    body(it * 2 + p, p)

        def groups(eng, body, lag, peeled=1):
            for G in range(peeled * ROUND):
                body(G // ROUND, G % ROUND)
            with eng.Fori(peeled, GROUPS // ROUND) as it:
                for g in range(ROUND):
                    body(it, g)
            for G in range(GROUPS, GROUPS + lag):
                body(G // ROUND, G % ROUND)

        def present(G, lag, total=GROUPS):
            return not isinstance(G, int) or 0 <= G - lag < total

        def unit_of(R, g, lag):
            return R * RING + (g - lag) // 2

        def pair_of(R, g, lag):
            return R * (RING // 2) + (g - lag) // 4

        def m_in_count(R, g, lag):
            return R * (32 * RING // 2) + 32 * ((g - lag) // 4 + 1)

        def s_at_least(s, n):
            return not isinstance(s, int) or s >= n

        def stores_before(s, p):
            return (s - p) * 40

        @block.sync
        def _(sp):
            xt = io["x"].rearrange("b (t p) d -> p (b t) d", p=P)
            for i in range(2):
                half = slice(i * TILES // 2, (i + 1) * TILES // 2)
                sp.dma_start(x_all[:, half, :], xt[:, half, :]).then_inc(x_in[i], 16)
            for n, name in enumerate(("Wq", "Wk", "Wv")):
                sp.dma_start(w_qkv[:, n, :], io[name]).then_inc(consts_in, 16)
            for n, name in enumerate(("bq", "bk", "bv")):
                sp.dma_start(b_qkv[:, n:n + 1], io[name].rearrange("(p o) -> p o", o=1)).then_inc(consts_in, 16)
            sp.dma_start(bo_all[:, :], io["bo"].rearrange("(o d) -> o d", o=1).broadcast_to([P, D])).then_inc(consts_in, 16)

            def store(s, p):
                at = bass.ds(s * STEP, STEP)
                for k, parts in enumerate((q_parts, k_parts)):
                    sp.wait_ge(lo_ready, 2 * s + k + 1)
                    src = parts_out[p][k][:, :, :].bitcast(F32)
                    sp.dma_start(parts[:, 0:2, at], src).then_inc(stored[p], 16)
                    sp.dma_start(parts[:, 2:4, at], src[:, ::-1, :] if k else src).then_inc(stored[p], 16)
                sp.wait_ge(v_ready, 4 * s + 4)
                sp.dma_start(v_rows[:, :, bass.ds(s * (STEP // 4), STEP // 4)],
                             v_out[p][:, :].rearrange("p (j t) -> p j t", j=4)).then_inc(stored[p], 16)

            def load(U, r, reuse):
                if reuse:
                    sp.wait_ge(st_ready, 4 * U - 4 * RING + 4)
                    sp.wait_ge(q_cleared, RING)
                    sp.wait_ge(vt_ready, 2 * U - 2 * RING + 2)
                at = bass.ds(U * P, P)
                for dst, src in ((qt[r], q_parts), (kt[r], k_parts)):
                    sp.dma_start(dst[0:PARTS, :, :].bitcast(F32).rearrange("d (c r) h -> d c (r h)", c=COLS),
                                 src[:, :, bass.ds(U * P, P)].rearrange("(c d) a t -> (d a) c t", d=HD)).then_inc(unit_in[r], 16)
                sp.dma_start(vs[r][0:PARTS, :, :].rearrange("d (c r) i -> d c (r i)", c=COLS),
                             v_rows[:, :, bass.ds(U * 32, 32)].rearrange("(c d) j t -> (d j) c t", d=HD)).then_inc(unit_in[r], 16)

            with sp.Fori(0, STEPS // 2 - 1) as it:
                for p in range(2):
                    store(it * 2 + p, p)
            sp.wait_ge(stored[0], 16 * 5)
            sp.wait_ge(q_cleared, RING)
            sp.wait_ge(k_cleared, 2 * RING)
            for r in range(2):
                load(r, r, False)
            store(STEPS - 2, 0)
            for r in range(2, RING):
                load(r, r, False)
            store(STEPS - 1, 1)

            def numden_store(K, p):
                sp.wait_ge(os_ready, 4 * K + 4)
                for j in range(4):
                    dst = numden[:, :, bass.ds(K * 2 * P + 64 * j, 64)].rearrange("c d t -> d c t")
                    sp.dma_start(dst, os_[p][32 * j:32 * j + 2 * HD, :, :]).then_inc(numden_out[p], 16)

            def group(R, g):
                G = R * ROUND + g
                if g % 4 == 0 and present(G, 12):
                    numden_store(pair_of(R, g, 12), (g - 12) // 4 % 2)
                if g % 2 == 0 and present(G, 0) and (not isinstance(G, int) or G >= ROUND):
                    if isinstance(G, int) and G == ROUND:
                        for p in range(2):
                            sp.wait_ge(stored[p], 16 * 5 * STEPS // 2)
                    load(unit_of(R, g, 0), g // 2, True)
                if g % 2 == 0 and present(G, 4):
                    sp.wait_ge(ml_ready, unit_of(R, g, 4) + 1)
                    r = (g - 4) % ROUND // 2
                    for o in range(MAX_ROWS):
                        dst = qt[r][ZERO_TO + o:ZERO_TO + o + 1, :, :].bitcast(F32)
                        sp.dma_start(dst.rearrange("o (p a) h -> o p (a h)", a=2),
                                     mhl[r % 2][:, o].bitcast(F32).rearrange("p a h -> p (a h)")).then_inc(m_in[r % 2], 16)

            groups(sp, group, 9, 2)
            for p in range(2):
                sp.wait_ge(numden_out[p], 16 * 4 * UNITS // 4)

        @block.gpsimd
        def _(pool):
            pool.memset(ident[:, :], 0.0).then_inc(ident_ready, 1)
            pool.wait_ge(ident_ready, 1)
            pool.affine_select(out=ident[:, :], in_=ident[:, :], compare_op=ALU.not_equal, fill=1.0, base=0,
                               pattern=[[-1, P]], channel_multiplier=1).then_inc(ident_ready, 1)
            for r in range(RING):
                pool.memset(qt[r][:, :, :].bitcast(F32), 0.0).then_inc(q_cleared, 1)
            for r in range(2):
                pool.memset(vt[r][:, :, :, :], 1.0).then_inc(v_cleared, 1)
            for r in range(RING):
                pool.memset(kt[r][:, :, :].bitcast(F32), 0.0).then_inc(k_cleared, 1)
            pool.wait_ge(v_cleared, 2)
            pool.wait_ge(q_cleared, RING)
            pool.wait_ge(k_cleared, RING)
            for r in range(RING):
                pool.memset(kt[r][ZERO_TO:P, :, :].bitcast(F32), 1.0).then_inc(k_cleared, 1)
            pool.wait_ge(k_cleared, 2 * RING)
            pool.wait_ge(consts_in, 7 * 16)

            def residual(s, p):
                for t in range(TPS):
                    pool.wait_ge(norm_ready, TPS * s + t + 1)
                    pool.tensor_tensor(u_all[:, bass.ds(TPS * s + t, 1), :].rearrange("p o d -> p (o d)"),
                                       u_step[p][:, t, :], bo_all[:, :], ALU.add).then_inc(ubo_ready, 1)

            steps(pool, residual)

        def numden_before(R, g):
            return R * 64 + 64 * ((g - LAG_OUT) // 8)

        @block.scalar
        def _(act):
            act.wait_ge(var_ready, 1)
            act.activation(dev[:, :], var[:, :], ACT.Sqrt).then_inc(dev_ready, 1)
            act.wait_ge(consts_in, 7 * 16)

            def turned(s, p):
                act.wait_ge(tp_ready, s + 1)
                if s_at_least(s, 2):
                    act.wait_ge(qkv_ready, 3 * s - 3)
                act.activation(ut[p][:, :].rearrange("p (t r h) -> p t h r", t=TPS, h=8),
                               ut_ps[p][:, :].rearrange("p (t h r) -> p t h r", t=TPS, h=8), ACT.Copy).then_inc(ut_ready, 1)

            def outputs(s, p):
                if s_at_least(s, 2):
                    act.wait_ge(stored[p], stores_before(s, p))
                for k in range(2):
                    act.wait_ge(qkv_ready, 3 * s + k + 1)
                    act.activation(parts_out[p][k][:, 0, :], qkv_ps[p][k], ACT.Identity, bias=b_qkv[:, k:k + 1])\
                        .then_inc(hi_ready, 1)
                act.wait_ge(qkv_ready, 3 * s + 3)
                for j in range(4):
                    act.activation(v_out[p][:, :].rearrange("p (j t r i) -> p j t r i", t=TPS, j=4, i=2)[:, j],
                                   qkv_ps[p][2].rearrange("p (t r i j) -> p j t r i", t=TPS, j=4, i=2)[:, j],
                                   ACT.Identity, bias=b_qkv[:, 2:3]).then_inc(v_ready, 1)

            turned(0, 0)
            turned(1, 1)
            outputs(0, 0)
            turned(2, 0)
            outputs(1, 1)
            turned(3, 1)
            outputs(2, 0)
            with act.Fori(2, STEPS // 2) as it:
                turned(it * 2, 0)
                outputs(it * 2 - 1, 1)
                turned(it * 2 + 1, 1)
                outputs(it * 2, 0)
            outputs(STEPS - 1, 1)

            def group(R, g):
                G = R * ROUND + g
                if present(G, LAG_OUT):
                    f = (g - LAG_OUT) % ROUND
                    act.wait_ge(pv_ready, G - LAG_OUT + 1)
                    if f % 4 == 0 and (not isinstance(G, int) or G - LAG_OUT >= 8):
                        act.wait_ge(numden_out[f // 4], numden_before(R, g))
                    at = (f % 4) * RPH
                    act.activation(os_[f // 4][:, :, at:at + RPH],
                                   pv_ps[:, 0:SEQ].rearrange("p (c r) -> p c r", r=RPH), ACT.Copy).then_inc(os_ready, 1)
                if present(G, LAG_T):
                    f = (g - LAG_T) % ROUND
                    for pair in range(2):
                        act.wait_ge(st_ready, 2 * (G - LAG_T) + pair + 1)
                        if not isinstance(G, int) or G - LAG_T >= 2:
                            act.wait_ge(pv_ready, G - LAG_T - 1)
                        if pair == 1:
                            act.wait_ge(vt_ready, G - LAG_T + 1)
                            act.activation(vt[f % 2][:, :, :, 0:HD], m_ps[:, 0:64].rearrange("p (a d j) -> p a j d", a=2, j=4),
                                           ACT.Copy).then_inc(vp_ready, 1)
                        act.activation(pt[(2 * f + pair) % 4][:, :], st_ps[pair][:, :, :].rearrange("p a b -> p (a b)"),
                                       ACT.Exp, scale=SCALE).then_inc(exp_ready, 1)

            act.wait_ge(v_cleared, 2)
            groups(act, group, LAG_OUT)

        @block.vector
        def _(dve):
            for i in range(2):
                dve.wait_ge(x_in[i], 16)
                with dve.Fori(i * TILES // 16, (i + 1) * TILES // 16) as it:
                    for t in range(8):
                        dve.bn_stats(bn[:, bass.ds(it * 8 + t, 1), :].rearrange("p o s -> p (o s)"),
                                     x_all[:, bass.ds(it * 8 + t, 1), :].rearrange("p o d -> p (o d)")).then_inc(stats_ready, 1)
            dve.wait_ge(stats_ready, TILES)
            dve.tensor_tensor(tmp[:, 0, :], bn[:, :, 1], bn[:, :, 4], ALU.add).then_inc(chain, 1)
            dve.tensor_tensor(tmp[:, 1, :], bn[:, :, 1], bn[:, :, 4], ALU.subtract).then_inc(chain, 1)
            dve.tensor_tensor(tmp[:, 2, :], bn[:, :, 2], bn[:, :, 5], ALU.add).then_inc(chain, 1)
            dve.wait_ge(chain, 3)
            dve.tensor_scalar(mean[:, :], tmp[:, 0, :], 0.5, None, ALU.mult).then_inc(chain, 1)
            dve.scalar_tensor_tensor(var[:, :], tmp[:, 1, :], 0.25, tmp[:, 1, :], ALU.mult, ALU.mult).then_inc(chain, 1)
            dve.tensor_scalar(tmp[:, 3, :], tmp[:, 2, :], 1.0 / D, 1e-5, ALU.mult, ALU.add).then_inc(chain, 1)
            dve.wait_ge(chain, 6)
            dve.tensor_tensor(var[:, :], var[:, :], tmp[:, 3, :], ALU.add).then_inc(var_ready, 1)
            dve.wait_ge(dev_ready, 1)
            dve.reciprocal(rstd[:, :], dev[:, :]).then_inc(rstd_ready, 1)
            dve.wait_ge(rstd_ready, 1)

            def normalise(s, p):
                if s_at_least(s, 2):
                    dve.wait_ge(tp_ready, s - 1)
                    dve.wait_ge(ubo_ready, TPS * s - TPS)
                for t in range(TPS):
                    at = bass.ds(TPS * s + t, 1)
                    dve.tensor_scalar(u_step[p][:, t, :], x_all[:, at, :].rearrange("p o d -> p (o d)"), mean[:, at], rstd[:, at],
                                      ALU.subtract, ALU.mult).then_inc(norm_ready, 1)

            def low_parts(s, p):
                if s_at_least(s, 2):
                    dve.wait_ge(stored[p], stores_before(s, p))
                for k in range(2):
                    dve.wait_ge(hi_ready, 2 * s + k + 1)
                    dve.scalar_tensor_tensor(parts_out[p][k][:, 1, :], qkv_ps[p][k], b_qkv[:, k:k + 1],
                                             parts_out[p][k][:, 0, :].bitcast(F32), ALU.add, ALU.subtract).then_inc(lo_ready, 1)

            dve.wait_ge(consts_in, 7 * 16)
            normalise(0, 0)
            normalise(1, 1)
            normalise(2, 0)
            low_parts(0, 0)
            normalise(3, 1)
            low_parts(1, 1)
            with dve.Fori(2, STEPS // 2) as it:
                normalise(it * 2, 0)
                low_parts(it * 2 - 2, 0)
                normalise(it * 2 + 1, 1)
                low_parts(it * 2 - 1, 1)
            low_parts(STEPS - 2, 0)
            low_parts(STEPS - 1, 1)

            def group(R, g):
                G = R * ROUND + g
                m = g // 2 % 2
                if g % 2 == 0 and (not isinstance(G, int) or G >= 4):
                    dve.wait_ge(ml_ready, unit_of(R, g, 2))
                for j in range(4):
                    dve.wait_ge(s_ready, 4 * G + j + 1)
                    dve.tensor_reduce(mx[m][:, :, 4 * (g % 2) + j], s_ps[j % 2][:, :].rearrange("p (a k) -> p a k", a=2),
                                      AX.X, ALU.max).then_inc(max_ready, 1)
                if g % 2 == 1:
                    dve.wait_ge(max_ready, 4 * G + 4)
                    if not isinstance(G, int) or G >= 4:
                        dve.wait_ge(m_in[m], m_in_count(R, g, 4))
                    high, low = mhl[m][:, 0], mhl[m][:, 1]
                    dve.tensor_scalar(high, mx[m][:, :, :], -1.0, None, ALU.mult).then_inc(mh_ready, 1)
                    dve.wait_ge(mh_ready, unit_of(R, g, 0) + 1)
                    dve.scalar_tensor_tensor(low, mx[m][:, :, :], -1.0, high.bitcast(F32),
                                             ALU.mult, ALU.subtract).then_inc(ml_ready, 1)

            groups(dve, group, 0)

        @block.tensor
        def _(pe):
            pe.wait_ge(ident_ready, 2)
            pe.wait_ge(consts_in, 7 * 16)

            def transposes(s, p):
                if s_at_least(s, 2):
                    pe.wait_ge(ut_ready, s - 1)
                for t in range(TPS):
                    pe.wait_ge(norm_ready, TPS * s + t + 1)
                    mm = pe.transpose(ut_ps[p][:, t * P:(t + 1) * P], u_step[p][:, t, :], ident[:, :])
                mm.then_inc(tp_ready, 1)

            def project(s, p):
                pe.wait_ge(ut_ready, s + 1)
                for k in range(3):
                    if s_at_least(s, 2):
                        if k < 2:
                            pe.wait_ge(lo_ready, 2 * s + k - 3)
                        else:
                            pe.wait_ge(v_ready, 4 * s - 4)
                    pe.matmul(qkv_ps[p][k], w_qkv[:, k, :], ut[p][:, :], start=True, stop=True).then_inc(qkv_ready, 1)

            transposes(0, 0)
            transposes(1, 1)
            project(0, 0)
            transposes(2, 0)
            project(1, 1)
            transposes(3, 1)
            project(2, 0)
            with pe.Fori(2, STEPS // 2) as it:
                transposes(it * 2, 0)
                project(it * 2 - 1, 1)
                transposes(it * 2 + 1, 1)
                project(it * 2, 0)
            project(STEPS - 1, 1)

            pe.wait_ge(lo_ready, 2 * STEPS)
            pe.wait_ge(v_ready, 4 * STEPS)

            def scores(R, G, g, j):
                r = g // 2 % RING
                if j == 0 and g % 2 == 0:
                    pe.wait_ge(unit_in[r], unit_count(R, g))
                if not isinstance(G, int) or 4 * G + j >= 2:
                    pe.wait_ge(max_ready, 4 * G + j - 1)
                for a in range(2):
                    mm = pe.matmul(s_ps[j % 2][:, a * SEQ:(a + 1) * SEQ],
                                   qt[r][0:ZERO_TO, a::2, 4 * (g % 2) + j],
                                   kt[r][0:ZERO_TO, :, 4 * (g % 2) + j], start=True, stop=True)
                mm.then_inc(s_ready, 1)

            def scores_t(R, G, g, j):
                f = (g - LAG_T) % ROUND
                r = f // 2
                if j == 0 and f % 2 == 0:
                    pe.wait_ge(m_in[r % 2], m_in_count(R, g, LAG_T))
                n = 2 * (G - LAG_T) + j // 2
                if j % 2 == 0 and (not isinstance(G, int) or n >= 2):
                    pe.wait_ge(exp_ready, n - 1)
                for a in range(2):
                    mm = pe.matmul(st_ps[j // 2][:, j % 2, a * SEQ:(a + 1) * SEQ],
                                   kt[r][0:ZERO_TO + MAX_ROWS, a::2, 4 * (f % 2) + j],
                                   qt[r][0:ZERO_TO + MAX_ROWS, :, 4 * (f % 2) + j], start=True, stop=True)
                if j % 2 == 1:
                    mm.then_inc(st_ready, 1)

            def values(g):
                f = (g - LAG_T) % ROUND
                for a in range(2):
                    mm = pe.transpose(m_ps[:, a * 32:(a + 1) * 32], vs[f // 2][0:PARTS, a::2, f % 2], ident[0:PARTS, 0:PARTS])
                mm.then_inc(vt_ready, 1)

            def weigh(G, g):
                f = (g - LAG_PV) % ROUND
                pe.wait_ge(exp_ready, 2 * (G - LAG_PV) + 2)
                pe.wait_ge(vp_ready, G - LAG_PV + 1)
                if not isinstance(G, int) or G - LAG_PV >= 1:
                    pe.wait_ge(os_ready, G - LAG_PV)
                for a in range(2):
                    for j in range(4):
                        mm = pe.matmul(pv_ps[32 * j:32 * j + 32, 0:SEQ], vt[f % 2][:, a, j, :],
                                       pt[(2 * f + j // 2) % 4][:, (2 * (j % 2) + a) * SEQ:(2 * (j % 2) + a + 1) * SEQ],
                                       start=(a == 0), stop=(a == 1))
                mm.then_inc(pv_ready, 1)

            def group(R, g):
                G = R * ROUND + g
                for j in range(4):
                    if j == 3 and present(G, LAG_T + 1):
                        pe.wait_ge(vp_ready, G - LAG_T)
                    if present(G, 0):
                        scores(R, G, g, j)
                    if j == 3 and present(G, LAG_T):
                        values(g)
                    if present(G, LAG_T):
                        scores_t(R, G, g, j)
                if present(G, LAG_PV):
                    weigh(G, g)

            def unit_count(R, g):
                return R * 48 + 48

            groups(pe, group, LAG_PV)



EXPERTS, HID = 8, 512
CHUNKS = HID // P
SLOTS = 2 * TOK // P + EXPERTS
DUMP = 2 * TOK
FROUND = 8
MAX_LAG = 5

BATCHES = 8
BT = TILES // BATCHES
BTOK = BT * P
EPS = 1e-5


def routing(nc, io, keep):
    K = keep
    with ExitStack() as ctx:
        def sb(name, shape, dt=F32):
            return ctx.enter_context(nc.sbuf_tensor(name, shape, dt))

        def ps(name, shape):
            return ctx.enter_context(nc.psum_tensor(name, shape, F32))

        def sem(name):
            return ctx.enter_context(nc.semaphore(name))

        wo = sb("wo", [P, D])
        vecs = sb("vecs", [P, 4, D])
        router = sb("router", [P, EXPERTS])
        ln_b_col = sb("ln_b_col", [P, 1])
        egb = sb("egb", [P, 2, EXPERTS])
        den = sb("den", [P, BATCHES + 1, BTOK // 8])
        num = sb("num", [P, TOK])
        spread = sb("spread", [P, 8, P])
        ot = [sb(f"ot{p}", [P, BTOK]) for p in range(2)]
        y = [sb(f"y{p}", [P, BT, D]) for p in range(2)]
        a = [sb(f"a{p}", [P, BT, D]) for p in range(2)]
        xf = [sb(f"xf{p}", [P, BT, D]) for p in range(2)]
        z = sb("z", [P, TILES, D])
        xft = sb("xft", [P, BTOK])
        zero = sb("zero", [1, D])
        bn = sb("bn2", [P, 4, BT, 6])
        mv = sb("mv", [P, 4, BT, 2])
        arg = sb("arg", [P, 4, BT])
        dev = sb("dev2", [P, 4, BT])
        law = sb("law", [P, 3, 4, BT])
        sc = [sb(f"sc{p}", [P, 2, 4, BT]) for p in range(2)]
        logits = sb("logits", [P, TILES, EXPERTS])
        tri = sb("tri", [P, P])
        ones = sb("ones", [P, P])
        shift = sb("shift", [P, P])
        keep_on = sb("keep_on", [P, EXPERTS, TILES])
        e_less = sb("e_less", [P, EXPERTS])
        sel = sb("sel", [P, 3, TILES, EXPERTS])
        work = sb("work", [P, 8, TILES, EXPERTS])
        few = sb("few", [P, 8, TILES])
        place_f = sb("place_f", [P, 2, TILES])
        place_i = sb("place_i", [P, 2, TILES], I32)
        part_i = sb("part_i", [P, 2, 2, TILES], I32)
        lane = sb("lane", [P, 2, TILES])
        tile = sb("tile", [P, 2, TILES])
        start_t = sb("start_t", [P, 2, TILES])
        tiles_i = sb("tiles_i", [P, SLOTS])
        lanes_i = sb("lanes_i", [P, P])
        chunk = sb("chunk", [P, TILES])
        ex = sb("ex", [P, 4, EXPERTS])
        tex = sb("tex", [P, SLOTS, EXPERTS])
        e_of = sb("e_of", [P, SLOTS])
        pair_id = sb("pair_id", [P, 2, TILES])
        at_lane = [num[:, p * 8 * P:(p + 1) * 8 * P].rearrange("p (t l) -> p t l", t=8) for p in range(2)]
        at_tile = [num[:, 16 * P + p * 8 * SLOTS:16 * P + (p + 1) * 8 * SLOTS].rearrange("p (t i) -> p t i", t=8) for p in range(2)]
        dump_row = sb("dump_row", [P, SLOTS])
        row_f = sb("row_f", [P, 3, SLOTS])
        row_i = sb("row_i", [P, SLOTS], I32)

        rb_ps = ps("rb_ps", [P, BTOK])
        y_ps = ps("y_ps", [P, BT, D])
        t_ps = ps("t_ps", [P, BTOK])
        lg_ps = ps("lg_ps", [P, BT, EXPERTS])
        cp = ps("cp", [P, 2, TILES * EXPERTS])
        fold_ps = [ps(f"fold_ps{n}", [P, HID]) for n in range(2)]
        tab_ps = ps("tab_ps", [P, SLOTS])

        den_in = sem("den_in")
        num_in = sem("num_in")
        params_in = sem("params_in")
        weights_in = sem("weights_in")
        gconst = sem("gconst")
        spread_made = sem("spread_made")
        rows_out = sem("rows_out")
        recip_ready = sem("recip_ready")
        rb_ready = sem("rb_ready")
        ot_ready = sem("ot_ready")
        yp_ready = sem("yp_ready")
        y_ready = sem("y_ready")
        bn_ready = sem("bn_ready")
        mv_ready = sem("mv_ready")
        arg_ready = sem("arg_ready")
        var_ready = sem("var_ready")
        dev_ready = sem("dev_ready")
        dev_added = sem("dev_added")
        inv_ready = sem("inv_ready")
        scales = sem("scales")
        n1_ready = sem("n1_ready")
        a_scaled = sem("a_scaled")
        a_ready = sem("a_ready")
        h_ready = sem("h_ready")
        n3_ready = sem("n3_ready")
        xf_scaled = sem("xf_scaled")
        xf_ready = sem("xf_ready")
        xt_done = sem("xt_done")
        xft_ready = sem("xft_ready")
        lg_done = sem("lg_done")
        lg_ready = sem("lg_ready")
        z_ready = sem("z_ready")
        z_out = sem("z_out")
        shift_ready = sem("shift_ready")
        bias_done = sem("bias_done")
        bias_cleared = sem("bias_cleared")
        bias_ready = sem("bias_ready")
        folded = sem("folded")
        dchain = sem("dchain")
        sel_ready = sem("sel_ready")
        cp_ready = sem("cp_ready")
        diff_ready = sem("diff_ready")
        exp_done = sem("exp_done")
        places_ready = sem("places_ready")
        lanes_made = [sem(f"lanes_made{p}") for p in range(2)]
        tiles_made = sem("tiles_made")
        put = sem("put")

        block = ctx.enter_context(nc.Block())
        PEELED = 4
        STAGE_LAG = (0, 1, 2, 4)

        def slots(eng, body):
            for s in range(PEELED):
                body(s, s % 2)
            with eng.Fori(PEELED // 2, BATCHES // 2) as it:
                for p in range(2):
                    body(it * 2 + p, p)
            for s in range(BATCHES, BATCHES + 4):
                body(s, s % 2)

        def present(s, lag):
            return not isinstance(s, int) or 0 <= s - lag < BATCHES

        def late(s, n):
            return not isinstance(s, int) or s >= n

        def tiles_of(b):
            return bass.ds(b * BT, BT)

        @block.sync
        def _(sp):
            for b in range(BATCHES):
                sp.dma_start(den[:, b, :], K.numden[:, HD, b * BTOK:(b + 1) * BTOK].rearrange("c (g r) -> c g r", g=8)).then_inc(den_in, 16)
            half = TOK // 2
            sp.dma_start(wo[:, :], io["Wo"]).then_inc(params_in, 16)
            for n in range(2):
                sp.dma_start(num[:, n * half:(n + 1) * half], K.numden[:, 0:HD, n * half:(n + 1) * half]).then_inc(num_in, 16)
            for n, name in enumerate(("gamma", "beta", "ln_g", "ln_b")):
                sp.dma_start(vecs[:, n, :], io[name].rearrange("(o d) -> o d", o=1).broadcast_to([P, D])).then_inc(params_in, 16)
            sp.dma_start(router[:, :], io["router_w"]).then_inc(params_in, 16)
            sp.dma_start(ln_b_col[:, :], io["ln_b"].rearrange("(d o) -> d o", o=1)).then_inc(params_in, 16)
            sp.dma_start(egb[:, 0, :], io["eg"].rearrange("e d -> d e"), allow_slow_non_contiguous=True).then_inc(params_in, 16)
            sp.dma_start(egb[:, 1, :], io["eb"].rearrange("e d -> d e"), allow_slow_non_contiguous=True).then_inc(params_in, 16)
            sp.dma_start(K.bo[:, :, :], io["ebo"].rearrange("(o e) h -> o e h", o=1).broadcast_to(K.bo.shape)).then_inc(weights_in, 16)
            sp.dma_start(K.w1[:, :, :], io["W1"].rearrange("e d h -> d e h")).then_inc(weights_in, 16)
            sp.dma_start(K.w2[:, :, :], io["W2"].rearrange("e d h -> d e h")).then_inc(weights_in, 16)
            sp.wait_ge(bias_cleared, 2)
            for dst, name in ((K.b1, "b1"), (K.b2, "b2")):
                sp.dma_start(dst[0:1, :, :], io[name].rearrange("(o e) h -> o e h", o=1)).then_inc(weights_in, 16)
            sp.dma_start(K.wo[:, :, :, :], io["eWo"].rearrange("e (c p) d -> p e c d", p=P)).then_inc(weights_in, 16)

            sp.wait_ge(gconst, 16)
            sp.dma_start(K.z_rows[TOK:TOK + 1, :], zero[:, :]).then_inc(rows_out, 16)

            def store(s, p):
                if present(s, 4):
                    b = s - 4
                    sp.wait_ge(z_ready, 4 * b + 4)
                    sp.dma_start(K.z_rows[0:TOK, :].rearrange("(t p) d -> p t d", p=P)[:, tiles_of(b), :],
                                 z[:, tiles_of(b), :]).then_inc(z_out, 16)

            slots(sp, store)
            sp.wait_ge(rows_out, 16)
            sp.wait_ge(z_out, 16 * BATCHES)
            sp.wait_ge(weights_in, 16 * 6)

        @block.gpsimd
        def _(pool):
            pool.memset(spread[:, :, :], 0.0).then_inc(spread_made, 1)
            pool.wait_ge(spread_made, 1)
            pool.affine_select(out=spread[:, :, :].rearrange("p g (c d) -> p g c d", d=HD),
                               in_=spread[:, :, :].rearrange("p g (c d) -> p g c d", d=HD), compare_op=ALU.not_equal,
                               fill=1.0, base=0, pattern=[[-1, 8], [-8, COLS], [0, HD]], channel_multiplier=1).then_inc(spread_made, 1)
            for n, by_stage in enumerate(((1.0, 1.0, 1.0 + EPS, 1.0), (0.0, EPS, EPS * EPS, EPS), (1e-8, 0.0, 0.0, 0.0))):
                for stage, value in enumerate(by_stage):
                    pool.memset(law[:, n, stage, :], value).then_inc(gconst, 1)
            pool.memset(mv[:, :, :, :], 1.0).then_inc(gconst, 1)
            pool.memset(zero[:, :], 0.0).then_inc(gconst, 1)
            pool.memset(ones[:, :], 1.0).then_inc(gconst, 1)
            pool.memset(den[:, BATCHES, :], 1.0).then_inc(gconst, 1)

            for dst in (K.b1, K.b2):
                pool.memset(dst[:, :, :], 0.0).then_inc(bias_cleared, 1)

            def slot(s, p):
                if present(s, 0):
                    pool.wait_ge(n1_ready, 4 * s + 4)
                    pool.tensor_tensor(a[p][:, :, :], a[p][:, :, :], vecs[:, 0:1, :].broadcast_to([P, BT, D]), ALU.mult).then_inc(a_scaled, 1)
                    pool.wait_ge(a_scaled, s + 1)
                    pool.tensor_tensor(a[p][:, :, :], a[p][:, :, :], vecs[:, 1:2, :].broadcast_to([P, BT, D]), ALU.add).then_inc(a_ready, 1)
                if present(s, 2):
                    b = s - 2
                    pool.wait_ge(n3_ready, 4 * b + 4)
                    pool.tensor_tensor(xf[p][:, :, :], xf[p][:, :, :], vecs[:, 2:3, :].broadcast_to([P, BT, D]), ALU.mult).then_inc(xf_scaled, 1)
                    pool.wait_ge(xf_scaled, b + 1)
                    pool.tensor_tensor(z[:, tiles_of(b), :], xf[p][:, :, :], vecs[:, 3:4, :].broadcast_to([P, BT, D]), ALU.add).then_inc(xf_ready, 1)

            pool.wait_ge(params_in, 16 * 9)
            slots(pool, slot)

            pool.memset(tri[:, :], 1.0).then_inc(gconst, 1)
            pool.memset(keep_on[:, :, :], 1.0).then_inc(gconst, 1)
            pool.wait_ge(gconst, 18)
            pool.affine_select(out=tri[:, :], in_=tri[:, :], compare_op=ALU.is_gt, fill=0.0, base=0,
                               pattern=[[1, P]], channel_multiplier=-1).then_inc(gconst, 1)
            pool.affine_select(out=keep_on[:, :, :], in_=keep_on[:, :, :], compare_op=ALU.is_gt, fill=0.0, base=0,
                               pattern=[[0, EXPERTS], [1, TILES]], channel_multiplier=0).then_inc(gconst, 1)

            def iota(dst, pattern, base, channel):
                pool.iota(dst, pattern, base=base, channel_multiplier=channel, allow_small_or_imprecise_dtypes=True).then_inc(gconst, 1)

            iota(e_less[:, :], [[1, EXPERTS]], -EXPERTS, 0)
            iota(tiles_i[:, :], [[1, SLOTS]], 0, 0)
            iota(lanes_i[:, :], [[1, P]], 0, 0)
            iota(chunk[:, :], [[P, TILES]], 0, 0)
            for k in range(2):
                iota(pair_id[:, k, :], [[2 * P, TILES]], k + 1, 2)
            iota(dump_row[:, :], [[P, SLOTS]], DUMP + 1, 1)
            for n in range(1, 8, 2):
                if n == 1:
                    pool.wait_ge(places_ready, 2)
                    pool.wait_ge(gconst, 27)
                k, t = n // 4, n % 4 * 8
                if n >= 3:
                    pool.wait_ge(put, n - 1)
                for i in range(8):
                    pool.tensor_scalar(at_lane[1][:, i, :], lanes_i[:, :], lane[:, k, t + i:t + i + 1], None, ALU.is_equal).then_inc(lanes_made[1], 1)

        @block.scalar
        def _(act):
            def keep_bias(b):
                for n, dst in enumerate((K.b1, K.b2)):
                    act.wait_ge(bias_done, 2 * b + n + 1)
                    act.activation(dst[:, bass.ds(b, 1), :].rearrange("p o h -> p (o h)"), fold_ps[n][:, :], ACT.Copy).then_inc(bias_ready, 1)

            def slot(s, p):
                if present(s, 4):
                    keep_bias(s - 4)
                if present(s, 3):
                    b = s - 3
                    act.wait_ge(xt_done, b + 1)
                    if late(s, 4):
                        act.wait_ge(lg_done, b)
                    act.activation(xft[:, :], t_ps[:, :], ACT.Identity, bias=ln_b_col[:, :]).then_inc(xft_ready, 1)
                act.wait_ge(var_ready, s + 1)
                act.activation(dev[:, :, :], arg[:, :, :], ACT.Sqrt).then_inc(dev_ready, 1)
                act.wait_ge(scales, s + 1)
                if present(s, 0):
                    if late(s, 2):
                        act.wait_ge(h_ready, 4 * s - 4)
                    for t in range(BT):
                        act.activation(a[p][:, t, :], y[p][:, t, :], ACT.Identity, scale=sc[p][:, 0, 0, t:t + 1],
                                       bias=sc[p][:, 1, 0, t:t + 1]).then_inc(n1_ready, 1)
                if present(s, 2):
                    b = s - 2
                    if late(s, 4):
                        act.wait_ge(xf_ready, s - 3)
                        act.wait_ge(xt_done, s - 3)
                    for t in range(BT):
                        act.activation(xf[p][:, t, :], K.x_all[:, bass.ds(b * BT + t, 1), :].rearrange("p o d -> p (o d)"),
                                       ACT.Identity, scale=sc[p][:, 0, 2, t:t + 1], bias=sc[p][:, 1, 2, t:t + 1]).then_inc(n3_ready, 1)
                if present(s, 4):
                    for t in range(BT):
                        row = z[:, bass.ds((s - 4) * BT + t, 1), :].rearrange("p o d -> p (o d)")
                        act.activation(row, row, ACT.Identity, scale=sc[p][:, 0, 3, t:t + 1],
                                       bias=sc[p][:, 1, 3, t:t + 1]).then_inc(z_ready, 1)
                if present(s, 2):
                    if late(s, 3):
                        act.wait_ge(bias_done, 2 * s - 4)
                    act.activation(shift[:, :], ones[:, :], ACT.Identity, scale=egb[:, 1, bass.ds(s - 2, 1)]).then_inc(shift_ready, 1)

            act.wait_ge(params_in, 16 * 9)
            act.wait_ge(gconst, 16)
            slots(act, slot)
            act.wait_ge(diff_ready, 1)
            act.activation(few[:, 3, :], few[:, 2, :], ACT.Exp).then_inc(exp_done, 1)
            with act.Fori(0, EXPERTS) as e:
                for w in (K.w1, K.w2):
                    we = w[:, bass.ds(e, 1), :].rearrange("p o h -> p (o h)")
                    act.activation(we, we, ACT.Copy, scale=egb[:, 0, bass.ds(e, 1)]).then_inc(folded, 1)

        @block.tensor
        def _(pe):
            pe.wait_ge(spread_made, 2)
            pe.wait_ge(params_in, 16 * 9)
            pe.wait_ge(gconst, 16)

            def broadcast(b):
                for g in range(8):
                    mm = pe.matmul(rb_ps[:, g * (BTOK // 8):(g + 1) * (BTOK // 8)], spread[:, g, :],
                                   den[:, bass.ds(b, 1), :].rearrange("p o r -> p (o r)"), start=True, stop=True)
                mm.then_inc(rb_ready, 1)

            def slot(s, p):
                if present(s, 0):
                    if not late(s, 1):
                        pe.wait_ge(recip_ready, 1)
                        broadcast(s)
                    pe.wait_ge(ot_ready, 2 * s + 2)
                    if late(s, 1):
                        pe.wait_ge(y_ready, s)
                    for t in range(BT):
                        mm = pe.matmul(y_ps[:, t, :], ot[p][:, t * P:(t + 1) * P], wo[:, :], start=True, stop=True)
                    mm.then_inc(yp_ready, 1)
                    if not late(s, 1):
                        pe.wait_ge(recip_ready, 2)
                    broadcast(s + 1)
                if present(s, 3):
                    b = s - 3
                    pe.wait_ge(xf_scaled, b + 1)
                    if late(s, 4):
                        pe.wait_ge(xft_ready, b)
                    for t in range(BT):
                        mm = pe.transpose(t_ps[:, t * P:(t + 1) * P], xf[1 - p][:, t, :], K.ident[:, :])
                    mm.then_inc(xt_done, 1)
                    pe.wait_ge(xft_ready, b + 1)
                    if late(s, 4):
                        pe.wait_ge(lg_ready, b)
                    for t in range(BT):
                        mm = pe.matmul(lg_ps[:, t, :], xft[:, t * P:(t + 1) * P], router[:, :], start=True, stop=True)
                    mm.then_inc(lg_done, 1)
                    if not late(s, 4):
                        pe.wait_ge(weights_in, 16 * 6)
                    pe.wait_ge(shift_ready, b + 1)
                    for n, w in enumerate((K.w1, K.w2)):
                        if late(s, 4):
                            pe.wait_ge(bias_ready, 2 * b + n - 1)
                        pe.matmul(fold_ps[n][:, :], shift[:, :], w[:, bass.ds(b, 1), :].rearrange("p o h -> p (o h)"),
                                  start=True, stop=False)
                        pe.matmul(fold_ps[n][:, :], ones[:, :], (K.b1, K.b2)[n][:, bass.ds(b, 1), :].rearrange("p o h -> p (o h)"),
                                  start=False, stop=True).then_inc(bias_done, 1)

            slots(pe, slot)
            pe.wait_ge(sel_ready, 1)
            pe.wait_ge(gconst, 19)
            chosen = sel[:, 2, :, :].rearrange("p t e -> p (t e)")
            pe.matmul(cp[:, 0, :], tri[:, :], chosen, start=True, stop=True)
            pe.matmul(cp[:, 1, :], ones[:, :], chosen, start=True, stop=True, skip_group_check=True).then_inc(cp_ready, 1)
            for n in range(8):
                pe.wait_ge(lanes_made[n % 2], (n // 2 + 1) * (8 if n % 2 else 1))
                pe.wait_ge(tiles_made, 2 * n + 2)
                for t in range(8):
                    mm = pe.matmul(tab_ps[:, :], at_lane[n % 2][:, t, :], at_tile[n % 2][:, t, :],
                                   start=(n == 0 and t == 0), stop=(n == 7 and t == 7))
                mm.then_inc(put, 1)

        @block.vector
        def _(dve):
            count = [0]

            def settled(*made):
                for ins in made:
                    ins.then_inc(dchain, 1)
                    count[0] += 1
                dve.wait_ge(dchain, count[0])

            def moments(stage, rows):
                for t in range(BT):
                    dve.bn_stats(bn[:, stage, t, :], rows(t)).then_inc(bn_ready, 1)

            dve.wait_ge(den_in, 16 * BATCHES)
            dve.reciprocal(den[:, 0, :], den[:, 0, :]).then_inc(recip_ready, 1)
            dve.reciprocal(den[:, 1:BATCHES, :], den[:, 1:BATCHES, :]).then_inc(recip_ready, 1)
            dve.wait_ge(params_in, 16 * 9)
            dve.wait_ge(gconst, 16)
            dve.wait_ge(num_in, 32)

            def keep_logits(b):
                dve.wait_ge(lg_done, b + 1)
                dve.tensor_copy(logits[:, tiles_of(b), :], lg_ps[:, :, :]).then_inc(lg_ready, 1)

            def slot(s, p):
                if present(s, 0):
                    dve.wait_ge(rb_ready, s + 1)
                    if late(s, 2):
                        dve.wait_ge(yp_ready, s - 1)
                    for n in range(2):
                        half = slice(n * 2 * P, (n + 1) * 2 * P)
                        ins = [v.rearrange("p (j u r) -> p u j r", j=4, u=4)
                               for v in (num[:, bass.ds(s * BTOK + n * 2 * P, 2 * P)], rb_ps[:, half])]
                        dve.tensor_tensor(ot[p][:, half].rearrange("p (u j r) -> p u j r", u=4, j=4), *ins, ALU.mult).then_inc(ot_ready, 1)
                if present(s, 4):
                    keep_logits(s - 4)
                if present(s, 2):
                    b = s - 2
                    dve.wait_ge(h_ready, 4 * b + 4)
                    dve.nop(nofuse=True)
                    moments(2, lambda t: K.x_all[:, bass.ds(b * BT + t, 1), :].rearrange("p o d -> p (o d)"))
                if present(s, 4):
                    dve.wait_ge(xf_ready, s - 3)
                    dve.nop(nofuse=True)
                    moments(3, lambda t: z[:, bass.ds((s - 4) * BT + t, 1), :].rearrange("p o d -> p (o d)"))
                if present(s, 0):
                    dve.wait_ge(yp_ready, s + 1)
                    if late(s, 2):
                        dve.wait_ge(n1_ready, 4 * s - 4)
                    dve.tensor_tensor(y[p][:, :, :], y_ps[:, :, :], K.u_all[:, tiles_of(s), :], ALU.add).then_inc(y_ready, 1)
                if present(s, 0):
                    dve.wait_ge(y_ready, s + 1)
                    moments(0, lambda t: y[p][:, t, :])
                if present(s, 1):
                    dve.wait_ge(a_ready, s)
                    moments(1, lambda t: a[1 - p][:, t, :])
                dve.wait_ge(bn_ready, stats(s))
                dve.nop(nofuse=True)
                for stage in range(4):
                    if present(s, STAGE_LAG[stage]):
                        for t in range(BT):
                            dve.bn_aggr(mv[:, stage, t, :], bn[:, stage, t, :]).then_inc(mv_ready, 1)
                dve.wait_ge(mv_ready, stats(s))
                if late(s, 1):
                    dve.wait_ge(dev_ready, s)
                dve.tensor_tensor(arg[:, :, :], mv[:, :, :, 1], law[:, 0, :, :], ALU.mult).then_inc(arg_ready, 1)
                dve.wait_ge(arg_ready, s + 1)
                dve.tensor_tensor(arg[:, :, :], arg[:, :, :], law[:, 1, :, :], ALU.add).then_inc(var_ready, 1)
                dve.wait_ge(dev_ready, s + 1)
                dve.tensor_tensor(dev[:, :, :], dev[:, :, :], law[:, 2, :, :], ALU.add).then_inc(dev_added, 1)
                dve.wait_ge(dev_added, s + 1)
                if late(s, 2):
                    dve.wait_ge(h_ready, h_before(s))
                    dve.wait_ge(n1_ready, 4 * min(s - 1, BATCHES) if isinstance(s, int) else 4 * s - 4)
                if isinstance(s, int) and s >= 6:
                    dve.wait_ge(n3_ready, 4 * min(s - 3, BATCHES))
                    dve.wait_ge(z_ready, 4 * (s - 5))
                dve.reciprocal(sc[p][:, 0, :, :], dev[:, :, :]).then_inc(inv_ready, 1)
                dve.wait_ge(inv_ready, s + 1)
                dve.scalar_tensor_tensor(sc[p][:, 1, :, :], mv[:, :, :, 0], -1.0, sc[p][:, 0, :, :], ALU.mult, ALU.mult).then_inc(scales, 1)
                dve.wait_ge(scales, s + 1)
                if present(s, 1):
                    for t in range(BT):
                        row = K.x_all[:, bass.ds((s - 1) * BT + t, 1), :].rearrange("p o d -> p (o d)")
                        dve.scalar_tensor_tensor(row, a[1 - p][:, t, :], sc[p][:, 0, 1, t:t + 1], row, ALU.mult, ALU.add).then_inc(h_ready, 1)
                    dve.tensor_copy(K.left_out[:, tiles_of(s - 1)], sc[p][:, 1, 1, :]).then_inc(dchain, 1)

            def stats(s):
                if isinstance(s, int):
                    return 4 * sum(max(0, min(s - lag + 1, BATCHES)) for lag in STAGE_LAG)
                return s * 16 - 12

            def h_before(s):
                return 4 * min(s - 2, BATCHES) if isinstance(s, int) else 4 * s - 8

            slots(dve, slot)
            count[0] += BATCHES

            wide = [P, TILES, EXPERTS]
            settled_logits = logits[:, :, :]

            def per_token(v):
                return v.rearrange("p (t o) -> p t o", o=1).broadcast_to(wide)

            def per_expert(v, n=TILES):
                return v.rearrange("p (o e) -> p o e", o=1).broadcast_to([P, n, EXPERTS])

            dve.wait_ge(lg_ready, BATCHES)
            dve.wait_ge(gconst, 27)
            for k in range(2):
                src = settled_logits if k == 0 else work[:, 2, :, :]
                settled(dve.tensor_reduce(few[:, k, :], src, AX.X, ALU.max))
                settled(dve.tensor_tensor(work[:, 0, :, :], src, per_token(few[:, k, :]), ALU.is_equal))
                settled(dve.tensor_tensor(work[:, 1, :, :], work[:, 0, :, :], per_expert(e_less[:, :]), ALU.mult))
                settled(dve.tensor_reduce(few[:, 4 + k, :], work[:, 1, :, :], AX.X, ALU.min))
                settled(dve.tensor_tensor(sel[:, k, :, :], per_expert(e_less[:, :]), per_token(few[:, 4 + k, :]), ALU.is_equal))
                if k == 0:
                    settled(dve.scalar_tensor_tensor(work[:, 2, :, :], sel[:, 0, :, :], -3e38, logits[:, :, :], ALU.mult, ALU.add))
            dve.tensor_tensor(sel[:, 2, :, :], sel[:, 0, :, :], sel[:, 1, :, :], ALU.add).then_inc(sel_ready, 1)
            dve.tensor_tensor(few[:, 2, :], few[:, 1, :], few[:, 0, :], ALU.subtract).then_inc(diff_ready, 1)
            dve.wait_ge(cp_ready, 1)
            total = work[:, 4, :, :].rearrange("p a b -> p (a b)").rearrange("p (e t) -> p e t", e=EXPERTS)
            upto = work[:, 5, :, :].rearrange("p a b -> p (a b)").rearrange("p (e t) -> p e t", e=EXPERTS)
            settled(dve.tensor_copy(total, cp[:, 1, :].rearrange("p (t e) -> p e t", t=TILES)))
            settled(dve.tensor_tensor_scan(upto.rearrange("p e t -> p (e t)"), keep_on[:, :, :].rearrange("p e t -> p (e t)"),
                                           total.rearrange("p e t -> p (e t)"), 0.0, ALU.mult, ALU.add))
            count_e, tiles_e, ends_e, first_e = (ex[:, n, :] for n in range(4))
            filled = work[:, 7, :, :].rearrange("p a b -> p (a b)").rearrange("p (e t) -> p e t", e=EXPERTS)
            settled(dve.tensor_copy(count_e, upto[:, :, TILES - 1]))
            settled(dve.tensor_tensor(filled, count_e.rearrange("p (e o) -> p e o", o=1).broadcast_to([P, EXPERTS, TILES]),
                                      chunk[:, :].rearrange("p (o t) -> p o t", o=1).broadcast_to([P, EXPERTS, TILES]), ALU.is_gt),
                    dve.tensor_tensor(upto, upto, total, ALU.subtract))
            place = work[:, 6, :, :]
            settled(dve.tensor_reduce(tiles_e, filled, AX.X, ALU.add),
                    dve.tensor_tensor(place, cp[:, 0, :].rearrange("p (t e) -> p t e", t=TILES),
                                      upto.rearrange("p e t -> p t e"), ALU.add))
            settled(dve.tensor_tensor_scan(ends_e, ones[:, 0:EXPERTS], tiles_e, 0.0, ALU.mult, ALU.add),
                    *[dve.tensor_tensor(work[:, k, :, :], place, sel[:, k, :, :], ALU.mult) for k in range(2)])
            settled(dve.tensor_tensor(first_e, ends_e, tiles_e, ALU.subtract),
                    *[dve.tensor_reduce(place_f[:, k, :], work[:, k, :, :], AX.X, ALU.add) for k in range(2)])
            settled(dve.tensor_copy(place_i[:, :, :], place_f[:, :, :]),
                    *[dve.tensor_tensor(work[:, 2 + k, :, :], sel[:, k, :, :], per_expert(first_e), ALU.mult) for k in range(2)])
            settled(dve.tensor_scalar(part_i[:, 0, :, :], place_i[:, :, :], P - 1, None, ALU.bitwise_and),
                    dve.tensor_scalar(part_i[:, 1, :, :], place_i[:, :, :], 7, None, ALU.arith_shift_right))
            dve.tensor_copy(lane[:, :, :], part_i[:, 0, :, :]).then_inc(places_ready, 1)
            settled(dve.tensor_copy(place_f[:, :, :], part_i[:, 1, :, :]),
                    *[dve.tensor_reduce(start_t[:, k, :], work[:, 2 + k, :, :], AX.X, ALU.add) for k in range(2)])
            dve.tensor_tensor(tile[:, :, :], place_f[:, :, :], start_t[:, :, :], ALU.add).then_inc(places_ready, 1)
            dve.wait_ge(places_ready, 2)
            for n in range(8):
                k, t = n // 4, n % 4 * 8
                if n >= 2:
                    dve.wait_ge(put, n - 1)
                if n % 2 == 0:
                    dve.tensor_tensor(at_lane[0][:, :, :], lane[:, k, t:t + 8].rearrange("p (t o) -> p t o", o=1).broadcast_to([P, 8, P]),
                                      lanes_i[:, :].rearrange("p (o l) -> p o l", o=1).broadcast_to([P, 8, P]), ALU.is_equal).then_inc(lanes_made[0], 1)
                shape = [P, 8, SLOTS]
                dve.tensor_tensor(at_tile[n % 2][:, :, :], tile[:, k, t:t + 8].rearrange("p (t o) -> p t o", o=1).broadcast_to(shape),
                                  tiles_i[:, :].rearrange("p (o i) -> p o i", o=1).broadcast_to(shape), ALU.is_equal).then_inc(tiles_made, 1)
                dve.wait_ge(tiles_made, 2 * n + 1)
                dve.tensor_tensor(at_tile[n % 2][:, :, :], at_tile[n % 2][:, :, :],
                                  pair_id[:, k, t:t + 8].rearrange("p (t o) -> p t o", o=1).broadcast_to(shape), ALU.mult).then_inc(tiles_made, 1)

            shape = [P, SLOTS, EXPERTS]
            settled(dve.tensor_tensor(tex[:, :, :], tiles_i[:, :].rearrange("p (i o) -> p i o", o=1).broadcast_to(shape),
                                      per_expert(ends_e, SLOTS), ALU.is_ge))
            settled(dve.tensor_reduce(e_of[:, :], tex[:, :, :], AX.X, ALU.add))
            settled(dve.memset(K.expert[:, 0:MAX_LAG], 0),
                    dve.tensor_scalar(K.expert[:, MAX_LAG:], e_of[:, :], float(EXPERTS - 1), None, ALU.min))
            dve.wait_ge(exp_done, 1)
            settled(dve.tensor_scalar(few[:, 6, :], few[:, 3, :], 1.0, None, ALU.add))
            settled(dve.reciprocal(K.gates[:, 0, :], few[:, 6, :]))
            settled(dve.tensor_tensor(K.gates[:, 1, :], few[:, 3, :], K.gates[:, 0, :], ALU.mult))

            dve.wait_ge(put, 8)
            settled(dve.tensor_scalar(row_f[:, 0, :], tab_ps[:, :], 0.0, None, ALU.is_equal))
            settled(dve.tensor_tensor(row_f[:, 1, :], row_f[:, 0, :], dump_row[:, :], ALU.mult),
                    dve.tensor_scalar(row_f[:, 2, :], tab_ps[:, :], -1.0, None, ALU.add))
            settled(dve.tensor_tensor(row_f[:, 0, :], row_f[:, 1, :], row_f[:, 2, :], ALU.add))
            settled(dve.tensor_copy(K.to[:, :], row_f[:, 0, :]), dve.tensor_copy(row_i[:, :], row_f[:, 0, :]))
            settled(dve.tensor_scalar(row_i[:, :], row_i[:, :], 1, None, ALU.arith_shift_right))
            settled(dve.tensor_scalar(K.source[:, 0:SLOTS], row_i[:, :], TOK, None, ALU.min),
                    dve.memset(K.source[:, SLOTS:], TOK))
            dve.wait_ge(folded, 2 * EXPERTS)


X_LAG, M_LAG, H_LAG, O_LAG = 1, 2, 4, 5
AHEAD = 2


def experts(nc, io, keep):
    K = keep
    w1, w2, wo, b1, b2, bo = K.w1, K.w2, K.wo, K.b1, K.b2, K.bo
    with ExitStack() as ctx:
        def sb(name, shape, dt=F32):
            return ctx.enter_context(nc.sbuf_tensor(name, shape, dt))

        def ps(name, shape):
            return ctx.enter_context(nc.psum_tensor(name, shape, F32))

        def sem(name):
            return ctx.enter_context(nc.semaphore(name))

        source = [sb(f"source{r}", [P, 1], U32) for r in range(FROUND)]
        to = [sb(f"to{r}", [P, 1], U32) for r in range(4)]
        rows = [sb(f"rows{r}", [P, D]) for r in range(4)]
        zt = [sb(f"zt{r}", [P, P]) for r in range(2)]
        gate_in = [sb(f"gate_in{r}", [P, HID]) for r in range(2)]
        silu = [sb(f"silu{r}", [P, HID]) for r in range(2)]
        up = [sb(f"up{r}", [P, HID]) for r in range(2)]
        hid = [sb(f"hid{r}", [P, HID]) for r in range(2)]
        ht = [sb(f"ht{r}", [P, HID]) for r in range(2)]
        o_f = [sb(f"o_f{r}", [P, D]) for r in range(2)]
        o = [sb(f"o{r}", [P, D]) for r in range(4)]

        x1_ps = [ps(f"x1_ps{r}", [P, HID]) for r in range(2)]
        x2_ps = [ps(f"x2_ps{r}", [P, HID]) for r in range(2)]
        ht_ps = ps("ht_ps", [P, HID])
        zt_ps = ps("zt_ps", [P, P])
        o_ps = [ps(f"o_ps{r}", [P, D]) for r in range(2)]

        rows_in = [sem(f"rows_in{r}") for r in range(4)]
        source_ready = sem("source_ready")
        to_ready = sem("to_ready")
        zt_done = sem("zt_done")
        zt_ready = sem("zt_ready")
        x2_ready = sem("x2_ready")
        x1_ready = sem("x1_ready")
        gate_sum = sem("gate_sum")
        gate_ready = sem("gate_ready")
        silu_ready = sem("silu_ready")
        up_ready = sem("up_ready")
        mul_ready = sem("mul_ready")
        hid_ready = sem("hid_ready")
        ht_done = sem("ht_done")
        ht_ready = sem("ht_ready")
        o_done = sem("o_done")
        o_sum = sem("o_sum")
        o_ready = sem("o_ready")
        sent = [sem(f"o_sent{r}") for r in range(4)]

        block = ctx.enter_context(nc.Block())

        def tiles(eng, body, lag):
            for J in range(FROUND):
                body(J, J)
            with eng.Fori(1, SLOTS // FROUND) as it:
                for q in range(FROUND):
                    body(it * FROUND + q, q)
            for q in range(lag):
                body(SLOTS + q, q)

        def present(J, lag):
            return not isinstance(J, int) or 0 <= J - lag < SLOTS

        def late(J, n):
            return not isinstance(J, int) or J >= n

        def filled(J, q, lag, ring, by=16):
            if isinstance(J, int):
                return by * ((J - lag) // ring + 1)
            return (J - q) * (by // ring) + by * ((q - lag) // ring + 1)

        def experts_of(eng, regs, J):
            at = slice(J, min(J + FROUND + MAX_LAG, SLOTS + MAX_LAG)) if isinstance(J, int) else bass.ds(J, FROUND + MAX_LAG)
            n = at.stop - at.start if isinstance(J, int) else FROUND + MAX_LAG
            eng.reg_load(regs[:n], K.expert[0:1, at])

        def expert(eng, regs, q, lag):
            return eng.snap(regs[q + MAX_LAG - lag], min_val=0, max_val=EXPERTS - 1)

        def registers(eng, name):
            return [eng.alloc_register(f"{name}{n}") for n in range(FROUND + MAX_LAG)]

        @block.gpsimd
        def _(pool):
            def step(J, q):
                if present(J, 0):
                    r = q % 4
                    pool.wait_ge(source_ready, J + 1)
                    if late(J, 4):
                        pool.wait_ge(zt_done, J - 3)
                    pool.nop(nofuse=True)
                    pool.indirect_dma_start(rows[r][:, :], None, K.z_rows[:, :],
                                            bass.IndirectOffsetOnAxis(source[q][:, :], 0)).then_inc(rows_in[r], 16)
                lag = AHEAD + O_LAG
                if present(J, lag):
                    f = (q - lag) % FROUND
                    pool.wait_ge(o_ready, J - lag + 1)
                    pool.wait_ge(to_ready, J - lag + 1)
                    pool.nop(nofuse=True)
                    pool.indirect_dma_start(K.results[:, :], bass.IndirectOffsetOnAxis(to[f % 4][:, :], 0),
                                            o[f % 4][:, :], None).then_inc(sent[f % 4], 16)

            tiles(pool, step, AHEAD + O_LAG)
            for r in range(4):
                pool.wait_ge(sent[r], 16 * SLOTS // 4)

        @block.scalar
        def _(act):
            def step(J, q):
                if present(J, H_LAG):
                    f = (q - H_LAG) % FROUND
                    act.wait_ge(ht_done, J - H_LAG + 1)
                    if late(J, H_LAG + 2):
                        act.wait_ge(o_done, J - H_LAG - 1)
                    act.activation(ht[f % 2][:, :], ht_ps[:, :], ACT.Copy).then_inc(ht_ready, 1)
                if present(J, 0):
                    act.wait_ge(zt_done, J + 1)
                    if late(J, 2):
                        act.wait_ge(x1_ready, J - 1)
                    act.activation(zt[q % 2][:, :], zt_ps[:, :], ACT.Copy).then_inc(zt_ready, 1)
                if present(J, X_LAG):
                    f = (q - X_LAG) % FROUND
                    act.wait_ge(gate_ready, J - X_LAG + 1)
                    if late(J, X_LAG + 2):
                        act.wait_ge(mul_ready, J - X_LAG - 1)
                    act.activation(silu[f % 2][:, :], gate_in[f % 2][:, :], ACT.Silu).then_inc(silu_ready, 1)

            tiles(act, step, H_LAG)

        @block.vector
        def _(dve):
            regs = registers(dve, "dve_e")

            def fetch(J, r):
                at = slice(J, J + 1) if isinstance(J, int) else bass.ds(J, 1)
                dve.tensor_copy(source[r][:, :], K.source[:, at]).then_inc(source_ready, 1)

            for r in range(4):
                fetch(r, r)

            def step(J, q):
                if q == 0:
                    experts_of(dve, regs, J)
                if present(J, X_LAG):
                    f = (q - X_LAG) % FROUND
                    n = J - X_LAG
                    e = expert(dve, regs, q, X_LAG)
                    bias = [v[:, bass.ds(e, 1), :].rearrange("p o h -> p (o h)") for v in (b1, b2)]
                    dve.wait_ge(x2_ready, n + 1)
                    if late(J, X_LAG + 2):
                        dve.wait_ge(silu_ready, n - 1)
                    dve.tensor_tensor(gate_in[f % 2][:, :], x2_ps[f % 2][:, :], bias[1], ALU.add).then_inc(gate_sum, 1)
                if present(J, M_LAG):
                    g = (q - M_LAG) % FROUND
                    m = J - M_LAG
                    dve.wait_ge(up_ready, m + 1)
                    dve.wait_ge(silu_ready, m + 1)
                    if late(J, M_LAG + 2):
                        dve.wait_ge(ht_done, m - 1)
                    dve.tensor_tensor(hid[g % 2][:, :], up[g % 2][:, :], silu[g % 2][:, :], ALU.mult).then_inc(mul_ready, 1)
                if present(J, X_LAG):
                    dve.wait_ge(gate_sum, n + 1)
                    dve.tensor_scalar(gate_in[f % 2][:, :], gate_in[f % 2][:, :], -20.0, 20.0, ALU.max, ALU.min).then_inc(gate_ready, 1)
                    dve.wait_ge(x1_ready, n + 1)
                    if late(J, X_LAG + 2):
                        dve.wait_ge(mul_ready, n - 1)
                    dve.tensor_tensor(up[f % 2][:, :], x1_ps[f % 2][:, :], bias[0], ALU.add).then_inc(up_ready, 1)
                if present(J, M_LAG):
                    dve.wait_ge(mul_ready, m + 1)
                    dve.tensor_scalar(hid[g % 2][:, :], hid[g % 2][:, :], -1e4, 1e4, ALU.max, ALU.min).then_inc(hid_ready, 1)
                if present(J, O_LAG):
                    f = (q - O_LAG) % FROUND
                    n = J - O_LAG
                    e = expert(dve, regs, q, O_LAG)
                    dve.wait_ge(o_done, n + 1)
                    if late(J, O_LAG + 2):
                        dve.wait_ge(o_ready, n - 1)
                    dve.tensor_tensor(o_f[f % 2][:, :], o_ps[f % 2][:, :], bo[:, bass.ds(e, 1), :].rearrange("p o d -> p (o d)"),
                                      ALU.add).then_inc(o_sum, 1)
                    if late(J, O_LAG + 4):
                        dve.wait_ge(sent[f % 4], filled(J, q, O_LAG + 4, 4))
                    at = slice(n, n + 1) if isinstance(J, int) else bass.ds(n, 1)
                    dve.tensor_copy(to[f % 4][:, :], K.to[:, at]).then_inc(to_ready, 1)
                if present(J, 0):
                    if late(J, 4):
                        dve.wait_ge(zt_done, J - 3)
                    fetch(J + 4, (q + 4) % FROUND)
                if present(J, O_LAG):
                    dve.wait_ge(o_sum, n + 1)
                    dve.tensor_scalar(o[f % 4][:, :], o_f[f % 2][:, :], -1e4, 1e4, ALU.max, ALU.min).then_inc(o_ready, 1)

            tiles(dve, step, O_LAG)

        @block.tensor
        def _(pe):
            regs = registers(pe, "pe_e")

            def step(J, q):
                if q == 0:
                    experts_of(pe, regs, J)
                if present(J, H_LAG):
                    f = (q - H_LAG) % FROUND
                    n = J - H_LAG
                    pe.wait_ge(hid_ready, n + 1)
                    if late(J, H_LAG + 1):
                        pe.wait_ge(ht_ready, n)
                    for c in range(CHUNKS):
                        mm = pe.transpose(ht_ps[:, c * P:(c + 1) * P], hid[f % 2][:, c * P:(c + 1) * P], K.ident[:, :])
                    mm.then_inc(ht_done, 1)
                if present(J, X_LAG):
                    f = (q - X_LAG) % FROUND
                    n = J - X_LAG
                    e = expert(pe, regs, q, X_LAG)
                    pe.wait_ge(zt_ready, n + 1)
                    if late(J, X_LAG + 2):
                        pe.wait_ge(gate_sum, n - 1)
                        pe.wait_ge(up_ready, n - 1)
                    pe.matmul(x2_ps[f % 2][:, :], zt[f % 2][:, :], w2[:, bass.ds(e, 1), :].rearrange("p o h -> p (o h)"),
                              start=True, stop=True).then_inc(x2_ready, 1)
                    pe.matmul(x1_ps[f % 2][:, :], zt[f % 2][:, :], w1[:, bass.ds(e, 1), :].rearrange("p o h -> p (o h)"),
                              start=True, stop=True).then_inc(x1_ready, 1)
                if present(J, 0):
                    pe.wait_ge(rows_in[q % 4], filled(J, q, 0, 4))
                    if late(J, 1):
                        pe.wait_ge(zt_ready, J)
                    pe.transpose(zt_ps[:, :], rows[q % 4][:, :], K.ident[:, :]).then_inc(zt_done, 1)
                if present(J, H_LAG):
                    f = (q - H_LAG) % FROUND
                    n = J - H_LAG
                    e = expert(pe, regs, q, H_LAG)
                    pe.wait_ge(ht_ready, n + 1)
                    if late(J, H_LAG + 2):
                        pe.wait_ge(o_sum, n - 1)
                    for c in range(CHUNKS):
                        mm = pe.matmul(o_ps[f % 2][:, :], ht[f % 2][:, c * P:(c + 1) * P],
                                       wo[:, bass.ds(e, 1), c, :].rearrange("p o d -> p (o d)"),
                                       start=(c == 0), stop=(c == CHUNKS - 1))
                    mm.then_inc(o_done, 1)

            tiles(pe, step, H_LAG)


def combine(nc, io, keep, out):
    K = keep
    PART = 4
    N = TILES // PART
    with ExitStack() as ctx:
        def sb(name, shape, dt=F32):
            return ctx.enter_context(nc.sbuf_tensor(name, shape, dt))

        def sem(name):
            return ctx.enter_context(nc.semaphore(name))

        f = [sb(f"f{n}", [P, N, 2, D]) for n in range(PART)]
        bn = sb("bn3", [P, TILES, 6])
        sm = sb("sm3", [P, 5, TILES])
        mv = sb("mv3", [P, 2, TILES])
        r = sb("r3", [P, TILES])
        rest = sb("rest", [P, 2, TILES])
        half = sb("half3", [P, TILES])
        f_in = [sem(f"f_in{n}") for n in range(PART)]
        chain = sem("chain3")
        half_made = sem("half_made")
        var_made = sem("var_made")
        r_made = sem("r_made")
        out_made = sem("out_made")
        out_sent = sem("out_sent")
        block = ctx.enter_context(nc.Block())

        @block.sync
        def _(sp):
            src = K.results[0:DUMP, :].rearrange("(t p k) d -> p t (k d)", p=P, k=2)
            for n in range(PART):
                sp.dma_start(f[n][:, :, :, :].rearrange("p t k d -> p t (k d)"), src[:, n * N:(n + 1) * N, :]).then_inc(f_in[n], 16)
            dst = out.rearrange("b (t p) d -> p (b t) d", p=P)
            for n in range(PART):
                sp.wait_ge(out_made, n + 1)
                sp.dma_start(dst[:, n * N:(n + 1) * N, :], K.x_all[:, n * N:(n + 1) * N, :]).then_inc(out_sent, 16)
            sp.wait_ge(out_sent, 16 * PART)

        @block.gpsimd
        def _(pool):
            pool.memset(half[:, :], -0.5).then_inc(half_made, 1)
            pool.wait_ge(half_made, 1)
            for n in range(PART):
                at = slice(n * N, (n + 1) * N)
                pool.wait_ge(var_made, n + 1)
                pool.tensor_tensor(r[:, at], mv[:, 1, at], half[:, at], ALU.pow).then_inc(r_made, 1)

        @block.vector
        def _(dve):
            count = [0]

            def settled(*made):
                for ins in made:
                    ins.then_inc(chain, 1)
                    count[0] += 1
                dve.wait_ge(chain, count[0])

            def by_row(v):
                return v.rearrange("p (t o) -> p t o", o=1).broadcast_to([P, N, D])

            def add_up(n):
                at = slice(n * N, (n + 1) * N)
                dve.wait_ge(f_in[n], 16)
                a, b = f[n][:, :, 0, :], f[n][:, :, 1, :]
                settled(dve.tensor_tensor(a, a, by_row(K.gates[:, 0, at]), ALU.mult),
                        dve.tensor_tensor(b, b, by_row(K.gates[:, 1, at]), ALU.mult))
                settled(dve.tensor_tensor(a, a, b, ALU.add))
                settled(*[dve.bn_stats(bn[:, n * N + t, :], f[n][:, t, 0, :]) for t in range(N)])
                settled(dve.tensor_tensor(sm[:, 0, at], bn[:, at, 1], bn[:, at, 4], ALU.add),
                        dve.tensor_tensor(sm[:, 1, at], bn[:, at, 1], bn[:, at, 4], ALU.subtract),
                        dve.tensor_tensor(sm[:, 2, at], bn[:, at, 2], bn[:, at, 5], ALU.add))
                settled(dve.tensor_scalar(mv[:, 0, at], sm[:, 0, at], 0.5, None, ALU.mult),
                        dve.scalar_tensor_tensor(sm[:, 3, at], sm[:, 1, at], 0.25, sm[:, 1, at], ALU.mult, ALU.mult),
                        dve.tensor_scalar(sm[:, 4, at], sm[:, 2, at], 1.0 / D, 1e-5, ALU.mult, ALU.add))
                dve.tensor_tensor(mv[:, 1, at], sm[:, 3, at], sm[:, 4, at], ALU.add).then_inc(var_made, 1)

            def finish(n):
                at = slice(n * N, (n + 1) * N)
                a = f[n][:, :, 0, :]
                dve.wait_ge(r_made, n + 1)
                settled(dve.tensor_tensor(rest[:, 0, at], mv[:, 0, at], r[:, at], ALU.mult))
                settled(dve.tensor_tensor(rest[:, 1, at], K.left_out[:, at], rest[:, 0, at], ALU.subtract))
                settled(*[dve.scalar_tensor_tensor(a[:, t, :], a[:, t, :], r[:, n * N + t:n * N + t + 1], K.x_all[:, n * N + t, :], ALU.mult, ALU.add)
                          for t in range(N)])
                dve.tensor_tensor(K.x_all[:, at, :], a, by_row(rest[:, 1, at]), ALU.add).then_inc(out_made, 1)

            for n in range(PART):
                add_up(n)
                if n:
                    finish(n - 1)
            finish(PART - 1)


def program(nc, io, out):
    with ExitStack() as ctx:
        class keep:
            x_all = ctx.enter_context(nc.sbuf_tensor("x_all", [P, TILES, D], F32))
            ident = ctx.enter_context(nc.sbuf_tensor("ident", [P, P], F32))
            gates = ctx.enter_context(nc.sbuf_tensor("gates", [P, 2, TILES], F32))
            expert = ctx.enter_context(nc.sbuf_tensor("expert", [P, MAX_LAG + SLOTS], I32))
            source = ctx.enter_context(nc.sbuf_tensor("source", [P, SLOTS + MAX_LAG], U32))
            to = ctx.enter_context(nc.sbuf_tensor("to", [P, SLOTS], U32))
            left_out = ctx.enter_context(nc.sbuf_tensor("left_out", [P, TILES], F32))
            numden = nc.dram_tensor("numden", [COLS, 2 * HD, TOK], F32).ap()
            z_rows = nc.dram_tensor("z_rows", [TOK + 1, D], F32).ap()
            results = nc.dram_tensor("results", [DUMP + P * SLOTS, D], F32).ap()

        keep.u_all = ctx.enter_context(nc.sbuf_tensor("u_all", [P, TILES, D], F32))
        attention(nc, io, keep)
        keep.w1 = ctx.enter_context(nc.sbuf_tensor("w1", [P, EXPERTS, HID], F32))
        keep.w2 = ctx.enter_context(nc.sbuf_tensor("w2", [P, EXPERTS, HID], F32))
        keep.wo = ctx.enter_context(nc.sbuf_tensor("expert_wo", [P, EXPERTS, CHUNKS, D], F32))
        keep.b1 = ctx.enter_context(nc.sbuf_tensor("b1", [P, EXPERTS, HID], F32))
        keep.b2 = ctx.enter_context(nc.sbuf_tensor("b2", [P, EXPERTS, HID], F32))
        keep.bo = ctx.enter_context(nc.sbuf_tensor("expert_bo", [P, EXPERTS, D], F32))
        routing(nc, io, keep)
        experts(nc, io, keep)
        combine(nc, io, keep, out)


_INS = {"x": "L0_attn_x", "Wq": "L0_attn_Wq", "bq": "L0_attn_bq", "Wk": "L0_attn_Wk", "bk": "L0_attn_bk",
        "Wv": "L0_attn_Wv", "bv": "L0_attn_bv", "Wo": "L0_attn_Wo", "bo": "L0_attn_bo", "gamma": "L0_attn_gamma",
        "beta": "L0_attn_beta", "ln_g": "L0_ffn_ln_g", "ln_b": "L0_ffn_ln_b", "router_w": "L0_ffn_router_w",
        "eg": "L0_ffn_eg", "eb": "L0_ffn_eb", "W1": "L0_ffn_W1", "b1": "L0_ffn_b1", "W2": "L0_ffn_W2",
        "b2": "L0_ffn_b2", "eWo": "L0_ffn_Wo", "ebo": "L0_ffn_bo"}


def kernel(**inputs):
    import numpy as np
    import concourse.bacc as bacc
    from concourse.bass_utils import run_bass_kernel_spmd

    nc = bacc.Bacc("TRN2", target_bir_lowering=False, num_devices=1)
    arrays, io = {}, {}
    for short, name in _INS.items():
        arrays[name] = np.ascontiguousarray(inputs[name])
        io[short] = nc.dram_tensor(name, arrays[name].shape, F32, kind="ExternalInput").ap()
    out = nc.dram_tensor("out", [BATCH, SEQ, D], F32, kind="ExternalOutput").ap()
    program(nc, io, out)
    result = run_bass_kernel_spmd(nc, [arrays], core_ids=[0])
    return result.results[0]["out"]
```

```python
from contextlib import ExitStack

import concourse.bass as bass
from concourse import mybir

F32 = mybir.dt.float32
F32R = mybir.dt.float32r
BF16 = mybir.dt.bfloat16
I32 = mybir.dt.int32
U32 = mybir.dt.uint32
ALU = mybir.AluOpType
ACT = mybir.ActivationFunctionType
AX = mybir.AxisListType

P = 128
BATCH, SEQ, D = 16, 256, 128
TOK = BATCH * SEQ
TILES = TOK // P
HEADS, HD = 16, 8
COLS = D // HD
RPH = SEQ // HEADS
SCALE = HD ** -0.5

STEP = 512
STEPS = TOK // STEP
TPS = STEP // P
UNITS = TOK // P
RING = 4
GROUPS = 2 * UNITS
ROUND = 2 * RING
PARTS = 4 * HD
ZERO_TO = 96
LAG_T, LAG_PV, LAG_OUT = 4, 5, 6
MAX_ROWS = 2


def attention(nc, io, keep):
    x_all, u_all, ident, numden = keep.x_all, keep.u_all, keep.ident, keep.numden
    with ExitStack() as ctx:
        def sb(name, shape, dt=F32):
            return ctx.enter_context(nc.sbuf_tensor(name, shape, dt))

        def ps(name, shape):
            return ctx.enter_context(nc.psum_tensor(name, shape, F32))

        def sem(name):
            return ctx.enter_context(nc.semaphore(name))

        def dram(name, shape, dt=F32):
            return nc.dram_tensor(name, shape, dt).ap()

        q_parts = dram("q_parts", [P, 4, TOK])
        k_parts = dram("k_parts", [P, 4, TOK])
        v_rows = dram("v_rows", [P, 4, TOK // 4])

        w_qkv = sb("w_qkv", [P, 3, D])
        b_qkv = sb("b_qkv", [P, 3])
        bo_all = sb("bo_all", [P, D])
        bn = sb("bn", [P, TILES, 6])
        mean = sb("mean", [P, TILES])
        var = sb("var", [P, TILES])
        rstd = sb("rstd", [P, TILES])
        tmp = sb("tmp", [P, 4, TILES])
        dev = sb("dev", [P, TILES])
        u_steps = sb("u_steps", [P, 2, TPS, D])
        u_step = [u_steps[:, i] for i in range(2)]
        ut = [sb(f"ut{i}", [P, STEP]) for i in range(2)]
        parts_out = [[sb(f"parts_out{i}{k}", [P, 2, STEP], F32R) for k in range(2)] for i in range(2)]
        v_out = [sb(f"v_out{i}", [P, STEP]) for i in range(2)]

        qt = [sb(f"qt{r}", [P, SEQ, 8], F32R) for r in range(RING)]
        kt = [sb(f"kt{r}", [P, SEQ, 8], F32R) for r in range(RING)]
        vs = [sb(f"vs{r}", [P, SEQ, 2]) for r in range(RING)]
        vt = [sb(f"vt{r}", [P, 2, 4, 32]) for r in range(2)]
        mx = [sb(f"mx{r}", [P, 2, 8]) for r in range(2)]
        mhl = [sb(f"mhl{r}", [P, MAX_ROWS, 2, 8], F32R) for r in range(2)]
        pt = [parts_out[r // 2][r % 2][:, :, :].bitcast(F32).rearrange("p a b -> p (a b)") for r in range(4)]
        os_ = [u_steps[:, :, :, :].rearrange("p i t d -> p (i t d)").rearrange("p (c t) -> p c t", c=COLS), sb("os1", [P, COLS, 64])]

        s_ps = [ps(f"s_ps{i}", [P, 512]) for i in range(2)]
        st_ps = [ps(f"st_ps{i}", [P, 2, 512]) for i in range(2)]
        pv_ps = ps("pv_ps", [P, 512])
        m_ps = ps("m_ps", [P, 512])
        ut_ps = s_ps
        qkv_ps = [[st_ps[0][:, 0, :], st_ps[0][:, 1, :], st_ps[1][:, 0, :]], [st_ps[1][:, 1, :], pv_ps[:, :], m_ps[:, :]]]

        consts_in = sem("consts_in")
        x_in = [sem(f"x_in{i}") for i in range(2)]
        ident_ready = sem("ident_ready")
        dev_ready = sem("x_dev_ready")
        stats_ready = sem("stats_ready")
        chain = sem("chain")
        var_ready = sem("var_ready")
        rstd_ready = sem("rstd_ready")
        norm_ready = sem("norm_ready")
        ubo_ready = sem("ubo_ready")
        tp_ready = sem("tp_ready")
        ut_ready = sem("ut_ready")
        qkv_ready = sem("qkv_ready")
        hi_ready = sem("hi_ready")
        lo_ready = sem("lo_ready")
        v_ready = sem("v_ready")
        stored = [sem(f"stored{i}") for i in range(2)]
        q_cleared = sem("q_cleared")
        k_cleared = sem("k_cleared")
        v_cleared = sem("v_cleared")
        unit_in = [sem(f"unit_in{r}") for r in range(RING)]
        s_ready = sem("s_ready")
        max_ready = sem("max_ready")
        mh_ready = sem("mh_ready")
        ml_ready = sem("ml_ready")
        m_in = [sem(f"m_in{r}") for r in range(2)]
        st_ready = sem("st_ready")
        exp_ready = sem("exp_ready")
        vt_ready = sem("vt_ready")
        vp_ready = sem("vp_ready")
        pv_ready = sem("pv_ready")
        os_ready = sem("os_ready")
        spread_made = sem("spread_made")
        gconst = sem("gconst")
        params_in = sem("params_in")
        results_in = sem("results_in")
        weights_in = sem("expert_weights_in")
        numden_out = [sem(f"numden_out{i}") for i in range(2)]

        block = ctx.enter_context(nc.Block())

        def steps(eng, body):
            with eng.Fori(0, STEPS // 2) as it:
                for p in range(2):
                    body(it * 2 + p, p)

        def groups(eng, body, lag, peeled=1):
            for G in range(peeled * ROUND):
                body(G // ROUND, G % ROUND)
            with eng.Fori(peeled, GROUPS // ROUND) as it:
                for g in range(ROUND):
                    body(it, g)
            for G in range(GROUPS, GROUPS + lag):
                body(G // ROUND, G % ROUND)

        def present(G, lag, total=GROUPS):
            return not isinstance(G, int) or 0 <= G - lag < total

        def unit_of(R, g, lag):
            return R * RING + (g - lag) // 2

        def pair_of(R, g, lag):
            return R * (RING // 2) + (g - lag) // 4

        def m_in_count(R, g, lag):
            return R * (32 * RING // 2) + 32 * ((g - lag) // 4 + 1)

        def s_at_least(s, n):
            return not isinstance(s, int) or s >= n

        def stores_before(s, p):
            return (s - p) * 40

        @block.sync
        def _(sp):
            xt = io["x"].rearrange("b (t p) d -> p (b t) d", p=P)
            for i in range(2):
                half = slice(i * TILES // 2, (i + 1) * TILES // 2)
                sp.dma_start(x_all[:, half, :], xt[:, half, :]).then_inc(x_in[i], 16)
            for n, name in enumerate(("Wq", "Wk", "Wv")):
                sp.dma_start(w_qkv[:, n, :], io[name]).then_inc(consts_in, 16)
            for n, name in enumerate(("bq", "bk", "bv")):
                sp.dma_start(b_qkv[:, n:n + 1], io[name].rearrange("(p o) -> p o", o=1)).then_inc(consts_in, 16)
            sp.dma_start(bo_all[:, :], io["bo"].rearrange("(o d) -> o d", o=1).broadcast_to([P, D])).then_inc(consts_in, 16)

            def store(s, p):
                at = bass.ds(s * STEP, STEP)
                for k, parts in enumerate((q_parts, k_parts)):
                    sp.wait_ge(lo_ready, 2 * s + k + 1)
                    src = parts_out[p][k][:, :, :].bitcast(F32)
                    sp.dma_start(parts[:, 0:2, at], src).then_inc(stored[p], 16)
                    sp.dma_start(parts[:, 2:4, at], src[:, ::-1, :] if k else src).then_inc(stored[p], 16)
                sp.wait_ge(v_ready, 4 * s + 4)
                sp.dma_start(v_rows[:, :, bass.ds(s * (STEP // 4), STEP // 4)],
                             v_out[p][:, :].rearrange("p (j t) -> p j t", j=4)).then_inc(stored[p], 16)

            def load(U, r, reuse):
                if reuse:
                    sp.wait_ge(st_ready, 4 * U - 4 * RING + 4)
                    sp.wait_ge(q_cleared, RING)
                    sp.wait_ge(vt_ready, 2 * U - 2 * RING + 2)
                at = bass.ds(U * P, P)
                for dst, src in ((qt[r], q_parts), (kt[r], k_parts)):
                    sp.dma_start(dst[0:PARTS, :, :].bitcast(F32).rearrange("d (c r) h -> d c (r h)", c=COLS),
                                 src[:, :, bass.ds(U * P, P)].rearrange("(c d) a t -> (d a) c t", d=HD)).then_inc(unit_in[r], 16)
                sp.dma_start(vs[r][0:PARTS, :, :].rearrange("d (c r) i -> d c (r i)", c=COLS),
                             v_rows[:, :, bass.ds(U * 32, 32)].rearrange("(c d) j t -> (d j) c t", d=HD)).then_inc(unit_in[r], 16)

            with sp.Fori(0, STEPS // 2 - 1) as it:
                for p in range(2):
                    store(it * 2 + p, p)
            sp.wait_ge(stored[0], 16 * 5)
            sp.wait_ge(q_cleared, RING)
            sp.wait_ge(k_cleared, 2 * RING)
            for r in range(2):
                load(r, r, False)
            store(STEPS - 2, 0)
            for r in range(2, RING):
                load(r, r, False)
            store(STEPS - 1, 1)

            def numden_store(K, p):
                sp.wait_ge(os_ready, 4 * K + 4)
                for j in range(4):
                    dst = numden[:, :, bass.ds(K * 2 * P + 64 * j, 64)].rearrange("c d t -> d c t")
                    sp.dma_start(dst, os_[p][32 * j:32 * j + 2 * HD, :, :]).then_inc(numden_out[p], 16)

            def group(R, g):
                G = R * ROUND + g
                if g % 4 == 0 and present(G, 12):
                    numden_store(pair_of(R, g, 12), (g - 12) // 4 % 2)
                if g % 2 == 0 and present(G, 0) and (not isinstance(G, int) or G >= ROUND):
                    if isinstance(G, int) and G == ROUND:
                        for p in range(2):
                            sp.wait_ge(stored[p], 16 * 5 * STEPS // 2)
                    load(unit_of(R, g, 0), g // 2, True)
                if isinstance(G, int) and G == ROUND + 1:
                    sp.dma_start(keep.wo_attn[:, :], io["Wo"]).then_inc(params_in, 16)
                    for n, name in enumerate(("gamma", "beta", "ln_g", "ln_b")):
                        sp.dma_start(keep.vecs[:, n, :], io[name].rearrange("(o d) -> o d", o=1).broadcast_to([P, D])).then_inc(params_in, 16)
                    sp.dma_start(keep.router[:, :], io["router_w"]).then_inc(params_in, 16)
                    sp.dma_start(keep.ln_b_col[:, :], io["ln_b"].rearrange("(d o) -> d o", o=1)).then_inc(params_in, 16)
                    sp.dma_start(keep.egb[:, 0, :], io["eg"].rearrange("e d -> d e"), allow_slow_non_contiguous=True).then_inc(params_in, 16)
                    sp.dma_start(keep.egb[:, 1, :], io["eb"].rearrange("e d -> d e"), allow_slow_non_contiguous=True).then_inc(params_in, 16)
                if g in (1, 3) and present(G, 0):
                    w, name = ((keep.w1, "W1"), (keep.w2, "W2"))[g // 2]
                    e = slice(R, R + 1) if isinstance(R, int) else bass.ds(R, 1)
                    sp.dma_start(w[:, e, :], io[name][e].rearrange("e d h -> d e h")).then_inc(weights_in, 16)
                if g % 2 == 0 and present(G, 4):
                    sp.wait_ge(ml_ready, unit_of(R, g, 4) + 1)
                    r = (g - 4) % ROUND // 2
                    for o in range(MAX_ROWS):
                        dst = qt[r][ZERO_TO + o:ZERO_TO + o + 1, :, :].bitcast(F32)
                        sp.dma_start(dst.rearrange("o (p a) h -> o p (a h)", a=2),
                                     mhl[r % 2][:, o].bitcast(F32).rearrange("p a h -> p (a h)")).then_inc(m_in[r % 2], 16)
                if isinstance(G, int) and G == GROUPS + 3:
                    for p in range(2):
                        sp.wait_ge(numden_out[p], 16 * 4 * (UNITS // 4 - 1))
                    load_results(0, BATCHES - 1)

            def load_results(b, n):
                sp.dma_start(keep.num[:, b * BTOK:(b + n) * BTOK], numden[:, 0:HD, b * BTOK:(b + n) * BTOK]).then_inc(results_in, 16)
                for c in range(b, b + n):
                    sp.dma_start(keep.den[:, c, :],
                                 numden[:, HD, c * BTOK:(c + 1) * BTOK].rearrange("c (g r) -> c g r", g=8)).then_inc(results_in, 16)

            groups(sp, group, 9, 2)
            for p in range(2):
                sp.wait_ge(numden_out[p], 16 * 4 * UNITS // 4)
            load_results(BATCHES - 1, 1)
            sp.wait_ge(params_in, 16 * 9)
            sp.wait_ge(weights_in, 16 * 2 * EXPERTS)
            sp.wait_ge(results_in, 16 * (BATCHES + 2))

        @block.gpsimd
        def _(pool):
            pool.memset(ident[:, :], 0.0).then_inc(ident_ready, 1)
            pool.wait_ge(ident_ready, 1)
            pool.affine_select(out=ident[:, :], in_=ident[:, :], compare_op=ALU.not_equal, fill=1.0, base=0,
                               pattern=[[-1, P]], channel_multiplier=1).then_inc(ident_ready, 1)
            for r in range(RING):
                pool.memset(qt[r][:, :, :].bitcast(F32), 0.0).then_inc(q_cleared, 1)
            for r in range(2):
                pool.memset(vt[r][:, :, :, :], 1.0).then_inc(v_cleared, 1)
            for r in range(RING):
                pool.memset(kt[r][:, :, :].bitcast(F32), 0.0).then_inc(k_cleared, 1)
            pool.wait_ge(v_cleared, 2)
            pool.wait_ge(q_cleared, RING)
            pool.wait_ge(k_cleared, RING)
            for r in range(RING):
                pool.memset(kt[r][ZERO_TO:P, :, :].bitcast(F32), 1.0).then_inc(k_cleared, 1)
            pool.wait_ge(k_cleared, 2 * RING)
            pool.wait_ge(consts_in, 7 * 16)

            def residual(s, p):
                for t in range(TPS):
                    pool.wait_ge(norm_ready, TPS * s + t + 1)
                    pool.tensor_tensor(u_all[:, bass.ds(TPS * s + t, 1), :].rearrange("p o d -> p (o d)"),
                                       u_step[p][:, t, :], bo_all[:, :], ALU.add).then_inc(ubo_ready, 1)

            steps(pool, residual)

            pool.memset(keep.spread[:, :, :], 0.0).then_inc(spread_made, 1)
            pool.wait_ge(spread_made, 1)
            pool.affine_select(out=keep.spread[:, :, :].rearrange("p g (c d) -> p g c d", d=HD),
                               in_=keep.spread[:, :, :].rearrange("p g (c d) -> p g c d", d=HD), compare_op=ALU.not_equal,
                               fill=1.0, base=0, pattern=[[-1, 8], [-8, COLS], [0, HD]], channel_multiplier=1).then_inc(spread_made, 1)
            for n, by_stage in enumerate(((1.0, 1.0, 1.0 + EPS, 1.0), (0.0, EPS, EPS * EPS, EPS), (1e-8, 0.0, 0.0, 0.0))):
                for stage, value in enumerate(by_stage):
                    pool.memset(keep.law[:, n, stage, :], value).then_inc(gconst, 1)
            pool.memset(keep.mv[:, :, :, :], 1.0).then_inc(gconst, 1)
            pool.memset(keep.zero[:, :], 0.0).then_inc(gconst, 1)
            pool.memset(keep.ones[:, :], 1.0).then_inc(gconst, 1)
            pool.memset(keep.den[:, BATCHES, :], 1.0).then_inc(gconst, 1)

            pool.memset(keep.tri[:, :], 1.0).then_inc(gconst, 1)
            pool.memset(keep.keep_on[:, :, :], 1.0).then_inc(gconst, 1)
            pool.wait_ge(gconst, 18)
            pool.affine_select(out=keep.tri[:, :], in_=keep.tri[:, :], compare_op=ALU.is_gt, fill=0.0, base=0,
                               pattern=[[1, P]], channel_multiplier=-1).then_inc(gconst, 1)
            pool.affine_select(out=keep.keep_on[:, :, :], in_=keep.keep_on[:, :, :], compare_op=ALU.is_gt, fill=0.0, base=0,
                               pattern=[[0, EXPERTS], [1, TILES]], channel_multiplier=0).then_inc(gconst, 1)

            def iota(dst, pattern, base, channel):
                pool.iota(dst, pattern, base=base, channel_multiplier=channel, allow_small_or_imprecise_dtypes=True).then_inc(gconst, 1)

            iota(keep.e_less[:, :], [[1, EXPERTS]], -EXPERTS, 0)
            iota(keep.tiles_i[:, :], [[1, SLOTS]], 0, 0)
            iota(keep.lanes_i[:, :], [[1, P]], 0, 0)
            iota(keep.chunk[:, :], [[P, TILES]], 0, 0)
            iota(keep.high[:, :], [[1, TILES]], 0, 0)
            iota(keep.low[:, :], [[1, 2]], 1, 2)
            iota(keep.dump_row[:, :], [[P, SLOTS]], DUMP + 1, 1)

        def numden_before(R, g):
            return R * 64 + 64 * ((g - LAG_OUT) // 8)

        @block.scalar
        def _(act):
            act.wait_ge(var_ready, 1)
            act.activation(dev[:, :], var[:, :], ACT.Sqrt).then_inc(dev_ready, 1)
            act.wait_ge(consts_in, 7 * 16)

            def turned(s, p):
                act.wait_ge(tp_ready, s + 1)
                if s_at_least(s, 2):
                    act.wait_ge(qkv_ready, 3 * s - 3)
                act.activation(ut[p][:, :].rearrange("p (t r h) -> p t h r", t=TPS, h=8),
                               ut_ps[p][:, :].rearrange("p (t h r) -> p t h r", t=TPS, h=8), ACT.Copy).then_inc(ut_ready, 1)

            def outputs(s, p):
                if s_at_least(s, 2):
                    act.wait_ge(stored[p], stores_before(s, p))
                for k in range(2):
                    act.wait_ge(qkv_ready, 3 * s + k + 1)
                    act.activation(parts_out[p][k][:, 0, :], qkv_ps[p][k], ACT.Identity, bias=b_qkv[:, k:k + 1])\
                        .then_inc(hi_ready, 1)
                act.wait_ge(qkv_ready, 3 * s + 3)
                for j in range(4):
                    act.activation(v_out[p][:, :].rearrange("p (j t r i) -> p j t r i", t=TPS, j=4, i=2)[:, j],
                                   qkv_ps[p][2].rearrange("p (t r i j) -> p j t r i", t=TPS, j=4, i=2)[:, j],
                                   ACT.Identity, bias=b_qkv[:, 2:3]).then_inc(v_ready, 1)

            turned(0, 0)
            turned(1, 1)
            outputs(0, 0)
            turned(2, 0)
            outputs(1, 1)
            turned(3, 1)
            outputs(2, 0)
            with act.Fori(2, STEPS // 2) as it:
                turned(it * 2, 0)
                outputs(it * 2 - 1, 1)
                turned(it * 2 + 1, 1)
                outputs(it * 2, 0)
            outputs(STEPS - 1, 1)

            def group(R, g):
                G = R * ROUND + g
                if present(G, LAG_OUT):
                    f = (g - LAG_OUT) % ROUND
                    act.wait_ge(pv_ready, G - LAG_OUT + 1)
                    if f % 4 == 0 and (not isinstance(G, int) or G - LAG_OUT >= 8):
                        act.wait_ge(numden_out[f // 4], numden_before(R, g))
                    at = (f % 4) * RPH
                    act.activation(os_[f // 4][:, :, at:at + RPH],
                                   pv_ps[:, 0:SEQ].rearrange("p (c r) -> p c r", r=RPH), ACT.Copy).then_inc(os_ready, 1)
                if present(G, LAG_T):
                    f = (g - LAG_T) % ROUND
                    for pair in range(2):
                        act.wait_ge(st_ready, 2 * (G - LAG_T) + pair + 1)
                        if not isinstance(G, int) or G - LAG_T >= 2:
                            act.wait_ge(pv_ready, G - LAG_T - 1)
                        if pair == 1:
                            act.wait_ge(vt_ready, G - LAG_T + 1)
                            act.activation(vt[f % 2][:, :, :, 0:HD], m_ps[:, 0:64].rearrange("p (a d j) -> p a j d", a=2, j=4),
                                           ACT.Copy).then_inc(vp_ready, 1)
                        act.activation(pt[(2 * f + pair) % 4][:, :], st_ps[pair][:, :, :].rearrange("p a b -> p (a b)"),
                                       ACT.Exp, scale=SCALE).then_inc(exp_ready, 1)

            act.wait_ge(v_cleared, 2)
            for p in range(2):
                act.wait_ge(stored[p], 16 * 5 * STEPS // 2)
            act.wait_ge(tp_ready, STEPS)
            act.wait_ge(ubo_ready, TILES)
            groups(act, group, LAG_OUT)

        @block.vector
        def _(dve):
            for i in range(2):
                dve.wait_ge(x_in[i], 16)
                with dve.Fori(i * TILES // 16, (i + 1) * TILES // 16) as it:
                    for t in range(8):
                        dve.bn_stats(bn[:, bass.ds(it * 8 + t, 1), :].rearrange("p o s -> p (o s)"),
                                     x_all[:, bass.ds(it * 8 + t, 1), :].rearrange("p o d -> p (o d)")).then_inc(stats_ready, 1)
            dve.wait_ge(stats_ready, TILES)
            dve.tensor_tensor(tmp[:, 0, :], bn[:, :, 1], bn[:, :, 4], ALU.add).then_inc(chain, 1)
            dve.tensor_tensor(tmp[:, 1, :], bn[:, :, 1], bn[:, :, 4], ALU.subtract).then_inc(chain, 1)
            dve.tensor_tensor(tmp[:, 2, :], bn[:, :, 2], bn[:, :, 5], ALU.add).then_inc(chain, 1)
            dve.wait_ge(chain, 3)
            dve.tensor_scalar(mean[:, :], tmp[:, 0, :], 0.5, None, ALU.mult).then_inc(chain, 1)
            dve.scalar_tensor_tensor(var[:, :], tmp[:, 1, :], 0.25, tmp[:, 1, :], ALU.mult, ALU.mult).then_inc(chain, 1)
            dve.tensor_scalar(tmp[:, 3, :], tmp[:, 2, :], 1.0 / D, 1e-5, ALU.mult, ALU.add).then_inc(chain, 1)
            dve.wait_ge(chain, 6)
            dve.tensor_tensor(var[:, :], var[:, :], tmp[:, 3, :], ALU.add).then_inc(var_ready, 1)
            dve.wait_ge(dev_ready, 1)
            dve.reciprocal(rstd[:, :], dev[:, :]).then_inc(rstd_ready, 1)
            dve.wait_ge(rstd_ready, 1)

            def normalise(s, p):
                if s_at_least(s, 2):
                    dve.wait_ge(tp_ready, s - 1)
                    dve.wait_ge(ubo_ready, TPS * s - TPS)
                for t in range(TPS):
                    at = bass.ds(TPS * s + t, 1)
                    dve.tensor_scalar(u_step[p][:, t, :], x_all[:, at, :].rearrange("p o d -> p (o d)"), mean[:, at], rstd[:, at],
                                      ALU.subtract, ALU.mult).then_inc(norm_ready, 1)

            def low_parts(s, p):
                if s_at_least(s, 2):
                    dve.wait_ge(stored[p], stores_before(s, p))
                for k in range(2):
                    dve.wait_ge(hi_ready, 2 * s + k + 1)
                    dve.scalar_tensor_tensor(parts_out[p][k][:, 1, :], qkv_ps[p][k], b_qkv[:, k:k + 1],
                                             parts_out[p][k][:, 0, :].bitcast(F32), ALU.add, ALU.subtract).then_inc(lo_ready, 1)

            dve.wait_ge(consts_in, 7 * 16)
            normalise(0, 0)
            normalise(1, 1)
            normalise(2, 0)
            low_parts(0, 0)
            normalise(3, 1)
            low_parts(1, 1)
            with dve.Fori(2, STEPS // 2) as it:
                normalise(it * 2, 0)
                low_parts(it * 2 - 2, 0)
                normalise(it * 2 + 1, 1)
                low_parts(it * 2 - 1, 1)
            low_parts(STEPS - 2, 0)
            low_parts(STEPS - 1, 1)

            def group(R, g):
                G = R * ROUND + g
                m = g // 2 % 2
                if g % 2 == 0 and (not isinstance(G, int) or G >= 4):
                    dve.wait_ge(ml_ready, unit_of(R, g, 2))
                for j in range(4):
                    dve.wait_ge(s_ready, 4 * G + j + 1)
                    dve.tensor_reduce(mx[m][:, :, 4 * (g % 2) + j], s_ps[j % 2][:, :].rearrange("p (a k) -> p a k", a=2),
                                      AX.X, ALU.max).then_inc(max_ready, 1)
                if g % 2 == 1:
                    dve.wait_ge(max_ready, 4 * G + 4)
                    if not isinstance(G, int) or G >= 4:
                        dve.wait_ge(m_in[m], m_in_count(R, g, 4))
                    high, low = mhl[m][:, 0], mhl[m][:, 1]
                    dve.tensor_scalar(high, mx[m][:, :, :], -1.0, None, ALU.mult).then_inc(mh_ready, 1)
                    dve.wait_ge(mh_ready, unit_of(R, g, 0) + 1)
                    dve.scalar_tensor_tensor(low, mx[m][:, :, :], -1.0, high.bitcast(F32),
                                             ALU.mult, ALU.subtract).then_inc(ml_ready, 1)

            groups(dve, group, 0)

        @block.tensor
        def _(pe):
            pe.wait_ge(ident_ready, 2)
            pe.wait_ge(consts_in, 7 * 16)

            def transposes(s, p):
                if s_at_least(s, 2):
                    pe.wait_ge(ut_ready, s - 1)
                for t in range(TPS):
                    pe.wait_ge(norm_ready, TPS * s + t + 1)
                    mm = pe.transpose(ut_ps[p][:, t * P:(t + 1) * P], u_step[p][:, t, :], ident[:, :])
                mm.then_inc(tp_ready, 1)

            def project(s, p):
                pe.wait_ge(ut_ready, s + 1)
                for k in range(3):
                    if s_at_least(s, 2):
                        if k < 2:
                            pe.wait_ge(lo_ready, 2 * s + k - 3)
                        else:
                            pe.wait_ge(v_ready, 4 * s - 4)
                    pe.matmul(qkv_ps[p][k], w_qkv[:, k, :], ut[p][:, :], start=True, stop=True).then_inc(qkv_ready, 1)

            transposes(0, 0)
            transposes(1, 1)
            project(0, 0)
            transposes(2, 0)
            project(1, 1)
            transposes(3, 1)
            project(2, 0)
            with pe.Fori(2, STEPS // 2) as it:
                transposes(it * 2, 0)
                project(it * 2 - 1, 1)
                transposes(it * 2 + 1, 1)
                project(it * 2, 0)
            project(STEPS - 1, 1)

            pe.wait_ge(lo_ready, 2 * STEPS)
            pe.wait_ge(v_ready, 4 * STEPS)

            def scores(R, G, g, j):
                r = g // 2 % RING
                if j == 0 and g % 2 == 0:
                    pe.wait_ge(unit_in[r], unit_count(R, g))
                if not isinstance(G, int) or 4 * G + j >= 2:
                    pe.wait_ge(max_ready, 4 * G + j - 1)
                for a in range(2):
                    mm = pe.matmul(s_ps[j % 2][:, a * SEQ:(a + 1) * SEQ],
                                   qt[r][0:ZERO_TO, a::2, 4 * (g % 2) + j],
                                   kt[r][0:ZERO_TO, :, 4 * (g % 2) + j], start=True, stop=True)
                mm.then_inc(s_ready, 1)

            def scores_t(R, G, g, j):
                f = (g - LAG_T) % ROUND
                r = f // 2
                if j == 0 and f % 2 == 0:
                    pe.wait_ge(m_in[r % 2], m_in_count(R, g, LAG_T))
                n = 2 * (G - LAG_T) + j // 2
                if j % 2 == 0 and (not isinstance(G, int) or n >= 2):
                    pe.wait_ge(exp_ready, n - 1)
                for a in range(2):
                    mm = pe.matmul(st_ps[j // 2][:, j % 2, a * SEQ:(a + 1) * SEQ],
                                   kt[r][0:ZERO_TO + MAX_ROWS, a::2, 4 * (f % 2) + j],
                                   qt[r][0:ZERO_TO + MAX_ROWS, :, 4 * (f % 2) + j], start=True, stop=True)
                if j % 2 == 1:
                    mm.then_inc(st_ready, 1)

            def values(g):
                f = (g - LAG_T) % ROUND
                for a in range(2):
                    mm = pe.transpose(m_ps[:, a * 32:(a + 1) * 32], vs[f // 2][0:PARTS, a::2, f % 2], ident[0:PARTS, 0:PARTS])
                mm.then_inc(vt_ready, 1)

            def weigh(G, g, a):
                f = (g - LAG_PV) % ROUND
                if a == 0:
                    pe.wait_ge(exp_ready, 2 * (G - LAG_PV) + 2)
                    pe.wait_ge(vp_ready, G - LAG_PV + 1)
                    if not isinstance(G, int) or G - LAG_PV >= 1:
                        pe.wait_ge(os_ready, G - LAG_PV)
                for j in range(4):
                    mm = pe.matmul(pv_ps[32 * j:32 * j + 32, 0:SEQ], vt[f % 2][:, a, j, :],
                                   pt[(2 * f + j // 2) % 4][:, (2 * (j % 2) + a) * SEQ:(2 * (j % 2) + a + 1) * SEQ],
                                   start=(a == 0), stop=(a == 1))
                if a == 1:
                    mm.then_inc(pv_ready, 1)

            def group(R, g):
                G = R * ROUND + g
                for j in range(4):
                    if j == 3 and present(G, LAG_T + 1):
                        pe.wait_ge(vp_ready, G - LAG_T)
                    if present(G, 0):
                        scores(R, G, g, j)
                    if j == 3 and present(G, LAG_T):
                        values(g)
                    if present(G, LAG_T):
                        scores_t(R, G, g, j)
                    if j in (1, 3) and present(G, LAG_PV):
                        weigh(G, g, j // 2)

            def unit_count(R, g):
                return R * 48 + 48

            groups(pe, group, LAG_PV)



EXPERTS, HID = 8, 512
CHUNKS = HID // P
SLOTS = 2 * TOK // P + EXPERTS
DUMP = 2 * TOK
FROUND = 8
MAX_LAG = 5

BATCHES = 8
BT = TILES // BATCHES
BTOK = BT * P
EPS = 1e-5


def routing(nc, io, keep):
    K = keep
    wo, vecs, router, ln_b_col, egb, den, num, zero = K.wo_attn, K.vecs, K.router, K.ln_b_col, K.egb, K.den, K.num, K.zero
    spread, law, mv, ones, tri, keep_on, e_less = K.spread, K.law, K.mv, K.ones, K.tri, K.keep_on, K.e_less
    tiles_i, lanes_i, chunk, high, low, dump_row = K.tiles_i, K.lanes_i, K.chunk, K.high, K.low, K.dump_row
    with ExitStack() as ctx:
        def sb(name, shape, dt=F32):
            return ctx.enter_context(nc.sbuf_tensor(name, shape, dt))

        def ps(name, shape):
            return ctx.enter_context(nc.psum_tensor(name, shape, F32))

        def sem(name):
            return ctx.enter_context(nc.semaphore(name))

        ot = [sb(f"ot{p}", [P, BTOK]) for p in range(2)]
        y = [sb(f"y{p}", [P, BT, D]) for p in range(2)]
        a = [sb(f"a{p}", [P, BT, D]) for p in range(2)]
        xf = [sb(f"xf{p}", [P, BT, D]) for p in range(2)]
        z = sb("z", [P, TILES, D])
        xft = sb("xft", [P, BTOK])
        bn = sb("bn2", [P, 4, BT, 6])
        arg = sb("arg", [P, 4, BT])
        dev = sb("dev2", [P, 4, BT])
        sc = [sb(f"sc{p}", [P, 2, 4, BT]) for p in range(2)]
        logits = sb("logits", [P, TILES, EXPERTS])
        shift = sb("shift", [P, P])
        sel = sb("sel", [P, 3, TILES, EXPERTS])
        work = sb("work", [P, 8, TILES, EXPERTS])
        few = sb("few", [P, 8, TILES])
        place_f = sb("place_f", [P, 2, TILES])
        place_i = sb("place_i", [P, 2, TILES], I32)
        part_i = sb("part_i", [P, 2, 2, TILES], I32)
        lane = sb("lane", [P, 2, TILES])
        tile = sb("tile", [P, 2, TILES])
        start_t = sb("start_t", [P, 2, TILES])
        ex = sb("ex", [P, 4, EXPERTS])
        tex = sb("tex", [P, SLOTS, EXPERTS])
        e_of = sb("e_of", [P, SLOTS])
        digits = num[:, :].bitcast(BF16)
        at_lane = [digits[:, p * 8 * P:(p + 1) * 8 * P].rearrange("p (t l) -> p t l", t=8) for p in range(4)]
        at_tile = [digits[:, (32 * P + p * 24 * SLOTS):(32 * P + (p + 1) * 24 * SLOTS)].rearrange("p (n t i) -> p n t i", n=3, t=8)
                   for p in range(2)]
        row_f = sb("row_f", [P, 4, SLOTS])
        row_i = sb("row_i", [P, SLOTS], I32)

        rb_ps = ps("rb_ps", [P, BTOK])
        y_ps = ps("y_ps", [P, BT, D])
        t_ps = ps("t_ps", [P, BTOK])
        lg_ps = ps("lg_ps", [P, BT, EXPERTS])
        cp = ps("cp", [P, 2, TILES * EXPERTS])
        fold_ps = [ps(f"fold_ps{n}", [P, HID]) for n in range(2)]
        tab_ps = ps("tab_ps", [P, 2, SLOTS])

        weights_in = sem("weights_in")
        biases_in = sem("biases_in")
        rows_out = sem("rows_out")
        recip_ready = sem("recip_ready")
        rb_ready = sem("rb_ready")
        ot_ready = sem("ot_ready")
        yp_ready = sem("yp_ready")
        y_ready = sem("y_ready")
        bn_ready = sem("bn_ready")
        mv_ready = sem("mv_ready")
        arg_ready = sem("arg_ready")
        var_ready = sem("var_ready")
        dev_ready = sem("dev_ready")
        dev_added = sem("dev_added")
        inv_ready = sem("inv_ready")
        scales = sem("scales")
        n1_ready = sem("n1_ready")
        a_scaled = sem("a_scaled")
        a_ready = sem("a_ready")
        h_ready = sem("h_ready")
        n3_ready = sem("n3_ready")
        xf_scaled = sem("xf_scaled")
        xf_ready = sem("xf_ready")
        xt_done = sem("xt_done")
        xft_ready = sem("xft_ready")
        lg_done = sem("lg_done")
        lg_ready = sem("lg_ready")
        z_ready = sem("z_ready")
        z_out = sem("z_out")
        shift_ready = sem("shift_ready")
        bias_done = sem("bias_done")
        bias_ready = sem("bias_ready")
        folded = sem("folded")
        dchain = sem("dchain")
        sel_ready = sem("sel_ready")
        cp_ready = sem("cp_ready")
        diff_ready = sem("diff_ready")
        exp_done = sem("exp_done")
        places_ready = sem("places_ready")
        lanes_made = [sem(f"lanes_made{p}") for p in range(2)]
        tiles_made = sem("tiles_made")
        low_made = sem("low_made")
        put = sem("put")

        block = ctx.enter_context(nc.Block())
        PEELED = 4
        STAGE_LAG = (0, 1, 2, 4)

        def slots(eng, body):
            for s in range(PEELED):
                body(s, s % 2)
            with eng.Fori(PEELED // 2, BATCHES // 2) as it:
                for p in range(2):
                    body(it * 2 + p, p)
            for s in range(BATCHES, BATCHES + 4):
                body(s, s % 2)

        def present(s, lag):
            return not isinstance(s, int) or 0 <= s - lag < BATCHES

        def late(s, n):
            return not isinstance(s, int) or s >= n

        def tiles_of(b):
            return bass.ds(b * BT, BT)

        @block.sync
        def _(sp):
            for dst, name in ((K.b1, "b1"), (K.b2, "b2")):
                sp.dma_start(dst[:, :, :], io[name].rearrange("(o e) h -> o e h", o=1).broadcast_to(dst.shape)).then_inc(biases_in, 16)
            sp.dma_start(K.wo[:, :, :, :], io["eWo"].rearrange("e (c p) d -> p e c d", p=P)).then_inc(weights_in, 16)
            sp.dma_start(K.bo[:, :, :], io["ebo"].rearrange("(o e) h -> o e h", o=1).broadcast_to(K.bo.shape)).then_inc(weights_in, 16)

            sp.dma_start(K.z_rows[TOK:TOK + 1, :], zero[:, :]).then_inc(rows_out, 16)

            def store(s, p):
                if present(s, 4):
                    b = s - 4
                    sp.wait_ge(z_ready, 4 * b + 4)
                    sp.dma_start(K.z_rows[0:TOK, :].rearrange("(t p) d -> p t d", p=P)[:, tiles_of(b), :],
                                 z[:, tiles_of(b), :]).then_inc(z_out, 16)

            slots(sp, store)
            sp.wait_ge(rows_out, 16)
            sp.wait_ge(z_out, 16 * BATCHES)
            sp.wait_ge(weights_in, 16 * 2)

        @block.gpsimd
        def _(pool):
            def slot(s, p):
                if present(s, 0):
                    pool.wait_ge(n1_ready, 4 * s + 4)
                    pool.tensor_tensor(a[p][:, :, :], a[p][:, :, :], vecs[:, 0:1, :].broadcast_to([P, BT, D]), ALU.mult).then_inc(a_scaled, 1)
                    pool.wait_ge(a_scaled, s + 1)
                    pool.tensor_tensor(a[p][:, :, :], a[p][:, :, :], vecs[:, 1:2, :].broadcast_to([P, BT, D]), ALU.add).then_inc(a_ready, 1)
                if present(s, 2):
                    b = s - 2
                    pool.wait_ge(n3_ready, 4 * b + 4)
                    pool.tensor_tensor(xf[p][:, :, :], xf[p][:, :, :], vecs[:, 2:3, :].broadcast_to([P, BT, D]), ALU.mult).then_inc(xf_scaled, 1)
                    pool.wait_ge(xf_scaled, b + 1)
                    pool.tensor_tensor(z[:, tiles_of(b), :], xf[p][:, :, :], vecs[:, 3:4, :].broadcast_to([P, BT, D]), ALU.add).then_inc(xf_ready, 1)

            slots(pool, slot)

            for n in range(1, 8, 2):
                if n == 1:
                    pool.wait_ge(places_ready, 2)
                k, t = n // 4, n % 4 * 8
                if n >= 5:
                    pool.wait_ge(put, n - 3)
                for i in range(8):
                    pool.tensor_scalar(at_lane[n % 4][:, i, :], lanes_i[:, :], lane[:, k, t + i:t + i + 1], None,
                                       ALU.is_equal).then_inc(lanes_made[1], 1)

        @block.scalar
        def _(act):
            def slot(s, p):
                if present(s, 3):
                    b = s - 3
                    act.wait_ge(xt_done, b + 1)
                    if late(s, 4):
                        act.wait_ge(lg_done, b)
                    act.activation(xft[:, :], t_ps[:, :], ACT.Identity, bias=ln_b_col[:, :]).then_inc(xft_ready, 1)
                act.wait_ge(var_ready, s + 1)
                act.activation(dev[:, :, :], arg[:, :, :], ACT.Sqrt).then_inc(dev_ready, 1)
                act.wait_ge(scales, s + 1)
                if present(s, 0):
                    if late(s, 2):
                        act.wait_ge(h_ready, 4 * s - 4)
                    for t in range(BT):
                        act.activation(a[p][:, t, :], y[p][:, t, :], ACT.Identity, scale=sc[p][:, 0, 0, t:t + 1],
                                       bias=sc[p][:, 1, 0, t:t + 1]).then_inc(n1_ready, 1)
                if present(s, 2):
                    b = s - 2
                    if late(s, 4):
                        act.wait_ge(xf_ready, s - 3)
                        act.wait_ge(xt_done, s - 3)
                    for t in range(BT):
                        act.activation(xf[p][:, t, :], K.x_all[:, bass.ds(b * BT + t, 1), :].rearrange("p o d -> p (o d)"),
                                       ACT.Identity, scale=sc[p][:, 0, 2, t:t + 1], bias=sc[p][:, 1, 2, t:t + 1]).then_inc(n3_ready, 1)
                if present(s, 4):
                    for t in range(BT):
                        row = z[:, bass.ds((s - 4) * BT + t, 1), :].rearrange("p o d -> p (o d)")
                        act.activation(row, row, ACT.Identity, scale=sc[p][:, 0, 3, t:t + 1],
                                       bias=sc[p][:, 1, 3, t:t + 1]).then_inc(z_ready, 1)
                if present(s, 2):
                    if late(s, 3):
                        act.wait_ge(bias_done, 2 * s - 4)
                    act.activation(shift[:, :], ones[:, :], ACT.Identity, scale=egb[:, 1, bass.ds(s - 2, 1)]).then_inc(shift_ready, 1)

            slots(act, slot)
            act.wait_ge(bias_done, 2 * EXPERTS)
            with act.Fori(0, EXPERTS) as e:
                for w in (K.w1, K.w2):
                    we = w[:, bass.ds(e, 1), :].rearrange("p o h -> p (o h)")
                    act.activation(we, we, ACT.Copy, scale=egb[:, 0, bass.ds(e, 1)]).then_inc(folded, 1)
            for n in range(8):
                act.wait_ge(tiles_made, 2 * n + 1)
                if n >= 2:
                    act.wait_ge(put, n - 1)
                act.activation(at_tile[n % 2][:, 2], at_tile[n % 2][:, 0], ACT.Copy, scale=low[:, n // 4:n // 4 + 1]).then_inc(low_made, 1)
            act.wait_ge(diff_ready, 1)
            act.activation(few[:, 3, :], few[:, 2, :], ACT.Exp).then_inc(exp_done, 1)

        @block.tensor
        def _(pe):
            def broadcast(b):
                for g in range(8):
                    mm = pe.matmul(rb_ps[:, g * (BTOK // 8):(g + 1) * (BTOK // 8)], spread[:, g, :],
                                   den[:, bass.ds(b, 1), :].rearrange("p o r -> p (o r)"), start=True, stop=True)
                mm.then_inc(rb_ready, 1)

            def slot(s, p):
                if present(s, 0):
                    if not late(s, 1):
                        pe.wait_ge(recip_ready, 1)
                        broadcast(s)
                    pe.wait_ge(ot_ready, 2 * s + 2)
                    if late(s, 1):
                        pe.wait_ge(y_ready, s)
                    for t in range(BT):
                        mm = pe.matmul(y_ps[:, t, :], ot[p][:, t * P:(t + 1) * P], wo[:, :], start=True, stop=True)
                    mm.then_inc(yp_ready, 1)
                    if not late(s, 1):
                        pe.wait_ge(recip_ready, 2)
                    broadcast(s + 1)
                if present(s, 3):
                    b = s - 3
                    pe.wait_ge(xf_scaled, b + 1)
                    if late(s, 4):
                        pe.wait_ge(xft_ready, b)
                    for t in range(BT):
                        mm = pe.transpose(t_ps[:, t * P:(t + 1) * P], xf[1 - p][:, t, :], K.ident[:, :])
                    mm.then_inc(xt_done, 1)
                    pe.wait_ge(xft_ready, b + 1)
                    if late(s, 4):
                        pe.wait_ge(lg_ready, b)
                    for t in range(BT):
                        mm = pe.matmul(lg_ps[:, t, :], xft[:, t * P:(t + 1) * P], router[:, :], start=True, stop=True)
                    mm.then_inc(lg_done, 1)
                    pe.wait_ge(shift_ready, b + 1)
                    for n, w in enumerate((K.w1, K.w2)):
                        if late(s, 4):
                            pe.wait_ge(bias_ready, 2 * b + n - 1)
                        pe.matmul(fold_ps[n][:, :], shift[:, :], w[:, bass.ds(b, 1), :].rearrange("p o h -> p (o h)"),
                                  start=True, stop=True).then_inc(bias_done, 1)

            slots(pe, slot)
            pe.wait_ge(sel_ready, 1)
            chosen = sel[:, 2, :, :].rearrange("p t e -> p (t e)")
            pe.matmul(cp[:, 0, :], tri[:, :], chosen, start=True, stop=True)
            pe.matmul(cp[:, 1, :], ones[:, :], chosen, start=True, stop=True, skip_group_check=True).then_inc(cp_ready, 1)
            for n in range(8):
                pe.wait_ge(lanes_made[n % 2], (n // 2 + 1) * (8 if n % 2 else 1))
                pe.wait_ge(tiles_made, 2 * n + 2)
                pe.wait_ge(low_made, n + 1)
                for t in range(8):
                    mm = pe.matmul(tab_ps[:, :, :], at_lane[n % 4][:, t, :], at_tile[n % 2][:, 1:3, t, :],
                                   start=(n == 0 and t == 0), stop=(n == 7 and t == 7))
                mm.then_inc(put, 1)

        @block.vector
        def _(dve):
            count = [0]

            def settled(*made):
                for ins in made:
                    ins.then_inc(dchain, 1)
                    count[0] += 1
                dve.wait_ge(dchain, count[0])

            def moments(stage, rows):
                for t in range(BT):
                    dve.bn_stats(bn[:, stage, t, :], rows(t)).then_inc(bn_ready, 1)

            dve.reciprocal(den[:, 0, :], den[:, 0, :]).then_inc(recip_ready, 1)
            dve.reciprocal(den[:, 1:BATCHES, :], den[:, 1:BATCHES, :]).then_inc(recip_ready, 1)

            def keep_logits(b):
                dve.wait_ge(lg_done, b + 1)
                dve.tensor_copy(logits[:, tiles_of(b), :], lg_ps[:, :, :]).then_inc(lg_ready, 1)

            def slot(s, p):
                if present(s, 0):
                    dve.wait_ge(rb_ready, s + 1)
                    if late(s, 2):
                        dve.wait_ge(yp_ready, s - 1)
                    for n in range(2):
                        half = slice(n * 2 * P, (n + 1) * 2 * P)
                        ins = [v.rearrange("p (j u r) -> p u j r", j=4, u=4)
                               for v in (num[:, bass.ds(s * BTOK + n * 2 * P, 2 * P)], rb_ps[:, half])]
                        dve.tensor_tensor(ot[p][:, half].rearrange("p (u j r) -> p u j r", u=4, j=4), *ins, ALU.mult).then_inc(ot_ready, 1)
                if isinstance(s, int) and s == PEELED - 1:
                    dve.wait_ge(biases_in, 16 * 2)
                if present(s, 4):
                    keep_logits(s - 4)
                if present(s, 2):
                    b = s - 2
                    dve.wait_ge(h_ready, 4 * b + 4)
                    dve.nop(nofuse=True)
                    moments(2, lambda t: K.x_all[:, bass.ds(b * BT + t, 1), :].rearrange("p o d -> p (o d)"))
                if present(s, 4):
                    dve.wait_ge(xf_ready, s - 3)
                    dve.nop(nofuse=True)
                    moments(3, lambda t: z[:, bass.ds((s - 4) * BT + t, 1), :].rearrange("p o d -> p (o d)"))
                if present(s, 4):
                    for n, dst in enumerate((K.b1, K.b2)):
                        dve.wait_ge(bias_done, 2 * (s - 4) + n + 1)
                        be = dst[:, bass.ds(s - 4, 1), :].rearrange("p o h -> p (o h)")
                        dve.tensor_tensor(be, be, fold_ps[n][:, :], ALU.add).then_inc(bias_ready, 1)
                if present(s, 0):
                    dve.wait_ge(yp_ready, s + 1)
                    if late(s, 2):
                        dve.wait_ge(n1_ready, 4 * s - 4)
                    dve.tensor_tensor(y[p][:, :, :], y_ps[:, :, :], K.u_all[:, tiles_of(s), :], ALU.add).then_inc(y_ready, 1)
                    dve.wait_ge(y_ready, s + 1)
                    moments(0, lambda t: y[p][:, t, :])
                if present(s, 1):
                    dve.wait_ge(a_ready, s)
                    moments(1, lambda t: a[1 - p][:, t, :])
                dve.wait_ge(bn_ready, stats(s))
                dve.nop(nofuse=True)
                for stage in range(4):
                    if present(s, STAGE_LAG[stage]):
                        for t in range(BT):
                            dve.bn_aggr(mv[:, stage, t, :], bn[:, stage, t, :]).then_inc(mv_ready, 1)
                dve.wait_ge(mv_ready, stats(s))
                if late(s, 1):
                    dve.wait_ge(dev_ready, s)
                dve.tensor_tensor(arg[:, :, :], mv[:, :, :, 1], law[:, 0, :, :], ALU.mult).then_inc(arg_ready, 1)
                dve.wait_ge(arg_ready, s + 1)
                dve.tensor_tensor(arg[:, :, :], arg[:, :, :], law[:, 1, :, :], ALU.add).then_inc(var_ready, 1)
                dve.wait_ge(dev_ready, s + 1)
                dve.tensor_tensor(dev[:, :, :], dev[:, :, :], law[:, 2, :, :], ALU.add).then_inc(dev_added, 1)
                dve.wait_ge(dev_added, s + 1)
                if late(s, 2):
                    dve.wait_ge(h_ready, h_before(s))
                    dve.wait_ge(n1_ready, 4 * min(s - 1, BATCHES) if isinstance(s, int) else 4 * s - 4)
                if isinstance(s, int) and s >= 6:
                    dve.wait_ge(n3_ready, 4 * min(s - 3, BATCHES))
                    dve.wait_ge(z_ready, 4 * (s - 5))
                dve.reciprocal(sc[p][:, 0, :, :], dev[:, :, :]).then_inc(inv_ready, 1)
                dve.wait_ge(inv_ready, s + 1)
                dve.scalar_tensor_tensor(sc[p][:, 1, :, :], mv[:, :, :, 0], -1.0, sc[p][:, 0, :, :], ALU.mult, ALU.mult).then_inc(scales, 1)
                dve.wait_ge(scales, s + 1)
                if present(s, 1):
                    for t in range(BT):
                        row = K.x_all[:, bass.ds((s - 1) * BT + t, 1), :].rearrange("p o d -> p (o d)")
                        dve.scalar_tensor_tensor(row, a[1 - p][:, t, :], sc[p][:, 0, 1, t:t + 1], row, ALU.mult, ALU.add).then_inc(h_ready, 1)
                    dve.tensor_copy(K.left_out[:, tiles_of(s - 1)], sc[p][:, 1, 1, :]).then_inc(dchain, 1)

            def stats(s):
                if isinstance(s, int):
                    return 4 * sum(max(0, min(s - lag + 1, BATCHES)) for lag in STAGE_LAG)
                return s * 16 - 12

            def h_before(s):
                return 4 * min(s - 2, BATCHES) if isinstance(s, int) else 4 * s - 8

            slots(dve, slot)
            count[0] += BATCHES

            wide = [P, TILES, EXPERTS]

            def per_token(v):
                return v.rearrange("p (t o) -> p t o", o=1).broadcast_to(wide)

            def per_expert(v, n=TILES):
                return v.rearrange("p (o e) -> p o e", o=1).broadcast_to([P, n, EXPERTS])

            dve.wait_ge(lg_ready, BATCHES)
            for k in range(2):
                src = logits[:, :, :] if k == 0 else work[:, 2, :, :]
                settled(dve.tensor_reduce(few[:, k, :], src, AX.X, ALU.max))
                settled(dve.tensor_tensor(work[:, 0, :, :], src, per_token(few[:, k, :]), ALU.is_equal))
                settled(dve.tensor_tensor(work[:, 1, :, :], work[:, 0, :, :], per_expert(e_less[:, :]), ALU.mult))
                settled(dve.tensor_reduce(few[:, 4 + k, :], work[:, 1, :, :], AX.X, ALU.min))
                settled(dve.tensor_tensor(sel[:, k, :, :], per_expert(e_less[:, :]), per_token(few[:, 4 + k, :]), ALU.is_equal))
                if k == 0:
                    settled(dve.scalar_tensor_tensor(work[:, 2, :, :], sel[:, 0, :, :], -3e38, logits[:, :, :], ALU.mult, ALU.add))
            dve.tensor_tensor(sel[:, 2, :, :], sel[:, 0, :, :], sel[:, 1, :, :], ALU.add).then_inc(sel_ready, 1)
            dve.tensor_tensor(few[:, 2, :], few[:, 1, :], few[:, 0, :], ALU.subtract).then_inc(diff_ready, 1)
            dve.wait_ge(cp_ready, 1)
            total = work[:, 4, :, :].rearrange("p a b -> p (a b)").rearrange("p (e t) -> p e t", e=EXPERTS)
            upto = work[:, 5, :, :].rearrange("p a b -> p (a b)").rearrange("p (e t) -> p e t", e=EXPERTS)
            settled(dve.tensor_copy(total, cp[:, 1, :].rearrange("p (t e) -> p e t", t=TILES)))
            settled(dve.tensor_tensor_scan(upto.rearrange("p e t -> p (e t)"), keep_on[:, :, :].rearrange("p e t -> p (e t)"),
                                           total.rearrange("p e t -> p (e t)"), 0.0, ALU.mult, ALU.add))
            count_e, tiles_e, ends_e, first_e = (ex[:, n, :] for n in range(4))
            filled = work[:, 7, :, :].rearrange("p a b -> p (a b)").rearrange("p (e t) -> p e t", e=EXPERTS)
            settled(dve.tensor_copy(count_e, upto[:, :, TILES - 1]))
            settled(dve.tensor_tensor(filled, count_e.rearrange("p (e o) -> p e o", o=1).broadcast_to([P, EXPERTS, TILES]),
                                      chunk[:, :].rearrange("p (o t) -> p o t", o=1).broadcast_to([P, EXPERTS, TILES]), ALU.is_gt),
                    dve.tensor_tensor(upto, upto, total, ALU.subtract))
            place = work[:, 6, :, :]
            settled(dve.tensor_reduce(tiles_e, filled, AX.X, ALU.add),
                    dve.tensor_tensor(place, cp[:, 0, :].rearrange("p (t e) -> p t e", t=TILES),
                                      upto.rearrange("p e t -> p t e"), ALU.add))
            settled(dve.tensor_tensor_scan(ends_e, ones[:, 0:EXPERTS], tiles_e, 0.0, ALU.mult, ALU.add),
                    *[dve.tensor_tensor(work[:, k, :, :], place, sel[:, k, :, :], ALU.mult) for k in range(2)])
            settled(dve.tensor_tensor(first_e, ends_e, tiles_e, ALU.subtract),
                    *[dve.tensor_reduce(place_f[:, k, :], work[:, k, :, :], AX.X, ALU.add) for k in range(2)])
            settled(dve.tensor_copy(place_i[:, :, :], place_f[:, :, :]),
                    *[dve.tensor_tensor(work[:, 2 + k, :, :], sel[:, k, :, :], per_expert(first_e), ALU.mult) for k in range(2)])
            settled(dve.tensor_scalar(part_i[:, 0, :, :], place_i[:, :, :], P - 1, None, ALU.bitwise_and),
                    dve.tensor_scalar(part_i[:, 1, :, :], place_i[:, :, :], 7, None, ALU.arith_shift_right))
            dve.tensor_copy(lane[:, :, :], part_i[:, 0, :, :]).then_inc(places_ready, 1)
            settled(dve.tensor_copy(place_f[:, :, :], part_i[:, 1, :, :]),
                    *[dve.tensor_reduce(start_t[:, k, :], work[:, 2 + k, :, :], AX.X, ALU.add) for k in range(2)])
            dve.tensor_tensor(tile[:, :, :], place_f[:, :, :], start_t[:, :, :], ALU.add).then_inc(places_ready, 1)
            dve.wait_ge(places_ready, 2)
            for n in range(8):
                k, t = n // 4, n % 4 * 8
                shape = [P, 8, SLOTS]
                if n >= 2:
                    dve.wait_ge(put, n - 1)
                dve.tensor_tensor(at_tile[n % 2][:, 0], tile[:, k, t:t + 8].rearrange("p (t o) -> p t o", o=1).broadcast_to(shape),
                                  tiles_i[:, :].rearrange("p (o i) -> p o i", o=1).broadcast_to(shape), ALU.is_equal).then_inc(tiles_made, 1)
                if n % 2 == 0:
                    dve.tensor_tensor(at_lane[n % 4][:, :, :],
                                      lane[:, k, t:t + 8].rearrange("p (t o) -> p t o", o=1).broadcast_to([P, 8, P]),
                                      lanes_i[:, :].rearrange("p (o l) -> p o l", o=1).broadcast_to([P, 8, P]), ALU.is_equal).then_inc(lanes_made[0], 1)
                dve.wait_ge(tiles_made, 2 * n + 1)
                dve.tensor_tensor(at_tile[n % 2][:, 1], at_tile[n % 2][:, 0],
                                  high[:, t:t + 8].rearrange("p (t o) -> p t o", o=1).broadcast_to(shape), ALU.mult).then_inc(tiles_made, 1)

            shape = [P, SLOTS, EXPERTS]
            settled(dve.tensor_tensor(tex[:, :, :], tiles_i[:, :].rearrange("p (i o) -> p i o", o=1).broadcast_to(shape),
                                      per_expert(ends_e, SLOTS), ALU.is_ge))
            settled(dve.tensor_reduce(e_of[:, :], tex[:, :, :], AX.X, ALU.add))
            settled(dve.memset(K.expert[:, 0:MAX_LAG], 0),
                    dve.tensor_scalar(K.expert[:, MAX_LAG:], e_of[:, :], float(EXPERTS - 1), None, ALU.min))
            dve.wait_ge(exp_done, 1)
            settled(dve.tensor_scalar(few[:, 6, :], few[:, 3, :], 1.0, None, ALU.add))
            settled(dve.reciprocal(K.gates[:, 0, :], few[:, 6, :]))
            settled(dve.tensor_tensor(K.gates[:, 1, :], few[:, 3, :], K.gates[:, 0, :], ALU.mult))

            dve.wait_ge(put, 8)
            settled(dve.tensor_scalar(row_f[:, 0, :], tab_ps[:, 1, :], 0.0, None, ALU.is_equal),
                    dve.tensor_scalar(row_f[:, 3, :], tab_ps[:, 1, :], -1.0, None, ALU.add))
            settled(dve.tensor_tensor(row_f[:, 1, :], row_f[:, 0, :], dump_row[:, :], ALU.mult),
                    dve.scalar_tensor_tensor(row_f[:, 2, :], tab_ps[:, 0, :], 2.0 * P, row_f[:, 3, :], ALU.mult, ALU.add))
            settled(dve.tensor_tensor(row_f[:, 0, :], row_f[:, 1, :], row_f[:, 2, :], ALU.add))
            settled(dve.tensor_copy(K.to[:, :], row_f[:, 0, :]), dve.tensor_copy(row_i[:, :], row_f[:, 0, :]))
            settled(dve.tensor_scalar(row_i[:, :], row_i[:, :], 1, None, ALU.arith_shift_right))
            settled(dve.tensor_scalar(K.source[:, 0:SLOTS], row_i[:, :], TOK, None, ALU.min),
                    dve.memset(K.source[:, SLOTS:], TOK))
            dve.wait_ge(folded, 2 * EXPERTS)


X_LAG, M_LAG, H_LAG, O_LAG = 1, 2, 4, 5
AHEAD = 2


def experts(nc, io, keep):
    K = keep
    w1, w2, wo, b1, b2, bo = K.w1, K.w2, K.wo, K.b1, K.b2, K.bo
    with ExitStack() as ctx:
        def sb(name, shape, dt=F32):
            return ctx.enter_context(nc.sbuf_tensor(name, shape, dt))

        def ps(name, shape):
            return ctx.enter_context(nc.psum_tensor(name, shape, F32))

        def sem(name):
            return ctx.enter_context(nc.semaphore(name))

        source = [sb(f"source{r}", [P, 1], U32) for r in range(FROUND)]
        to = [sb(f"to{r}", [P, 1], U32) for r in range(4)]
        rows = [sb(f"rows{r}", [P, D]) for r in range(4)]
        zt = [sb(f"zt{r}", [P, P]) for r in range(2)]
        gate_in = [sb(f"gate_in{r}", [P, HID]) for r in range(2)]
        silu = [sb(f"silu{r}", [P, HID]) for r in range(2)]
        up = [sb(f"up{r}", [P, HID]) for r in range(2)]
        hid = [sb(f"hid{r}", [P, HID]) for r in range(2)]
        ht = [sb(f"ht{r}", [P, HID]) for r in range(2)]
        o_f = [sb(f"o_f{r}", [P, D]) for r in range(2)]
        o = [sb(f"o{r}", [P, D]) for r in range(4)]

        x1_ps = [ps(f"x1_ps{r}", [P, HID]) for r in range(2)]
        x2_ps = [ps(f"x2_ps{r}", [P, HID]) for r in range(2)]
        ht_ps = ps("ht_ps", [P, HID])
        zt_ps = ps("zt_ps", [P, P])
        o_ps = [ps(f"o_ps{r}", [P, D]) for r in range(2)]

        rows_in = [sem(f"rows_in{r}") for r in range(4)]
        source_ready = sem("source_ready")
        to_ready = sem("to_ready")
        zt_done = sem("zt_done")
        zt_ready = sem("zt_ready")
        x2_ready = sem("x2_ready")
        x1_ready = sem("x1_ready")
        gate_sum = sem("gate_sum")
        gate_ready = sem("gate_ready")
        silu_ready = sem("silu_ready")
        up_ready = sem("up_ready")
        mul_ready = sem("mul_ready")
        hid_ready = sem("hid_ready")
        ht_done = sem("ht_done")
        ht_ready = sem("ht_ready")
        o_done = sem("o_done")
        o_sum = sem("o_sum")
        o_ready = sem("o_ready")
        sent = [sem(f"o_sent{r}") for r in range(4)]

        block = ctx.enter_context(nc.Block())

        def tiles(eng, body, lag):
            for J in range(FROUND):
                body(J, J)
            with eng.Fori(1, SLOTS // FROUND) as it:
                for q in range(FROUND):
                    body(it * FROUND + q, q)
            for q in range(lag):
                body(SLOTS + q, q)

        def present(J, lag):
            return not isinstance(J, int) or 0 <= J - lag < SLOTS

        def late(J, n):
            return not isinstance(J, int) or J >= n

        def filled(J, q, lag, ring, by=16):
            if isinstance(J, int):
                return by * ((J - lag) // ring + 1)
            return (J - q) * (by // ring) + by * ((q - lag) // ring + 1)

        def experts_of(eng, regs, J):
            at = slice(J, min(J + FROUND + MAX_LAG, SLOTS + MAX_LAG)) if isinstance(J, int) else bass.ds(J, FROUND + MAX_LAG)
            n = at.stop - at.start if isinstance(J, int) else FROUND + MAX_LAG
            eng.reg_load(regs[:n], K.expert[0:1, at])

        def expert(eng, regs, q, lag):
            return eng.snap(regs[q + MAX_LAG - lag], min_val=0, max_val=EXPERTS - 1)

        def registers(eng, name):
            return [eng.alloc_register(f"{name}{n}") for n in range(FROUND + MAX_LAG)]

        @block.gpsimd
        def _(pool):
            def step(J, q):
                if present(J, 0):
                    r = q % 4
                    pool.wait_ge(source_ready, J + 1)
                    if late(J, 4):
                        pool.wait_ge(zt_done, J - 3)
                    pool.nop(nofuse=True)
                    pool.indirect_dma_start(rows[r][:, :], None, K.z_rows[:, :],
                                            bass.IndirectOffsetOnAxis(source[q][:, :], 0)).then_inc(rows_in[r], 16)
                lag = AHEAD + O_LAG
                if present(J, lag):
                    f = (q - lag) % FROUND
                    pool.wait_ge(o_ready, J - lag + 1)
                    pool.wait_ge(to_ready, J - lag + 1)
                    pool.nop(nofuse=True)
                    pool.indirect_dma_start(K.results[:, :], bass.IndirectOffsetOnAxis(to[f % 4][:, :], 0),
                                            o[f % 4][:, :], None).then_inc(sent[f % 4], 16)

            tiles(pool, step, AHEAD + O_LAG)
            for r in range(4):
                pool.wait_ge(sent[r], 16 * SLOTS // 4)

        @block.scalar
        def _(act):
            def step(J, q):
                if present(J, H_LAG):
                    f = (q - H_LAG) % FROUND
                    act.wait_ge(ht_done, J - H_LAG + 1)
                    if late(J, H_LAG + 2):
                        act.wait_ge(o_done, J - H_LAG - 1)
                    act.activation(ht[f % 2][:, :], ht_ps[:, :], ACT.Copy).then_inc(ht_ready, 1)
                if present(J, 0):
                    act.wait_ge(zt_done, J + 1)
                    if late(J, 2):
                        act.wait_ge(x1_ready, J - 1)
                    act.activation(zt[q % 2][:, :], zt_ps[:, :], ACT.Copy).then_inc(zt_ready, 1)
                if present(J, X_LAG):
                    f = (q - X_LAG) % FROUND
                    act.wait_ge(gate_ready, J - X_LAG + 1)
                    if late(J, X_LAG + 2):
                        act.wait_ge(mul_ready, J - X_LAG - 1)
                    act.activation(silu[f % 2][:, :], gate_in[f % 2][:, :], ACT.Silu).then_inc(silu_ready, 1)

            tiles(act, step, H_LAG)

        @block.vector
        def _(dve):
            regs = registers(dve, "dve_e")

            def fetch(J, r):
                at = slice(J, J + 1) if isinstance(J, int) else bass.ds(J, 1)
                dve.tensor_copy(source[r][:, :], K.source[:, at]).then_inc(source_ready, 1)

            for r in range(4):
                fetch(r, r)

            def step(J, q):
                if q == 0:
                    experts_of(dve, regs, J)
                if present(J, X_LAG):
                    f = (q - X_LAG) % FROUND
                    n = J - X_LAG
                    e = expert(dve, regs, q, X_LAG)
                    bias = [v[:, bass.ds(e, 1), :].rearrange("p o h -> p (o h)") for v in (b1, b2)]
                    dve.wait_ge(x2_ready, n + 1)
                    if late(J, X_LAG + 2):
                        dve.wait_ge(silu_ready, n - 1)
                    dve.tensor_tensor(gate_in[f % 2][:, :], x2_ps[f % 2][:, :], bias[1], ALU.add).then_inc(gate_sum, 1)
                if present(J, M_LAG):
                    g = (q - M_LAG) % FROUND
                    m = J - M_LAG
                    dve.wait_ge(up_ready, m + 1)
                    dve.wait_ge(silu_ready, m + 1)
                    if late(J, M_LAG + 2):
                        dve.wait_ge(ht_done, m - 1)
                    dve.tensor_tensor(hid[g % 2][:, :], up[g % 2][:, :], silu[g % 2][:, :], ALU.mult).then_inc(mul_ready, 1)
                if present(J, X_LAG):
                    dve.wait_ge(gate_sum, n + 1)
                    dve.tensor_scalar(gate_in[f % 2][:, :], gate_in[f % 2][:, :], -20.0, 20.0, ALU.max, ALU.min).then_inc(gate_ready, 1)
                    dve.wait_ge(x1_ready, n + 1)
                    if late(J, X_LAG + 2):
                        dve.wait_ge(mul_ready, n - 1)
                    dve.tensor_tensor(up[f % 2][:, :], x1_ps[f % 2][:, :], bias[0], ALU.add).then_inc(up_ready, 1)
                if present(J, M_LAG):
                    dve.wait_ge(mul_ready, m + 1)
                    dve.tensor_scalar(hid[g % 2][:, :], hid[g % 2][:, :], -1e4, 1e4, ALU.max, ALU.min).then_inc(hid_ready, 1)
                if present(J, O_LAG):
                    f = (q - O_LAG) % FROUND
                    n = J - O_LAG
                    e = expert(dve, regs, q, O_LAG)
                    dve.wait_ge(o_done, n + 1)
                    if late(J, O_LAG + 2):
                        dve.wait_ge(o_ready, n - 1)
                    dve.tensor_tensor(o_f[f % 2][:, :], o_ps[f % 2][:, :], bo[:, bass.ds(e, 1), :].rearrange("p o d -> p (o d)"),
                                      ALU.add).then_inc(o_sum, 1)
                    if late(J, O_LAG + 4):
                        dve.wait_ge(sent[f % 4], filled(J, q, O_LAG + 4, 4))
                    at = slice(n, n + 1) if isinstance(J, int) else bass.ds(n, 1)
                    dve.tensor_copy(to[f % 4][:, :], K.to[:, at]).then_inc(to_ready, 1)
                if present(J, 0):
                    if late(J, 4):
                        dve.wait_ge(zt_done, J - 3)
                    fetch(J + 4, (q + 4) % FROUND)
                if present(J, O_LAG):
                    dve.wait_ge(o_sum, n + 1)
                    dve.tensor_scalar(o[f % 4][:, :], o_f[f % 2][:, :], -1e4, 1e4, ALU.max, ALU.min).then_inc(o_ready, 1)

            tiles(dve, step, O_LAG)

        @block.tensor
        def _(pe):
            regs = registers(pe, "pe_e")

            def step(J, q):
                if q == 0:
                    experts_of(pe, regs, J)
                if present(J, H_LAG):
                    f = (q - H_LAG) % FROUND
                    n = J - H_LAG
                    pe.wait_ge(hid_ready, n + 1)
                    if late(J, H_LAG + 1):
                        pe.wait_ge(ht_ready, n)
                    for c in range(CHUNKS):
                        mm = pe.transpose(ht_ps[:, c * P:(c + 1) * P], hid[f % 2][:, c * P:(c + 1) * P], K.ident[:, :])
                    mm.then_inc(ht_done, 1)
                if present(J, X_LAG):
                    f = (q - X_LAG) % FROUND
                    n = J - X_LAG
                    e = expert(pe, regs, q, X_LAG)
                    pe.wait_ge(zt_ready, n + 1)
                    if late(J, X_LAG + 2):
                        pe.wait_ge(gate_sum, n - 1)
                        pe.wait_ge(up_ready, n - 1)
                    pe.matmul(x2_ps[f % 2][:, :], zt[f % 2][:, :], w2[:, bass.ds(e, 1), :].rearrange("p o h -> p (o h)"),
                              start=True, stop=True).then_inc(x2_ready, 1)
                    pe.matmul(x1_ps[f % 2][:, :], zt[f % 2][:, :], w1[:, bass.ds(e, 1), :].rearrange("p o h -> p (o h)"),
                              start=True, stop=True).then_inc(x1_ready, 1)
                if present(J, 0):
                    pe.wait_ge(rows_in[q % 4], filled(J, q, 0, 4))
                    if late(J, 1):
                        pe.wait_ge(zt_ready, J)
                    pe.transpose(zt_ps[:, :], rows[q % 4][:, :], K.ident[:, :]).then_inc(zt_done, 1)
                if present(J, H_LAG):
                    f = (q - H_LAG) % FROUND
                    n = J - H_LAG
                    e = expert(pe, regs, q, H_LAG)
                    pe.wait_ge(ht_ready, n + 1)
                    if late(J, H_LAG + 2):
                        pe.wait_ge(o_sum, n - 1)
                    for c in range(CHUNKS):
                        mm = pe.matmul(o_ps[f % 2][:, :], ht[f % 2][:, c * P:(c + 1) * P],
                                       wo[:, bass.ds(e, 1), c, :].rearrange("p o d -> p (o d)"),
                                       start=(c == 0), stop=(c == CHUNKS - 1))
                    mm.then_inc(o_done, 1)

            tiles(pe, step, H_LAG)


def combine(nc, io, keep, out):
    K = keep
    PARTS_OUT = 8
    N = TILES // PARTS_OUT
    with ExitStack() as ctx:
        def sb(name, shape, dt=F32):
            return ctx.enter_context(nc.sbuf_tensor(name, shape, dt))

        def sem(name):
            return ctx.enter_context(nc.semaphore(name))

        f = [sb(f"f{n}", [P, N, 2, D]) for n in range(PARTS_OUT)]
        bn = sb("bn3", [P, TILES, 6])
        mv = sb("mv3", [P, TILES, 2])
        arg = sb("arg3", [P, TILES])
        dev = sb("dev3", [P, TILES])
        inv = sb("inv3", [P, TILES])
        shift = sb("shift3", [P, 2, TILES])
        f_in = [sem(f"f_in{n}") for n in range(PARTS_OUT)]
        second_gated = sem("second_gated")
        summed = sem("summed")
        bn_made = sem("bn_made")
        mv_made = sem("mv_made")
        arg_made = sem("arg_made")
        dev_made = sem("dev_made")
        inv_made = sem("inv_made")
        mean_scaled = sem("mean_scaled")
        shift_made = sem("shift_made")
        normed = sem("normed")
        out_made = sem("out_made")
        out_sent = sem("out_sent")
        block = ctx.enter_context(nc.Block())

        def part(n):
            return slice(n * N, (n + 1) * N)

        @block.sync
        def _(sp):
            src = K.results[0:DUMP, :].rearrange("(t p k) d -> p t (k d)", p=P, k=2)
            for n in range(PARTS_OUT):
                sp.dma_start(f[n][:, :, :, :].rearrange("p t k d -> p t (k d)"), src[:, part(n), :]).then_inc(f_in[n], 16)
            dst = out.rearrange("b (t p) d -> p (b t) d", p=P)
            for n in range(PARTS_OUT):
                sp.wait_ge(out_made, n + 1)
                sp.dma_start(dst[:, part(n), :], K.x_all[:, part(n), :]).then_inc(out_sent, 16)
            sp.wait_ge(out_sent, 16 * PARTS_OUT)

        @block.gpsimd
        def _(pool):
            def add(n):
                pool.wait_ge(normed, N * (n + 1))
                pool.tensor_tensor(K.x_all[:, part(n), :], K.x_all[:, part(n), :], f[n][:, :, 0, :], ALU.add).then_inc(out_made, 1)

            for n in range(PARTS_OUT):
                add(n)

        @block.scalar
        def _(act):
            def gate(n):
                act.wait_ge(f_in[n], 16)
                for t in range(N):
                    act.activation(f[n][:, t, 1, :], f[n][:, t, 1, :], ACT.Copy,
                                   scale=K.gates[:, 1, n * N + t:n * N + t + 1]).then_inc(second_gated, 1)

            def normalise(n):
                act.wait_ge(arg_made, n + 1)
                act.activation(dev[:, part(n)], arg[:, part(n)], ACT.Sqrt).then_inc(dev_made, 1)
                act.wait_ge(shift_made, n + 1)
                for t in range(N):
                    at = slice(n * N + t, n * N + t + 1)
                    act.activation(f[n][:, t, 0, :], f[n][:, t, 0, :], ACT.Identity, scale=inv[:, at], bias=shift[:, 1, at]).then_inc(normed, 1)

            gate(0)
            gate(1)
            for n in range(PARTS_OUT):
                if n + 2 < PARTS_OUT:
                    gate(n + 2)
                normalise(n)

        @block.vector
        def _(dve):
            def scales(n):
                at = part(n)
                dve.wait_ge(dev_made, n + 1)
                dve.reciprocal(inv[:, at], dev[:, at]).then_inc(inv_made, 1)
                dve.wait_ge(inv_made, n + 1)
                dve.tensor_tensor(shift[:, 0, at], mv[:, at, 0], inv[:, at], ALU.mult).then_inc(mean_scaled, 1)
                dve.wait_ge(mean_scaled, n + 1)
                dve.tensor_tensor(shift[:, 1, at], K.left_out[:, at], shift[:, 0, at], ALU.subtract).then_inc(shift_made, 1)

            for n in range(PARTS_OUT):
                dve.wait_ge(f_in[n], 16)
                for t in range(N):
                    dve.wait_ge(second_gated, N * n + t + 1)
                    dve.scalar_tensor_tensor(f[n][:, t, 0, :], f[n][:, t, 0, :], K.gates[:, 0, n * N + t:n * N + t + 1],
                                             f[n][:, t, 1, :], ALU.mult, ALU.add).then_inc(summed, 1)
                for t in range(N):
                    dve.wait_ge(summed, N * n + t + 1)
                    dve.bn_stats(bn[:, n * N + t, :], f[n][:, t, 0, :]).then_inc(bn_made, 1)
                if n:
                    scales(n - 1)
                for t in range(N):
                    dve.wait_ge(bn_made, N * n + t + 1)
                    dve.bn_aggr(mv[:, n * N + t, :], bn[:, n * N + t, :]).then_inc(mv_made, 1)
                dve.wait_ge(mv_made, N * (n + 1))
                dve.tensor_scalar(arg[:, part(n)], mv[:, part(n), 1], EPS, None, ALU.add).then_inc(arg_made, 1)
            scales(PARTS_OUT - 1)


def program(nc, io, out):
    with ExitStack() as ctx:
        class keep:
            x_all = ctx.enter_context(nc.sbuf_tensor("x_all", [P, TILES, D], F32))
            ident = ctx.enter_context(nc.sbuf_tensor("ident", [P, P], F32))
            gates = ctx.enter_context(nc.sbuf_tensor("gates", [P, 2, TILES], F32))
            expert = ctx.enter_context(nc.sbuf_tensor("expert", [P, MAX_LAG + SLOTS], I32))
            source = ctx.enter_context(nc.sbuf_tensor("source", [P, SLOTS + MAX_LAG], U32))
            to = ctx.enter_context(nc.sbuf_tensor("to", [P, SLOTS], U32))
            left_out = ctx.enter_context(nc.sbuf_tensor("left_out", [P, TILES], F32))
            numden = nc.dram_tensor("numden", [COLS, 2 * HD, TOK], F32).ap()
            z_rows = nc.dram_tensor("z_rows", [TOK + 1, D], F32).ap()
            results = nc.dram_tensor("results", [DUMP + P * SLOTS, D], F32).ap()

        keep.u_all = ctx.enter_context(nc.sbuf_tensor("u_all", [P, TILES, D], F32))
        keep.wo_attn = ctx.enter_context(nc.sbuf_tensor("wo_attn", [P, D], F32))
        keep.vecs = ctx.enter_context(nc.sbuf_tensor("vecs", [P, 4, D], F32))
        keep.router = ctx.enter_context(nc.sbuf_tensor("router", [P, EXPERTS], F32))
        keep.ln_b_col = ctx.enter_context(nc.sbuf_tensor("ln_b_col", [P, 1], F32))
        keep.egb = ctx.enter_context(nc.sbuf_tensor("egb", [P, 2, EXPERTS], F32))
        keep.den = ctx.enter_context(nc.sbuf_tensor("den", [P, BATCHES + 1, BTOK // 8], F32))
        keep.num = ctx.enter_context(nc.sbuf_tensor("num", [P, TOK], F32))
        keep.spread = ctx.enter_context(nc.sbuf_tensor("spread", [P, 8, P], F32))
        keep.law = ctx.enter_context(nc.sbuf_tensor("law", [P, 3, 4, BT], F32))
        keep.mv = ctx.enter_context(nc.sbuf_tensor("mv", [P, 4, BT, 2], F32))
        keep.zero = ctx.enter_context(nc.sbuf_tensor("zero", [1, D], F32))
        keep.ones = ctx.enter_context(nc.sbuf_tensor("ones", [P, P], F32))
        keep.tri = ctx.enter_context(nc.sbuf_tensor("tri", [P, P], F32))
        keep.keep_on = ctx.enter_context(nc.sbuf_tensor("keep_on", [P, EXPERTS, TILES], F32))
        keep.e_less = ctx.enter_context(nc.sbuf_tensor("e_less", [P, EXPERTS], F32))
        keep.tiles_i = ctx.enter_context(nc.sbuf_tensor("tiles_i", [P, SLOTS], F32))
        keep.lanes_i = ctx.enter_context(nc.sbuf_tensor("lanes_i", [P, P], F32))
        keep.chunk = ctx.enter_context(nc.sbuf_tensor("chunk", [P, TILES], F32))
        keep.high = ctx.enter_context(nc.sbuf_tensor("high", [P, TILES], F32))
        keep.low = ctx.enter_context(nc.sbuf_tensor("low", [P, 2], F32))
        keep.dump_row = ctx.enter_context(nc.sbuf_tensor("dump_row", [P, SLOTS], F32))
        keep.w1 = ctx.enter_context(nc.sbuf_tensor("w1", [P, EXPERTS, HID], F32))
        keep.w2 = ctx.enter_context(nc.sbuf_tensor("w2", [P, EXPERTS, HID], F32))
        attention(nc, io, keep)
        keep.wo = ctx.enter_context(nc.sbuf_tensor("expert_wo", [P, EXPERTS, CHUNKS, D], F32))
        keep.b1 = ctx.enter_context(nc.sbuf_tensor("b1", [P, EXPERTS, HID], F32))
        keep.b2 = ctx.enter_context(nc.sbuf_tensor("b2", [P, EXPERTS, HID], F32))
        keep.bo = ctx.enter_context(nc.sbuf_tensor("expert_bo", [P, EXPERTS, D], F32))
        routing(nc, io, keep)
        experts(nc, io, keep)
        combine(nc, io, keep, out)


_INS = {"x": "L0_attn_x", "Wq": "L0_attn_Wq", "bq": "L0_attn_bq", "Wk": "L0_attn_Wk", "bk": "L0_attn_bk",
        "Wv": "L0_attn_Wv", "bv": "L0_attn_bv", "Wo": "L0_attn_Wo", "bo": "L0_attn_bo", "gamma": "L0_attn_gamma",
        "beta": "L0_attn_beta", "ln_g": "L0_ffn_ln_g", "ln_b": "L0_ffn_ln_b", "router_w": "L0_ffn_router_w",
        "eg": "L0_ffn_eg", "eb": "L0_ffn_eb", "W1": "L0_ffn_W1", "b1": "L0_ffn_b1", "W2": "L0_ffn_W2",
        "b2": "L0_ffn_b2", "eWo": "L0_ffn_Wo", "ebo": "L0_ffn_bo"}


def kernel(**inputs):
    import numpy as np
    import concourse.bacc as bacc
    from concourse.bass_utils import run_bass_kernel_spmd

    nc = bacc.Bacc("TRN2", target_bir_lowering=False, num_devices=1)
    arrays, io = {}, {}
    for short, name in _INS.items():
        arrays[name] = np.ascontiguousarray(inputs[name])
        io[short] = nc.dram_tensor(name, arrays[name].shape, F32, kind="ExternalInput").ap()
    out = nc.dram_tensor("out", [BATCH, SEQ, D], F32, kind="ExternalOutput").ap()
    program(nc, io, out)
    result = run_bass_kernel_spmd(nc, [arrays], core_ids=[0])
    return result.results[0]["out"]
```
